# Optimizing a Trainium2 kernel written in Bass

```python
import numpy as np
import jax
import jax.numpy as jnp

def _softmax(x, axis=-1):
    return jax.nn.softmax(x, axis=axis)

def _gelu(x):
    return jax.nn.gelu(x, approximate=True)

def _silu(x):
    return jax.nn.silu(x)

def _sigmoid(x):
    return jax.nn.sigmoid(x)

def _layernorm(x, axis=-1, eps=1e-05):
    m = jnp.mean(x, axis=axis, keepdims=True)
    v = jnp.var(x, axis=axis, keepdims=True)
    return (x - m) / jnp.sqrt(v + eps)

def _scatter_add(tgt, idx, src, axis=0):
    return tgt.at[idx].add(src)

def _segment_sum(src, seg, n):
    return jax.ops.segment_sum(src, seg, n)
kernel_name = 'mk_flamingo_gated_d4_seqx_r8_96be85'

def setup_inputs(seed: int=0):
    np.random.seed(seed)
    _w = jnp.asarray

    def _rec_inputs():
        import jax
        import jax.numpy as jnp
        _rk = jax.random.key(seed)
        x = 7.22e-05 + 1 * jax.random.normal(jax.random.fold_in(_rk, 1), (4, 256, 256), jnp.float32)
        _lenS = 256 - jax.random.randint(jax.random.fold_in(_rk, 7), (4,), 0, max(1, 256 // 4) + 1, jnp.int32)
        _lenS2 = 256 - jax.random.randint(jax.random.fold_in(_rk, 8), (4,), 0, max(1, 256 // 4) + 1, jnp.int32)
        _ctx_1024P = jax.random.normal(jax.random.fold_in(_rk, 11), (4, 16, 128), jnp.float32)
        _ctx_1024c = jax.random.dirichlet(jax.random.fold_in(_rk, 511), 0.3 * jnp.ones((16,), jnp.float32), (4, 256))
        _ctx_1024t = jnp.einsum('bsk,bkd->bsd', _ctx_1024c, _ctx_1024P)
        _ctx_1024t = _ctx_1024t * jax.lax.rsqrt(jnp.mean(jnp.square(_ctx_1024t)) + 1e-12) * 0.953939
        ctx_1024 = 2.81802e-05 + 1.00001 * (_ctx_1024t + 0.3 * jax.random.normal(jax.random.fold_in(_rk, 611), (4, 256, 128), jnp.float32))
        _g = jax.random.normal(jax.random.fold_in(_rk, 9001), (2, 4), jnp.float32)
        _g = jnp.sign(_g) * jnp.maximum(jnp.abs(_g), 1.0) + (_g == 0) * 1.0
        g_xattn = _g[0]
        g_ffn = _g[1]
        return (x, ctx_1024, g_xattn, g_ffn)
    x, ctx_1024, g_xattn, g_ffn = _rec_inputs()

    def _L0_xattn_setup():
        import jax, jax.numpy as jnp
        import numpy as np
        key = jax.random.key(seed)
        ks = jax.random.split(key, 6)
        B, L, N, C, D = (8, 64, 256, 128, 128)
        return {'teacher_logits': jax.random.normal(ks[0], (B, L, N), dtype=jnp.float32), 'teacher_features': jax.random.normal(ks[1], (B, N, C), dtype=jnp.float32), 'Wq': jax.random.normal(ks[2], (D, C), dtype=jnp.float32) * (1.0 / np.sqrt(C)), 'bq': jnp.zeros((D,), dtype=jnp.float32), 'Wk': jax.random.normal(ks[3], (D, C), dtype=jnp.float32) * (1.0 / np.sqrt(C)), 'bk': jnp.zeros((D,), dtype=jnp.float32)}
    _L0_xattn_all = _L0_xattn_setup()
    _L0_xattn_in = {k: v for k, v in _L0_xattn_all.items() if k in ('Wq', 'bq', 'Wk', 'bk')}
    del _L0_xattn_all

    def _L0_ffn_setup():
        import jax, jax.numpy as jnp
        import numpy as np
        B, S, D = (2, 256, 256)
        F = 128
        E = 64
        K = 8
        C = 128
        NORM_TOPK = False

        def _moe(x, gate_w, w_gate, w_up, w_down):
            b, s, d = x.shape
            T = b * s
            x2 = x.reshape(T, d)
            logits = x2 @ gate_w.T
            probs = jax.nn.softmax(logits.astype(jnp.float32), axis=-1)
            top_w, top_i = jax.lax.top_k(probs, K)
            if NORM_TOPK:
                top_w = top_w / jnp.sum(top_w, axis=-1, keepdims=True)
            top_w = top_w.astype(x.dtype)
            flat_e = top_i.reshape(-1)
            flat_w = top_w.reshape(-1)
            tok = jnp.arange(T * K) // K
            onehot = jax.nn.one_hot(flat_e, E, dtype=jnp.int32)
            pos = jnp.sum(jnp.cumsum(onehot, axis=0) * onehot, axis=-1) - 1
            valid = pos < C
            loc = flat_e * C + jnp.minimum(pos, C - 1)
            flat_w = jnp.where(valid, flat_w, 0.0)
            safe_loc = jnp.where(valid, loc, E * C)
            xg = jnp.zeros((E * C + 1, d), dtype=x.dtype).at[safe_loc].set(x2[tok])[:E * C]
            xg = xg.reshape(E, C, d)
            h = jax.nn.silu(jnp.einsum('ecd,edf->ecf', xg, w_gate)) * jnp.einsum('ecd,edf->ecf', xg, w_up)
            y = jnp.einsum('ecf,efd->ecd', h, w_down).reshape(E * C, d)
            y_tok = y[loc] * flat_w[:, None]
            out = jnp.zeros((T, d), dtype=x.dtype).at[tok].add(y_tok)
            return out.reshape(b, s, d)
        key = jax.random.key(seed)
        ks = jax.random.split(key, 5)
        scale = 0.02
        return {'hidden_states': jax.random.normal(ks[0], (B, S, D), dtype=jnp.float32), 'gate_w': jax.random.normal(ks[1], (E, D), dtype=jnp.float32) * scale, 'w_gate': jax.random.normal(ks[2], (E, D, F), dtype=jnp.float32) * scale, 'w_up': jax.random.normal(ks[3], (E, D, F), dtype=jnp.float32) * scale, 'w_down': jax.random.normal(ks[4], (E, F, D), dtype=jnp.float32) * scale}
    _L0_ffn_all = _L0_ffn_setup()
    _L0_ffn_in = {k: v for k, v in _L0_ffn_all.items() if k in ('gate_w', 'w_gate', 'w_up', 'w_down')}
    del _L0_ffn_all

    def _L1_xattn_setup():
        import jax, jax.numpy as jnp
        import numpy as np
        import math
        B, L, DM = (2, 256, 128)
        DS, DC, EXP = (16, 4, 2)
        DI = EXP * DM
        DR = math.ceil(DM / 16)
        DT_MIN, DT_MAX, DT_FLOOR = (0.001, 0.1, 0.0001)

        def _ssm_forward(hidden_states, z, in_proj_w, conv_w, conv_b, x_proj_w, dt_proj_w, dt_proj_b, A_log, D):
            b = hidden_states.shape[0]
            x = jnp.einsum('ed,bld->bel', in_proj_w, hidden_states)
            xp = jnp.pad(x, ((0, 0), (0, 0), (DC - 1, 0)))
            xc = jax.lax.conv_general_dilated(xp, conv_w[:, None, :], window_strides=(1,), padding='VALID', dimension_numbers=('NCH', 'OIH', 'NCH'), feature_group_count=DI)
            u = jax.nn.silu(xc + conv_b[None, :, None])
            x_dbl = jnp.einsum('ke,bel->bkl', x_proj_w, u)
            dt_lo = x_dbl[:, :DR]
            Bm = x_dbl[:, DR:DR + DS]
            Cm = x_dbl[:, DR + DS:]
            delta = jax.nn.softplus(jnp.einsum('er,brl->bel', dt_proj_w, dt_lo) + dt_proj_b[None, :, None])
            A = -jnp.exp(A_log)

            def step(state, xs):
                d_t, B_t, C_t, u_t = xs
                dA = jnp.exp(d_t[..., None] * A)
                state = state * dA + (d_t * u_t)[..., None] * B_t[:, None, :]
                y_t = jnp.einsum('ben,bn->be', state, C_t)
                return (state, y_t)
            xs = (jnp.moveaxis(delta, -1, 0), jnp.moveaxis(Bm, -1, 0), jnp.moveaxis(Cm, -1, 0), jnp.moveaxis(u, -1, 0))
            state0 = jnp.zeros((b, DI, DS), delta.dtype)
            _, ys = jax.lax.scan(step, state0, xs)
            y = jnp.moveaxis(ys, 0, -1)
            y = y + D[None, :, None] * u
            y = y * jax.nn.silu(z)
            return jnp.swapaxes(y, 1, 2)
        key = jax.random.key(seed)
        ks = jax.random.split(key, 8)
        hidden_states = jax.random.normal(ks[0], (B, L, DM), jnp.float32)
        z = jax.random.normal(ks[1], (B, DI, L), jnp.float32)
        in_proj_w = jax.random.normal(ks[2], (DI, DM), jnp.float32) * DM ** (-0.5)
        conv_w = jax.random.normal(ks[3], (DI, DC), jnp.float32) * DC ** (-0.5)
        conv_b = jnp.zeros((DI,), jnp.float32)
        x_proj_w = jax.random.normal(ks[4], (DR + 2 * DS, DI), jnp.float32) * DI ** (-0.5)
        dt_std = DR ** (-0.5)
        dt_proj_w = jax.random.uniform(ks[5], (DI, DR), jnp.float32, -dt_std, dt_std)
        dt = jnp.exp(jax.random.uniform(ks[6], (DI,), jnp.float32) * (math.log(DT_MAX) - math.log(DT_MIN)) + math.log(DT_MIN))
        dt = jnp.clip(dt, DT_FLOOR)
        dt_proj_b = dt + jnp.log(-jnp.expm1(-dt))
        A_log = jnp.log(jnp.broadcast_to(jnp.arange(1, DS + 1, dtype=jnp.float32), (DI, DS)))
        D = jnp.ones((DI,), jnp.float32)
        return dict(hidden_states=hidden_states, z=z, in_proj_w=in_proj_w, conv_w=conv_w, conv_b=conv_b, x_proj_w=x_proj_w, dt_proj_w=dt_proj_w, dt_proj_b=dt_proj_b, A_log=A_log, D=D)
    _L1_xattn_all = _L1_xattn_setup()
    _L1_xattn_in = {k: v for k, v in _L1_xattn_all.items() if k in ('in_proj_w', 'conv_w', 'conv_b', 'x_proj_w', 'dt_proj_w', 'dt_proj_b', 'A_log', 'D')}
    del _L1_xattn_all

    def _L1_ffn_setup():
        import jax, jax.numpy as jnp
        import numpy as np
        TOPK = 4
        key = jax.random.key(seed)
        k_x, k_a, k_b, k_w, k_bias = jax.random.split(key, 5)
        b, s, h, j, a, r = (4, 256, 256, 256, 64, 16)
        x = jax.random.normal(k_x, (b, s, h), dtype=jnp.float32)
        A = jax.random.normal(k_a, (a, r, h), dtype=jnp.float32) * 0.02
        B = jax.random.normal(k_b, (a, j, r), dtype=jnp.float32) * 0.02
        W = jax.random.normal(k_w, (j, h), dtype=jnp.float32) * 0.02
        bias = jax.random.normal(k_bias, (j,), dtype=jnp.float32) * 0.02
        return {'x': x, 'A': A, 'B': B, 'W': W, 'bias': bias}
    _L1_ffn_all = _L1_ffn_setup()
    _L1_ffn_in = {k: v for k, v in _L1_ffn_all.items() if k in ('A', 'B', 'W', 'bias')}
    del _L1_ffn_all

    def _L2_xattn_setup():
        import jax, jax.numpy as jnp
        import numpy as np
        EPS = 1e-05

        def rmsnorm(x, g, eps=EPS):
            var = jnp.mean(jnp.square(x), axis=-1, keepdims=True)
            return x * jax.lax.rsqrt(var + eps) * g
        key = jax.random.key(seed)
        ks = jax.random.split(key, 8)
        B, Sq, Skv = (2, 512, 64)
        dim, cdim, H, D = (256, 128, 16, 128)
        inner = H * D
        s = lambda f: 1.0 / np.sqrt(f)
        return {'hidden_states': jax.random.normal(ks[0], (B, Sq, dim), jnp.float32), 'encoder_hidden_states': jax.random.normal(ks[1], (B, Skv, cdim), jnp.float32), 'Wq': jax.random.normal(ks[2], (dim, inner), jnp.float32) * s(dim), 'Wk': jax.random.normal(ks[3], (cdim, inner), jnp.float32) * s(cdim), 'Wv': jax.random.normal(ks[4], (cdim, inner), jnp.float32) * s(cdim), 'Wo': jax.random.normal(ks[5], (inner, dim), jnp.float32) * s(inner), 'gq': jnp.ones((D,), jnp.float32), 'gk': jnp.ones((D,), jnp.float32)}
    _L2_xattn_all = _L2_xattn_setup()
    _L2_xattn_in = {k: v for k, v in _L2_xattn_all.items() if k in ('Wq', 'Wk', 'Wv', 'Wo', 'gq', 'gk')}
    del _L2_xattn_all

    def _L2_ffn_setup():
        import jax, jax.numpy as jnp
        import numpy as np
        D = 256
        F = 176
        E = 8
        K = 2
        FS = 352
        B, S = (2, 128)
        key = jax.random.key(seed)
        ks = jax.random.split(key, 9)
        sc = 0.02
        return {'x': jax.random.normal(ks[0], (B, S, D), dtype=jnp.float32), 'Wr': jax.random.normal(ks[1], (E, D), dtype=jnp.float32) * sc, 'Wg': jax.random.normal(ks[2], (E, F, D), dtype=jnp.float32) * sc, 'Wu': jax.random.normal(ks[3], (E, F, D), dtype=jnp.float32) * sc, 'Wd': jax.random.normal(ks[4], (E, D, F), dtype=jnp.float32) * sc, 'Wsg': jax.random.normal(ks[5], (FS, D), dtype=jnp.float32) * sc, 'Wsu': jax.random.normal(ks[6], (FS, D), dtype=jnp.float32) * sc, 'Wsd': jax.random.normal(ks[7], (D, FS), dtype=jnp.float32) * sc}
    _L2_ffn_all = _L2_ffn_setup()
    _L2_ffn_in = {k: v for k, v in _L2_ffn_all.items() if k in ('Wr', 'Wg', 'Wu', 'Wd', 'Wsg', 'Wsu', 'Wsd')}
    del _L2_ffn_all

    def _L3_xattn_setup():
        import jax, jax.numpy as jnp
        import numpy as np
        B_, L_, D_MODEL = (4, 256, 128)
        D_STATE, D_CONV, EXPAND = (16, 4, 2)
        D_INNER = EXPAND * D_MODEL
        DT_RANK = (D_MODEL + 15) // 16

        def silu(x):
            return x * jax.nn.sigmoid(x)
        key = jax.random.key(seed)
        ks = jax.random.split(key, 10)
        f32 = jnp.float32
        hidden_states = jax.random.normal(ks[0], (B_, L_, D_MODEL), dtype=f32)
        z = jax.random.normal(ks[1], (B_, D_INNER, L_), dtype=f32)
        in_proj_w = jax.random.normal(ks[2], (D_INNER, D_MODEL), dtype=f32) * 0.02
        conv_w = jax.random.normal(ks[3], (D_INNER, 1, D_CONV), dtype=f32) * 0.1
        conv_b = jax.random.normal(ks[4], (D_INNER,), dtype=f32) * 0.02
        x_proj_w = jax.random.normal(ks[5], (DT_RANK + 2 * D_STATE, D_INNER), dtype=f32) * 0.02
        dt_proj_w = jax.random.uniform(ks[6], (D_INNER, DT_RANK), dtype=f32, minval=-DT_RANK ** (-0.5), maxval=DT_RANK ** (-0.5))
        dt = jnp.exp(jax.random.uniform(ks[7], (D_INNER,), dtype=f32, minval=np.log(0.001), maxval=np.log(0.1)))
        dt_proj_b = jnp.log(jnp.expm1(dt))
        A_log = jnp.log(jnp.broadcast_to(jnp.arange(1, D_STATE + 1, dtype=f32), (D_INNER, D_STATE)))
        D = jnp.ones((D_INNER,), f32)
        return {'hidden_states': hidden_states, 'z': z, 'in_proj_w': in_proj_w, 'conv_w': conv_w, 'conv_b': conv_b, 'x_proj_w': x_proj_w, 'dt_proj_w': dt_proj_w, 'dt_proj_b': dt_proj_b, 'A_log': A_log, 'D': D}
    _L3_xattn_all = _L3_xattn_setup()
    _L3_xattn_in = {k: v for k, v in _L3_xattn_all.items() if k in ('in_proj_w', 'conv_w', 'conv_b', 'x_proj_w', 'dt_proj_w', 'dt_proj_b', 'A_log', 'D')}
    del _L3_xattn_all

    def _L3_ffn_setup():
        import jax, jax.numpy as jnp
        import numpy as np
        HIDDEN = 256
        NUM_EXPERTS = 32
        TOP_K = 4
        MOE_INTER = 96
        GROUP = 2
        NUM_CHUNK = NUM_EXPERTS // GROUP
        CHUNK_INTER = 128
        SMALL_SCALE = 0.05

        def _routing(x2d, gate_w):
            logits = x2d @ gate_w.T
            rw = jax.nn.softmax(logits.astype(jnp.float32), axis=-1)
            scores = jax.nn.sigmoid(logits.astype(jnp.float32))
            _, sel = jax.lax.top_k(scores, TOP_K)
            w = jnp.take_along_axis(rw, sel, axis=-1)
            w = w / w.sum(axis=-1, keepdims=True)
            return (w.astype(x2d.dtype), sel)

        def _moe(x2d, Wg, Wu, Wd, cw):
            g = jnp.einsum('th,ehi->eti', x2d, Wg)
            u = jnp.einsum('th,ehi->eti', x2d, Wu)
            a = jax.nn.silu(g) * u * cw.T[:, :, None]
            return jnp.einsum('eti,eih->th', a, Wd)
        key = jax.random.key(seed)
        ks = jax.random.split(key, 8)
        s = 0.02
        B, S = (2, 256)
        return {'hidden_states': jax.random.normal(ks[0], (B, S, HIDDEN), jnp.float32), 'gate_w': jax.random.normal(ks[1], (NUM_EXPERTS, HIDDEN), jnp.float32) * s, 'Wg': jax.random.normal(ks[2], (NUM_EXPERTS, HIDDEN, MOE_INTER), jnp.float32) * s, 'Wu': jax.random.normal(ks[3], (NUM_EXPERTS, HIDDEN, MOE_INTER), jnp.float32) * s, 'Wd': jax.random.normal(ks[4], (NUM_EXPERTS, MOE_INTER, HIDDEN), jnp.float32) * s, 'cWg': jax.random.normal(ks[5], (NUM_CHUNK, HIDDEN, CHUNK_INTER), jnp.float32) * s, 'cWu': jax.random.normal(ks[6], (NUM_CHUNK, HIDDEN, CHUNK_INTER), jnp.float32) * s, 'cWd': jax.random.normal(ks[7], (NUM_CHUNK, CHUNK_INTER, HIDDEN), jnp.float32) * s}
    _L3_ffn_all = _L3_ffn_setup()
    _L3_ffn_in = {k: v for k, v in _L3_ffn_all.items() if k in ('gate_w', 'Wg', 'Wu', 'Wd', 'cWg', 'cWu', 'cWd')}
    del _L3_ffn_all
    return {'x': x, 'ctx_1024': ctx_1024, 'g_xattn': g_xattn, 'g_ffn': g_ffn, 'L0_xattn_Wq': _L0_xattn_in['Wq'], 'L0_xattn_bq': _L0_xattn_in['bq'], 'L0_xattn_Wk': _L0_xattn_in['Wk'], 'L0_xattn_bk': _L0_xattn_in['bk'], 'L0_ffn_gate_w': _L0_ffn_in['gate_w'], 'L0_ffn_w_gate': _L0_ffn_in['w_gate'], 'L0_ffn_w_up': _L0_ffn_in['w_up'], 'L0_ffn_w_down': _L0_ffn_in['w_down'], 'L1_xattn_in_proj_w': _L1_xattn_in['in_proj_w'], 'L1_xattn_conv_w': _L1_xattn_in['conv_w'], 'L1_xattn_conv_b': _L1_xattn_in['conv_b'], 'L1_xattn_x_proj_w': _L1_xattn_in['x_proj_w'], 'L1_xattn_dt_proj_w': _L1_xattn_in['dt_proj_w'], 'L1_xattn_dt_proj_b': _L1_xattn_in['dt_proj_b'], 'L1_xattn_A_log': _L1_xattn_in['A_log'], 'L1_xattn_D': _L1_xattn_in['D'], 'L1_ffn_A': _L1_ffn_in['A'], 'L1_ffn_B': _L1_ffn_in['B'], 'L1_ffn_W': _L1_ffn_in['W'], 'L1_ffn_bias': _L1_ffn_in['bias'], 'L2_xattn_Wq': _L2_xattn_in['Wq'], 'L2_xattn_Wk': _L2_xattn_in['Wk'], 'L2_xattn_Wv': _L2_xattn_in['Wv'], 'L2_xattn_Wo': _L2_xattn_in['Wo'], 'L2_xattn_gq': _L2_xattn_in['gq'], 'L2_xattn_gk': _L2_xattn_in['gk'], 'L2_ffn_Wr': _L2_ffn_in['Wr'], 'L2_ffn_Wg': _L2_ffn_in['Wg'], 'L2_ffn_Wu': _L2_ffn_in['Wu'], 'L2_ffn_Wd': _L2_ffn_in['Wd'], 'L2_ffn_Wsg': _L2_ffn_in['Wsg'], 'L2_ffn_Wsu': _L2_ffn_in['Wsu'], 'L2_ffn_Wsd': _L2_ffn_in['Wsd'], 'L3_xattn_in_proj_w': _L3_xattn_in['in_proj_w'], 'L3_xattn_conv_w': _L3_xattn_in['conv_w'], 'L3_xattn_conv_b': _L3_xattn_in['conv_b'], 'L3_xattn_x_proj_w': _L3_xattn_in['x_proj_w'], 'L3_xattn_dt_proj_w': _L3_xattn_in['dt_proj_w'], 'L3_xattn_dt_proj_b': _L3_xattn_in['dt_proj_b'], 'L3_xattn_A_log': _L3_xattn_in['A_log'], 'L3_xattn_D': _L3_xattn_in['D'], 'L3_ffn_gate_w': _L3_ffn_in['gate_w'], 'L3_ffn_Wg': _L3_ffn_in['Wg'], 'L3_ffn_Wu': _L3_ffn_in['Wu'], 'L3_ffn_Wd': _L3_ffn_in['Wd'], 'L3_ffn_cWg': _L3_ffn_in['cWg'], 'L3_ffn_cWu': _L3_ffn_in['cWu'], 'L3_ffn_cWd': _L3_ffn_in['cWd']}

def reference(x, ctx_1024, g_xattn, g_ffn, L0_xattn_Wq, L0_xattn_bq, L0_xattn_Wk, L0_xattn_bk, L0_ffn_gate_w, L0_ffn_w_gate, L0_ffn_w_up, L0_ffn_w_down, L1_xattn_in_proj_w, L1_xattn_conv_w, L1_xattn_conv_b, L1_xattn_x_proj_w, L1_xattn_dt_proj_w, L1_xattn_dt_proj_b, L1_xattn_A_log, L1_xattn_D, L1_ffn_A, L1_ffn_B, L1_ffn_W, L1_ffn_bias, L2_xattn_Wq, L2_xattn_Wk, L2_xattn_Wv, L2_xattn_Wo, L2_xattn_gq, L2_xattn_gk, L2_ffn_Wr, L2_ffn_Wg, L2_ffn_Wu, L2_ffn_Wd, L2_ffn_Wsg, L2_ffn_Wsu, L2_ffn_Wsd, L3_xattn_in_proj_w, L3_xattn_conv_w, L3_xattn_conv_b, L3_xattn_x_proj_w, L3_xattn_dt_proj_w, L3_xattn_dt_proj_b, L3_xattn_A_log, L3_xattn_D, L3_ffn_gate_w, L3_ffn_Wg, L3_ffn_Wu, L3_ffn_Wd, L3_ffn_cWg, L3_ffn_cWu, L3_ffn_cWd):
    import jax
    import jax.numpy as jnp

    def _L0_xattn_ref(teacher_logits, teacher_features, Wq, bq, Wk, bk):
        import jax, jax.numpy as jnp
        import numpy as np
        query = jnp.einsum('bnc,dc->bnd', teacher_features, Wq) + bq
        key = jnp.einsum('bnc,dc->bnd', teacher_features, Wk) + bk
        energy = jnp.einsum('bnd,bmd->bnm', query, key)
        attention = jax.nn.softmax(energy, axis=-1)
        x_m = jnp.einsum('bln,bmn->blm', teacher_logits, attention)
        return x_m

    def _L0_ffn_ref(hidden_states, gate_w, w_gate, w_up, w_down):
        import jax, jax.numpy as jnp
        import numpy as np
        B, S, D = (2, 256, 256)
        F = 128
        E = 64
        K = 8
        C = 128
        NORM_TOPK = False

        def _moe(x, gate_w, w_gate, w_up, w_down):
            b, s, d = x.shape
            T = b * s
            x2 = x.reshape(T, d)
            logits = x2 @ gate_w.T
            probs = jax.nn.softmax(logits.astype(jnp.float32), axis=-1)
            top_w, top_i = jax.lax.top_k(probs, K)
            if NORM_TOPK:
                top_w = top_w / jnp.sum(top_w, axis=-1, keepdims=True)
            top_w = top_w.astype(x.dtype)
            flat_e = top_i.reshape(-1)
            flat_w = top_w.reshape(-1)
            tok = jnp.arange(T * K) // K
            onehot = jax.nn.one_hot(flat_e, E, dtype=jnp.int32)
            pos = jnp.sum(jnp.cumsum(onehot, axis=0) * onehot, axis=-1) - 1
            valid = pos < C
            loc = flat_e * C + jnp.minimum(pos, C - 1)
            flat_w = jnp.where(valid, flat_w, 0.0)
            safe_loc = jnp.where(valid, loc, E * C)
            xg = jnp.zeros((E * C + 1, d), dtype=x.dtype).at[safe_loc].set(x2[tok])[:E * C]
            xg = xg.reshape(E, C, d)
            h = jax.nn.silu(jnp.einsum('ecd,edf->ecf', xg, w_gate)) * jnp.einsum('ecd,edf->ecf', xg, w_up)
            y = jnp.einsum('ecf,efd->ecd', h, w_down).reshape(E * C, d)
            y_tok = y[loc] * flat_w[:, None]
            out = jnp.zeros((T, d), dtype=x.dtype).at[tok].add(y_tok)
            return out.reshape(b, s, d)
        return _moe(hidden_states, gate_w, w_gate, w_up, w_down)

    def _L1_xattn_ref(hidden_states, z, in_proj_w, conv_w, conv_b, x_proj_w, dt_proj_w, dt_proj_b, A_log, D):
        import jax, jax.numpy as jnp
        import numpy as np
        import math
        B, L, DM = (2, 256, 128)
        DS, DC, EXP = (16, 4, 2)
        DI = EXP * DM
        DR = math.ceil(DM / 16)
        DT_MIN, DT_MAX, DT_FLOOR = (0.001, 0.1, 0.0001)

        def _ssm_forward(hidden_states, z, in_proj_w, conv_w, conv_b, x_proj_w, dt_proj_w, dt_proj_b, A_log, D):
            b = hidden_states.shape[0]
            x = jnp.einsum('ed,bld->bel', in_proj_w, hidden_states)
            xp = jnp.pad(x, ((0, 0), (0, 0), (DC - 1, 0)))
            xc = jax.lax.conv_general_dilated(xp, conv_w[:, None, :], window_strides=(1,), padding='VALID', dimension_numbers=('NCH', 'OIH', 'NCH'), feature_group_count=DI)
            u = jax.nn.silu(xc + conv_b[None, :, None])
            x_dbl = jnp.einsum('ke,bel->bkl', x_proj_w, u)
            dt_lo = x_dbl[:, :DR]
            Bm = x_dbl[:, DR:DR + DS]
            Cm = x_dbl[:, DR + DS:]
            delta = jax.nn.softplus(jnp.einsum('er,brl->bel', dt_proj_w, dt_lo) + dt_proj_b[None, :, None])
            A = -jnp.exp(A_log)

            def step(state, xs):
                d_t, B_t, C_t, u_t = xs
                dA = jnp.exp(d_t[..., None] * A)
                state = state * dA + (d_t * u_t)[..., None] * B_t[:, None, :]
                y_t = jnp.einsum('ben,bn->be', state, C_t)
                return (state, y_t)
            xs = (jnp.moveaxis(delta, -1, 0), jnp.moveaxis(Bm, -1, 0), jnp.moveaxis(Cm, -1, 0), jnp.moveaxis(u, -1, 0))
            state0 = jnp.zeros((b, DI, DS), delta.dtype)
            _, ys = jax.lax.scan(step, state0, xs)
            y = jnp.moveaxis(ys, 0, -1)
            y = y + D[None, :, None] * u
            y = y * jax.nn.silu(z)
            return jnp.swapaxes(y, 1, 2)
        return _ssm_forward(hidden_states, z, in_proj_w, conv_w, conv_b, x_proj_w, dt_proj_w, dt_proj_b, A_log, D)

    def _L1_ffn_ref(x, A, B, W, bias):
        import jax, jax.numpy as jnp
        import numpy as np
        TOPK = 4
        vecs = jnp.einsum('arh,bsh->bsar', A, x)
        arrows = jnp.linalg.norm(vecs, axis=-1)
        _, idx = jax.lax.top_k(arrows, TOPK)
        routes = jax.nn.one_hot(idx, arrows.shape[-1], dtype=x.dtype).sum(-2) / TOPK
        v = jnp.einsum('bsa,bsar->bsr', routes, vecs)
        delta = jnp.einsum('bsa,ajr,bsr->bsj', routes, B, v)
        base = jnp.einsum('bsh,jh->bsj', x, W) + bias
        return base + delta

    def _L2_xattn_ref(hidden_states, encoder_hidden_states, Wq, Wk, Wv, Wo, gq, gk):
        import jax, jax.numpy as jnp
        import numpy as np
        EPS = 1e-05

        def rmsnorm(x, g, eps=EPS):
            var = jnp.mean(jnp.square(x), axis=-1, keepdims=True)
            return x * jax.lax.rsqrt(var + eps) * g
        B, Sq, _ = hidden_states.shape
        Skv = encoder_hidden_states.shape[1]
        D = gq.shape[0]
        H = Wq.shape[1] // D
        scale = 1.0 / np.sqrt(D)
        q = (hidden_states @ Wq).reshape(B, Sq, H, D)
        k = (encoder_hidden_states @ Wk).reshape(B, Skv, H, D)
        v = (encoder_hidden_states @ Wv).reshape(B, Skv, H, D)
        q = rmsnorm(q, gq)
        k = rmsnorm(k, gk)
        scores = jnp.einsum('bqhd,bkhd->bhqk', q, k) * scale
        attn = jax.nn.softmax(scores, axis=-1)
        out = jnp.einsum('bhqk,bkhd->bqhd', attn, v)
        out = out.reshape(B, Sq, H * D)
        return out @ Wo

    def _L2_ffn_ref(x, Wr, Wg, Wu, Wd, Wsg, Wsu, Wsd):
        import jax, jax.numpy as jnp
        import numpy as np
        D = 256
        F = 176
        E = 8
        K = 2
        FS = 352
        B, S = (2, 128)
        silu = jax.nn.silu
        sg = silu(jnp.einsum('bsd,fd->bsf', x, Wsg))
        su = jnp.einsum('bsd,fd->bsf', x, Wsu)
        shared_out = jnp.einsum('bsf,df->bsd', sg * su, Wsd)
        logits = jnp.einsum('bsd,ed->bse', x, Wr)
        scores = jax.nn.softmax(logits, axis=-1)
        topk_scores, topk_idx = jax.lax.top_k(scores, K)
        w_full = jnp.sum(jax.nn.one_hot(topk_idx, E, dtype=x.dtype) * topk_scores[..., None], axis=-2)
        g = silu(jnp.einsum('bsd,efd->bsef', x, Wg))
        u = jnp.einsum('bsd,efd->bsef', x, Wu)
        out_e = jnp.einsum('bsef,edf->bsed', g * u, Wd)
        routed_out = jnp.einsum('bsed,bse->bsd', out_e, w_full)
        return routed_out + shared_out

    def _L3_xattn_ref(hidden_states, z, in_proj_w, conv_w, conv_b, x_proj_w, dt_proj_w, dt_proj_b, A_log, D):
        import jax, jax.numpy as jnp
        import numpy as np
        B_, L_, D_MODEL = (4, 256, 128)
        D_STATE, D_CONV, EXPAND = (16, 4, 2)
        D_INNER = EXPAND * D_MODEL
        DT_RANK = (D_MODEL + 15) // 16

        def silu(x):
            return x * jax.nn.sigmoid(x)
        Bsz, L, _ = hidden_states.shape
        d_inner, _, d_conv = conv_w.shape
        dt_rank = dt_proj_w.shape[1]
        d_state = A_log.shape[1]
        x = jnp.einsum('bld,ed->bel', hidden_states, in_proj_w)
        xc = jax.lax.conv_general_dilated(x, conv_w, window_strides=(1,), padding=[(d_conv - 1, 0)], feature_group_count=d_inner, dimension_numbers=('NCH', 'OIH', 'NCH'))
        x = silu(xc + conv_b[None, :, None])
        x_dbl = jnp.einsum('bdl,ed->bel', x, x_proj_w)
        dt_low, Bm, Cm = jnp.split(x_dbl, [dt_rank, dt_rank + d_state], axis=1)
        dt = jnp.einsum('brl,dr->bdl', dt_low, dt_proj_w)
        dt = jax.nn.softplus(dt + dt_proj_b[None, :, None])
        A = -jnp.exp(A_log)
        dt_t = jnp.moveaxis(dt, -1, 0)
        B_t = jnp.moveaxis(Bm, -1, 0)
        C_t = jnp.moveaxis(Cm, -1, 0)
        u_t = jnp.moveaxis(x, -1, 0)

        def step(state, inp):
            d, b, c, u = inp
            dA = jnp.exp(d[..., None] * A)
            state = state * dA + (d * u)[..., None] * b[:, None, :]
            y = jnp.einsum('bdn,bn->bd', state, c)
            return (state, y)
        state0 = jnp.zeros((Bsz, d_inner, d_state), x.dtype)
        _, ys = jax.lax.scan(step, state0, (dt_t, B_t, C_t, u_t))
        y = jnp.moveaxis(ys, 0, 2)
        y = y + D[None, :, None] * x
        y = y * silu(z)
        return jnp.swapaxes(y, 1, 2)

    def _L3_ffn_ref(hidden_states, gate_w, Wg, Wu, Wd, cWg, cWu, cWd):
        import jax, jax.numpy as jnp
        import numpy as np
        HIDDEN = 256
        NUM_EXPERTS = 32
        TOP_K = 4
        MOE_INTER = 96
        GROUP = 2
        NUM_CHUNK = NUM_EXPERTS // GROUP
        CHUNK_INTER = 128
        SMALL_SCALE = 0.05

        def _routing(x2d, gate_w):
            logits = x2d @ gate_w.T
            rw = jax.nn.softmax(logits.astype(jnp.float32), axis=-1)
            scores = jax.nn.sigmoid(logits.astype(jnp.float32))
            _, sel = jax.lax.top_k(scores, TOP_K)
            w = jnp.take_along_axis(rw, sel, axis=-1)
            w = w / w.sum(axis=-1, keepdims=True)
            return (w.astype(x2d.dtype), sel)

        def _moe(x2d, Wg, Wu, Wd, cw):
            g = jnp.einsum('th,ehi->eti', x2d, Wg)
            u = jnp.einsum('th,ehi->eti', x2d, Wu)
            a = jax.nn.silu(g) * u * cw.T[:, :, None]
            return jnp.einsum('eti,eih->th', a, Wd)
        B, S, H = hidden_states.shape
        T = B * S
        x = hidden_states.reshape(T, H)
        w, sel = _routing(x, gate_w)
        rows = jnp.arange(T)[:, None]
        cw_large = jnp.zeros((T, NUM_EXPERTS), x.dtype).at[rows, sel].add(w)
        cw_small = jnp.zeros((T, NUM_CHUNK), x.dtype).at[rows, sel // GROUP].add(w)
        large = _moe(x, Wg, Wu, Wd, cw_large)
        small = _moe(x, cWg, cWu, cWd, cw_small)
        return (large + SMALL_SCALE * small).reshape(B, S, H)
    x = x + jnp.tanh(g_xattn[0]) * _L0_xattn_ref(_layernorm(x, axis=-1), ctx_1024, L0_xattn_Wq, L0_xattn_bq, L0_xattn_Wk, L0_xattn_bk)
    x = x + jnp.tanh(g_ffn[0]) * _L0_ffn_ref(_layernorm(x, axis=-1), L0_ffn_gate_w, L0_ffn_w_gate, L0_ffn_w_up, L0_ffn_w_down)
    x = x + jnp.tanh(g_xattn[1]) * _L1_xattn_ref(ctx_1024, _layernorm(x, axis=-1), L1_xattn_in_proj_w, L1_xattn_conv_w, L1_xattn_conv_b, L1_xattn_x_proj_w, L1_xattn_dt_proj_w, L1_xattn_dt_proj_b, L1_xattn_A_log, L1_xattn_D)
    x = x + jnp.tanh(g_ffn[1]) * _L1_ffn_ref(_layernorm(x, axis=-1), L1_ffn_A, L1_ffn_B, L1_ffn_W, L1_ffn_bias)
    x = x + jnp.tanh(g_xattn[2]) * _L2_xattn_ref(_layernorm(x, axis=-1), ctx_1024, L2_xattn_Wq, L2_xattn_Wk, L2_xattn_Wv, L2_xattn_Wo, L2_xattn_gq, L2_xattn_gk)
    x = x + jnp.tanh(g_ffn[2]) * _L2_ffn_ref(_layernorm(x, axis=-1), L2_ffn_Wr, L2_ffn_Wg, L2_ffn_Wu, L2_ffn_Wd, L2_ffn_Wsg, L2_ffn_Wsu, L2_ffn_Wsd)
    x = x + jnp.tanh(g_xattn[3]) * _L3_xattn_ref(ctx_1024, _layernorm(x, axis=-1), L3_xattn_in_proj_w, L3_xattn_conv_w, L3_xattn_conv_b, L3_xattn_x_proj_w, L3_xattn_dt_proj_w, L3_xattn_dt_proj_b, L3_xattn_A_log, L3_xattn_D)
    x = x + jnp.tanh(g_ffn[3]) * _L3_ffn_ref(_layernorm(x, axis=-1), L3_ffn_gate_w, L3_ffn_Wg, L3_ffn_Wu, L3_ffn_Wd, L3_ffn_cWg, L3_ffn_cWu, L3_ffn_cWd)
    return x

_drawn_inputs = setup_inputs


def setup_inputs(seed=0):
    import zlib

    import numpy as np

    out = dict(_drawn_inputs(seed))
    spreads = {'L0_xattn_bq': (0.0, 0.1),
     'L0_xattn_bk': (0.0, 0.8),
     'L1_xattn_conv_b': (0.0, 0.303),
     'L1_xattn_D': (1.0, 0.2),
     'L2_xattn_gq': (1.0, 0.6),
     'L2_xattn_gk': (1.0, 0.6),
     'L3_xattn_D': (1.0, 0.6)}
    factors = {'g_ffn': 6.388,
     'L0_ffn_gate_w': 8.0,
     'L0_ffn_w_gate': 8.0,
     'L0_ffn_w_up': 8.0,
     'L0_ffn_w_down': 8.0,
     'L1_xattn_dt_proj_w': 7.4,
     'L1_xattn_dt_proj_b': 3.016,
     'L1_xattn_A_log': 2.914,
     'L1_ffn_A': 7.34,
     'L1_ffn_B': 6.155,
     'L1_ffn_bias': 4.175,
     'L2_ffn_Wr': 8.0,
     'L2_ffn_Wg': 8.0,
     'L2_ffn_Wu': 8.0,
     'L2_ffn_Wd': 8.0,
     'L2_ffn_Wsg': 5.007,
     'L2_ffn_Wsu': 4.914,
     'L2_ffn_Wsd': 4.912,
     'L3_xattn_in_proj_w': 7.837,
     'L3_xattn_conv_w': 8.0,
     'L3_xattn_conv_b': 8.0,
     'L3_xattn_x_proj_w': 8.0,
     'L3_xattn_dt_proj_w': 8.0,
     'L3_xattn_dt_proj_b': 8.0,
     'L3_xattn_A_log': 8.0,
     'L3_ffn_gate_w': 8.0,
     'L3_ffn_Wg': 8.0,
     'L3_ffn_Wu': 8.0,
     'L3_ffn_Wd': 8.0,
     'L3_ffn_cWg': 8.0,
     'L3_ffn_cWu': 8.0,
     'L3_ffn_cWd': 8.0}
    for name, (base, spread) in spreads.items():
        noise = np.random.default_rng([zlib.crc32(name.encode()), seed]).standard_normal(out[name].shape)
        drawn = base * np.exp(spread * noise) if base else spread * noise
        out[name] = jnp.asarray(drawn.astype(out[name].dtype))
    for name, factor in factors.items():
        out[name] = (out[name] * factor).astype(out[name].dtype)
    return out
```

```python
from contextlib import ExitStack

import concourse.bass as bass
from concourse import mybir

F32 = mybir.dt.float32
BF16 = mybir.dt.bfloat16
I32 = mybir.dt.int32
U32 = mybir.dt.uint32
ALU = mybir.AluOpType
ACT = mybir.ActivationFunctionType
AX_X = mybir.AxisListType.X
ds = bass.ds

P = 128
B, S, D = 4, 256, 256
C = 128
T = B * S
NT = T // P
HD = D // P
TPB = S // P
HALF = 512
EPS = 1e-5
LAYERS = 4
F0_W_AT = 1536
SSM_AT = 16800
ARENA = 32768


class Link:

    def __init__(self, eng, sem):
        self.eng, self.sem, self.base, self.i, self.per, self.n = eng, sem, 0, None, 0, 0

    def enter(self, i, per):
        self.i, self.per, self.n = i, per, 0

    def leave(self, turns):
        assert self.n == self.per, (self.n, self.per)
        self.base += turns * self.per
        self.i = None

    def __call__(self, ins):
        ins.then_inc(self.sem, 1)
        if self.i is None:
            self.base += 1
            self.eng.wait_ge(self.sem, self.base)
        else:
            self.n += 1
            self.eng.wait_ge(self.sem, self.i * self.per + (self.base + self.n))


def flamingo_kernel(nc, A, out):
    with ExitStack() as ctx:
        def sb(name, shape, dt=F32):
            return ctx.enter_context(nc.sbuf_tensor(name, shape, dt))

        def sem(name):
            return ctx.enter_context(nc.semaphore(name))

        ctx.enter_context(nc.allow_non_contiguous_dma(reason="small parameters, loaded once"))
        bank = [ctx.enter_context(nc.psum_tensor(f"bank{i}", [P, HALF], F32)) for i in range(8)]

        x = sb("x", [P, NT, D])
        y = sb("y", [P, NT, D])
        yT = sb("yT", [P, HD, T])
        ctxT = sb("ctxT", [P, T])
        ident = sb("ident", [P, P])
        stats = sb("stats", [P, NT, 6])
        moments = sb("moments", [P, NT, 2])
        var_eps = sb("var_eps", [P, NT])
        rstd = sb("rstd", [P, NT])
        minus_half = sb("minus_half", [P, NT])
        gates = sb("gates", [P, 2, LAYERS])
        tanh_g = sb("tanh_g", [P, 2, LAYERS])
        arena = sb("arena", [P, ARENA])

        def area(at, *shape):
            n = 1
            for k in shape:
                n *= k
            assert at + n <= ARENA, (at, n)
            v = arena[:, at:at + n]
            if len(shape) == 2:
                v = v.rearrange("p (a b) -> p a b", a=shape[0])
            elif len(shape) == 3:
                v = v.rearrange("p (a b c) -> p a b c", a=shape[0], b=shape[1])
            return v

        s_dve = sem("s_dve")
        s_act = sem("s_act")
        s_pool = sem("s_pool")

        ctx_rows = y[:, :, 0:C]
        wqk_rows = sb("wqk_rows", [P, 2, C])
        gw_rows = sb("gw_rows", [64, D])
        wqkT = sb("wqkT", [P, 2, P])
        gwT = sb("gwT", [P, HD, 64])
        bqk = sb("bqk", [P, 2])
        s_ld_ctx = sem("s_ld_ctx")
        s_ld_w0 = sem("s_ld_w0")
        s_ld_x = sem("s_ld_x")
        s_ld_g = sem("s_ld_g")
        s_const = sem("s_const")
        s_prep_t = sem("s_prep_t")
        s_prep = sem("s_prep")
        s_gate = sem("s_gate")

        N_W0 = 5
        prep_groups = [
            ([ctx_rows[:, i, :] for i in range(4)], ctxT[:, 0:512]),
            ([ctx_rows[:, i, :] for i in range(4, 8)], ctxT[:, 512:1024]),
            ([wqk_rows[:, i, :] for i in range(2)], wqkT[:, :, :].rearrange("p a b -> p (a b)")),
            ([gw_rows[:, h * P:(h + 1) * P] for h in range(HD)], gwT[:, :, :].rearrange("p a b -> p (a b)")),
        ]

        def prep_sp(sp):
            sp.dma_start(ctx_rows, A["ctx_1024"].rearrange("b (h p) c -> p (b h) c", p=P)).then_inc(s_ld_ctx, 16)
            sp.dma_start(wqk_rows[:, 0, :], A["L0_xattn_Wq"]).then_inc(s_ld_w0, 16)
            sp.dma_start(wqk_rows[:, 1, :], A["L0_xattn_Wk"]).then_inc(s_ld_w0, 16)
            sp.dma_start(gw_rows[:, :], A["L0_ffn_gate_w"]).then_inc(s_ld_w0, 16)
            sp.dma_start(bqk[:, 0:1], A["L0_xattn_bq"].rearrange("(p a) -> p a", a=1)).then_inc(s_ld_w0, 16)
            sp.dma_start(bqk[:, 1:2], A["L0_xattn_bk"].rearrange("(p a) -> p a", a=1)).then_inc(s_ld_w0, 16)
            ssm_loads_sp(sp)
            sp.dma_start(x[:, :, :], A["x"].rearrange("b (h p) d -> p (b h) d", p=P)).then_inc(s_ld_x, 16)
            sp.dma_start(gates[:, 0, :], A["g_xattn"].rearrange("(a n) -> a n", a=1).to_broadcast([P, LAYERS])).then_inc(s_ld_g, 16)
            sp.dma_start(gates[:, 1, :], A["g_ffn"].rearrange("(a n) -> a n", a=1).to_broadcast([P, LAYERS])).then_inc(s_ld_g, 16)

        def prep_pool(pool):
            link = pool_link
            link(nc.gpsimd.memset(ident[:, :], 0.0))
            nc.gpsimd.affine_select(out=ident[:, :], in_=ident[:, :], compare_op=ALU.not_equal, fill=1.0, base=0,
                                    pattern=[[-1, P]], channel_multiplier=1).then_inc(s_const, 1)
            nc.gpsimd.memset(minus_half[:, :], -0.5).then_inc(s_const, 1)

        def prep_pe(pe):
            pe.wait_ge(s_const, 2)
            for n, (blocks, dst) in enumerate(prep_groups):
                if n == 0:
                    pe.wait_ge(s_ld_ctx, 16)
                if n == 2:
                    pe.wait_ge(s_ld_w0, 16 * N_W0)
                if n == 4:
                    pe.wait_ge(s_ld_ssm, 16 * 16)
                if n >= 2:
                    pe.wait_ge(s_prep, n - 1)
                at = 0
                for src in blocks:
                    rows = src.shape[0]
                    last = nc.tensor.transpose(bank[n % 2][0:src.shape[1], at:at + rows], src, ident[0:rows, 0:rows])
                    at += rows
                last.then_inc(s_prep_t, 1)

        def prep_act(act):
            for n, (blocks, dst) in enumerate(prep_groups):
                act.wait_ge(s_prep_t, n + 1)
                nc.scalar.copy(dst, bank[n % 2][0:dst.shape[0], 0:dst.shape[1]]).then_inc(s_prep, 1)
            act.wait_ge(s_ld_g, 32)
            nc.scalar.activation(tanh_g[:, :, :], gates[:, :, :], ACT.Tanh).then_inc(s_gate, 1)

        s_var = sem("s_var")
        s_rstd = sem("s_rstd")
        s_y = sem("s_y")
        s_yT_t = sem("s_yT_t")
        s_yT = sem("s_yT")
        norms = {"n": 0, "t": 0}

        def norm_dve(dve, k):
            for i in range(NT):
                last = nc.vector.bn_stats(stats[:, i, :], x[:, i, :])
            dve_link(last)
            for i in range(NT):
                last = nc.vector.bn_aggr(moments[:, i, :], stats[:, i, :])
            dve_link(last)
            nc.vector.tensor_scalar(var_eps[:, :], moments[:, :, 1], EPS, None, ALU.add).then_inc(s_var, 1)
            dve.wait_ge(s_rstd, k + 1)
            for i in range(NT):
                nc.vector.tensor_scalar(y[:, i, :], x[:, i, :], moments[:, i, 0:1], rstd[:, i:i + 1],
                                        ALU.subtract, ALU.mult).then_inc(s_y, 1)

        def norm_pool(pool, k):
            pool.wait_ge(s_var, k + 1)
            nc.gpsimd.tensor_tensor(rstd[:, :], var_eps[:, :], minus_half[:, :], ALU.pow).then_inc(s_rstd, 1)

        def norm_pe(pe, k, t):
            for j in range(NT // 2):
                pe.wait_ge(s_y, NT * k + 2 * j + 2)
                m = t * NT // 2 + j
                if m >= 2:
                    pe.wait_ge(s_yT, m - 1)
                for h in range(HD):
                    for i in range(2):
                        last = nc.tensor.transpose(bank[m % 2][:, (2 * h + i) * P:(2 * h + i + 1) * P],
                                                   y[:, 2 * j + i, h * P:(h + 1) * P], ident[:, :])
                last.then_inc(s_yT_t, 1)

        def norm_act(act, t):
            for j in range(NT // 2):
                m = t * NT // 2 + j
                act.wait_ge(s_yT_t, m + 1)
                nc.scalar.copy(yT[:, :, 2 * j * P:(2 * j + 2) * P],
                               bank[m % 2][:, :].rearrange("p (h n) -> p h n", h=HD)).then_inc(s_yT, 1)

        SSM = ("L1_xattn_", "L3_xattn_")
        DI, DS, DR, DC = 256, 16, 8, 4
        HC = DI // P
        NB = 4
        GB = DS // NB
        GROUPS = B * GB * HC
        PAD = 4 + S
        bc_rows = nc.dram_tensor("bc_rows", [2, B, 2 * DS, S], F32, kind="Internal").ap()
        ssm_y = sb("ssm_y", [P, 2, B, HC, S])
        at = SSM_AT
        ssm_delta = area(at, HC, T); at += HC * T
        ssm_du = area(at, HC, T); at += HC * T
        ssm_tmp = at
        ssm_B = area(at, 2, NB * S); at += 2 * NB * S
        ssm_C = area(at, 2, NB * S); at += 2 * NB * S
        ssm_decay = area(at, 2, NB * S); at += 2 * NB * S
        ssm_h = area(at, 2, NB * S); at += 2 * NB * S
        ssm_hC_buf = area(at, 2, NB * S); at += 2 * NB * S
        ssm_in = area(at, NB * S); at += NB * S
        SSM_END = at
        at = ssm_tmp
        ssm_pad = area(at, HC * B, PAD); at += HC * B * PAD
        ssm_v = area(at, HC, T); at += HC * T
        ssm_u = area(at, HC, T); at += HC * T
        ssm_lin = area(at, HC, T); at += HC * T
        ssm_e = area(at, HC, T); at += HC * T
        assert at <= SSM_END
        ssm_w = ssm_v
        ssm_s = ssm_du
        win_rows = sb("win_rows", [P, 2, HC, C])
        xp_rows = sb("xp_rows", [DR + 2 * DS, 2, DI])
        dt_rows = sb("dt_rows", [P, 2, HC, DR])
        winT = sb("winT", [P, 2 * HC, P])
        xpT = sb("xpT", [P, 2 * HC, DR + 2 * DS])
        dtT = sb("dtT", [DR, 2 * HC, P])
        conv_w = sb("conv_w", [P, 2, HC, DC])
        ssm_par = sb("ssm_par", [P, 3, 2, HC])
        ssm_A = sb("ssm_A", [P, 2, HC, DS])
        x_dbl = sb("x_dbl", [DR + 2 * DS, T])
        s_ld_ssm = sem("s_ld_ssm")
        s_sp_xin = sem("s_sp_xin")
        s_sp_pad = sem("s_sp_pad")
        s_sp_v = sem("s_sp_v")
        s_sp_u = sem("s_sp_u")
        s_sp_dblp = sem("s_sp_dblp")
        s_sp_dbl = sem("s_sp_dbl")
        s_sp_bc = sem("s_sp_bc")
        s_sp_dtp = sem("s_sp_dtp")
        s_sp_e = sem("s_sp_e")
        s_sp_done = sem("s_sp_done")
        s_A = sem("s_A")
        s_ssm_B = [sem(f"s_ssm_B{r}") for r in range(2)]
        s_ssm_C = [sem(f"s_ssm_C{r}") for r in range(2)]
        s_ssm_decay = sem("s_ssm_decay")
        s_ssm_in = sem("s_ssm_in")
        s_ssm_go = sem("s_ssm_go")
        s_ssm_h = sem("s_ssm_h")
        s_ssm_hC = sem("s_ssm_hC")
        s_ssm_sum = sem("s_ssm_sum")
        s_ssm_y = sem("s_ssm_y")
        s_ssm_red = sem("s_ssm_red")
        s_ssm_red_y = sem("s_ssm_red_y")
        ssm_part = sb("ssm_part", [P, S])

        prep_groups += [
            ([win_rows[:, m, c, :] for m in range(2) for c in range(HC)], winT[:, :, :].rearrange("p a b -> p (a b)")),
            ([xp_rows[:, m, c * P:(c + 1) * P] for m in range(2) for c in range(HC)],
             xpT[:, :, :].rearrange("p a b -> p (a b)")),
            ([dt_rows[:, m, c, :] for m in range(2) for c in range(HC)], dtT[:, :, :].rearrange("p a b -> p (a b)")),
        ]

        def ssm_loads_sp(sp):
            for m, name in enumerate(SSM):
                loads = [
                    (win_rows[:, m, :, :], A[name + "in_proj_w"].rearrange("(c p) k -> p c k", p=P)),
                    (xp_rows[:, m, :], A[name + "x_proj_w"]),
                    (dt_rows[:, m, :, :], A[name + "dt_proj_w"].rearrange("(c p) r -> p c r", p=P)),
                    (conv_w[:, m, :, :], A[name + "conv_w"].rearrange("(c p) k -> p c k" if m == 0 else "(c p) a k -> p c (a k)", p=P)),
                    (ssm_par[:, 0, m, :], A[name + "conv_b"].rearrange("(c p) -> p c", p=P)),
                    (ssm_par[:, 1, m, :], A[name + "dt_proj_b"].rearrange("(c p) -> p c", p=P)),
                    (ssm_par[:, 2, m, :], A[name + "D"].rearrange("(c p) -> p c", p=P)),
                    (ssm_A[:, m, :, :], A[name + "A_log"].rearrange("(c p) n -> p c n", p=P)),
                ]
                for dst, src in loads:
                    sp.dma_start(dst, src).then_inc(s_ld_ssm, 16)

        def ssm_A_act(act):
            act.wait_ge(s_ld_ssm, 16 * 16)
            flat = ssm_A[:, :, :, :].rearrange("p m c n -> p (m c n)")
            act_link(nc.scalar.activation(flat, flat, ACT.Exp))
            nc.scalar.mul(flat, flat, -1.0).then_inc(s_A, 1)

        def ssm_bank(i):
            return bank[4 + i]

        def ssm_in_pe(pe, m):
            if m:
                pe.wait_ge(s_ssm_y, B * HC)
                pe.wait_ge(s_f0_ye, PAIRS)
            pe.wait_ge(s_prep, len(prep_groups))
            for c in range(HC):
                for h in range(2):
                    nc.tensor.matmul(ssm_bank(2 * c + h)[:, :], winT[:, HC * m + c, :], ctxT[:, h * HALF:(h + 1) * HALF],
                                     start=True, stop=True).then_inc(s_sp_xin, 1)

        def ssm_in_act(act, m):
            if m:
                act.wait_ge(s_ssm_sum, GROUPS)
                act.wait_ge(s_ssm_y, B * HC)
            for c in range(HC):
                for h in range(2):
                    act.wait_ge(s_sp_xin, 4 * m + 2 * c + h + 1)
                    nc.scalar.copy(ssm_pad[:, 4 * c + 2 * h:4 * c + 2 * h + 2, DC - 1:DC - 1 + S],
                                   ssm_bank(2 * c + h)[:, :].rearrange("p (b l) -> p b l", b=2)).then_inc(s_sp_pad, 1)
            for c in range(HC):
                act.wait_ge(s_sp_v, HC * m + c + 1)
                nc.scalar.activation(ssm_u[:, c, :], ssm_v[:, c, :], ACT.Silu).then_inc(s_sp_u, 1)

        def ssm_in_dve(dve, m):
            if m:
                dve.wait_ge(s_ssm_sum, GROUPS)
            else:
                dve.wait_ge(s_ld_ssm, 16 * 16)
            dve_link(nc.vector.memset(ssm_pad[:, :, 0:DC - 1], 0.0))
            for c in range(HC):
                dve.wait_ge(s_sp_pad, 4 * m + 2 * c + 2)
                v = ssm_v[:, c, :].rearrange("p (b l) -> p b l", b=B)
                for k in range(DC):
                    tap = ssm_pad[:, B * c:B * (c + 1), k:k + S]
                    if k == 0:
                        dve_link(nc.vector.tensor_scalar(v, tap, conv_w[:, m, c, 0:1], ssm_par[:, 0, m, c:c + 1],
                                                         ALU.mult, ALU.add))
                    else:
                        last = nc.vector.scalar_tensor_tensor(out=v, in0=tap, scalar=conv_w[:, m, c, k:k + 1], in1=v,
                                                              op0=ALU.mult, op1=ALU.add)
                        if k < DC - 1:
                            dve_link(last)
                last.then_inc(s_sp_v, 1)

        def ssm_dt_pe(pe, m):
            pe.wait_ge(s_sp_u, HC * (m + 1))
            for h in range(2):
                for c in range(HC):
                    last = nc.tensor.matmul(ssm_bank(h)[0:DR + 2 * DS, :], xpT[:, HC * m + c, :],
                                            ssm_u[:, c, h * HALF:(h + 1) * HALF], start=(c == 0), stop=(c == HC - 1))
                last.then_inc(s_sp_dblp, 1)
            pe.wait_ge(s_sp_dbl, 2 * m + 2)
            for c in range(HC):
                for h in range(2):
                    nc.tensor.matmul(ssm_bank(2 * c + h)[:, :], dtT[:, HC * m + c, :],
                                     x_dbl[0:DR, h * HALF:(h + 1) * HALF], start=True, stop=True).then_inc(s_sp_dtp, 1)

        def ssm_dt_act(act, m):
            for h in range(2):
                act.wait_ge(s_sp_dblp, 2 * m + h + 1)
                if m:
                    act.wait_ge(s_sp_bc, 16)
                nc.scalar.copy(x_dbl[:, h * HALF:(h + 1) * HALF], ssm_bank(h)[0:DR + 2 * DS, :]).then_inc(s_sp_dbl, 1)
            for c in range(HC):
                for h in range(2):
                    cols = slice(h * HALF, (h + 1) * HALF)
                    act.wait_ge(s_sp_dtp, 4 * m + 2 * c + h + 1)
                    bias = ssm_par[:, 1, m, c:c + 1]
                    nc.scalar.activation(ssm_lin[:, c, cols], ssm_bank(2 * c + h)[:, :], ACT.Relu, bias=bias)
                    act_link(nc.scalar.activation(ssm_e[:, c, cols], ssm_bank(2 * c + h)[:, :], ACT.Abs, bias=bias))
                    nc.scalar.activation(ssm_e[:, c, cols], ssm_e[:, c, cols], ACT.Exp, scale=-1.0).then_inc(s_sp_e, 1)

        def ssm_bc_sp(sp, m):
            sp.wait_ge(s_sp_dbl, 2 * m + 2)
            sp.dma_start(bc_rows[m].rearrange("b n l -> n b l"),
                         x_dbl[DR:, :].rearrange("n (b l) -> n b l", b=B)).then_inc(s_sp_bc, 16)

        def ssm_dt_dve(dve, m):
            V = nc.vector
            e, s, w, t = (z.rearrange("p c n -> p (c n)") for z in (ssm_e, ssm_s, ssm_w, ssm_delta))
            lin, u = (z.rearrange("p c n -> p (c n)") for z in (ssm_lin, ssm_u))
            dve.wait_ge(s_sp_e, 4 * (m + 1))
            dve_link(V.tensor_scalar(t, e, 2.0, None, ALU.add))
            dve_link(V.reciprocal(t, t))
            dve_link(V.tensor_tensor(s, e, t, ALU.mult))
            dve_link(V.tensor_tensor(w, s, s, ALU.mult))
            dve_link(V.tensor_scalar(t, w, 1.0 / 13.0, None, ALU.mult))
            for k in (11, 9, 7, 5, 3):
                dve_link(V.scalar_tensor_tensor(out=t, in0=t, scalar=1.0 / k, in1=w, op0=ALU.add, op1=ALU.mult))
            dve_link(V.scalar_tensor_tensor(out=t, in0=t, scalar=1.0, in1=s, op0=ALU.add, op1=ALU.mult))
            dve_link(V.scalar_tensor_tensor(out=t, in0=t, scalar=2.0, in1=lin, op0=ALU.mult, op1=ALU.add))
            V.tensor_tensor(ssm_du.rearrange("p c n -> p (c n)"), t, u, ALU.mult)
            for c in range(HC):
                last = V.tensor_scalar(ssm_y[:, m, :, c, :], ssm_u[:, c, :].rearrange("p (b l) -> p b l", b=B),
                                       ssm_par[:, 2, m, c:c + 1], None, ALU.mult)
            dve_link(last)
            V.memset(ssm_decay.rearrange("p a (n l) -> p (a n) l", l=S)[:, :, 0:1], 0.0).then_inc(s_sp_done, 1)

        def ssm_load_sp(sp, m, b, g):
            n = m * B * GB + b * GB + g
            if not (isinstance(b, int) and m == 0 and b == 0 and g < 2):
                sp.wait_ge(s_ssm_in, HC * (n - 1))
                sp.wait_ge(s_ssm_hC, HC * (n - 1))
            if g == 0 and isinstance(b, int) and b == 0:
                sp.wait_ge(s_sp_bc, 16 * (m + 1))
                sp.wait_ge(s_sp_done, m + 1)
            for k, (dst, sems) in enumerate(((ssm_B, s_ssm_B), (ssm_C, s_ssm_C))):
                src = bc_rows[m][ds(b, 1), k * DS + g * NB:k * DS + (g + 1) * NB, :].rearrange("a n l -> a (n l)")
                sp.dma_start(dst[:, g % 2, :], src.to_broadcast([P, NB * S])).then_inc(sems[g % 2], 16)

        def ssm_act(act, m, b, j):
            g, c = j // HC, j % HC
            q = m * GROUPS + b * GB * HC + j
            if j == 0 and isinstance(b, int) and b == 0:
                act.wait_ge(s_A, 1)
                act.wait_ge(s_sp_done, m + 1)
            if not (isinstance(b, int) and m == 0 and b == 0 and j < 2):
                act.wait_ge(s_ssm_h, q - 1)
                act.sem_inc(s_ssm_go, 1)
            for n in range(NB):
                last = nc.scalar.activation(ssm_decay[:, j % 2, n * S + 1:(n + 1) * S], ssm_delta[:, c, ds(b * S + 1, S - 1)],
                                            ACT.Exp, scale=ssm_A[:, m, c, NB * g + n:NB * g + n + 1])
            last.then_inc(s_ssm_decay, 1)

        def ssm_dve(dve, m, b, j, pool=False):
            g, c = j // HC, j % HC
            q = m * GROUPS + b * GB * HC + j
            turns = (m * B + b) * (GB // 2) + g // 2
            dve.wait_ge(s_ssm_B[g % 2], turns * 16 + 16)
            if not (isinstance(b, int) and m == 0 and b == 0 and j < 1):
                dve.wait_ge(s_ssm_h, q)
            nc.vector.tensor_tensor(ssm_in.rearrange("p (n l) -> p n l", n=NB),
                                    ssm_B[:, g % 2, :].rearrange("p (n l) -> p n l", n=NB),
                                    ssm_du[:, c, ds(b * S, S)].unsqueeze(1).to_broadcast([P, NB, S]),
                                    ALU.mult).then_inc(s_ssm_in, 1)
            dve.wait_ge(s_ssm_in, q + 1)
            dve.wait_ge(s_ssm_decay, q + 1)
            if not (isinstance(b, int) and m == 0 and b == 0 and j < 2):
                dve.wait_ge(s_ssm_hC, q - 1)
            nc.vector.tensor_tensor_scan(ssm_h[:, j % 2, :], ssm_decay[:, j % 2, :], ssm_in, 0.0,
                                         ALU.mult, ALU.add).then_inc(s_ssm_h, 1)
            if j == 1 and m == 0 and not (isinstance(b, int) and b == 0):
                ssm_sum_dve(dve, m, b - 1)
            if not pool:
                ssm_hC(dve, nc.vector, m, b, j)

        def ssm_hC(eng, ops, m, b, j):
            g = j // HC
            q = m * GROUPS + b * GB * HC + j
            turns = (m * B + b) * (GB // 2) + g // 2
            eng.wait_ge(s_ssm_h, q + 1)
            eng.wait_ge(s_ssm_C[g % 2], turns * 16 + 16)
            if not (isinstance(b, int) and b == 0 and j < 2):
                eng.wait_ge((s_ssm_sum, s_ssm_red)[m], b * GB * HC + (j - 1))
            ops.tensor_tensor(ssm_hC_buf[:, j % 2, :], ssm_h[:, j % 2, :], ssm_C[:, g % 2, :], ALU.mult).then_inc(s_ssm_hC, 1)

        def ssm_pe(pe, m, b, j):
            g, c = j // HC, j % HC
            q = m * GROUPS + b * GB * HC + j
            if g == 0 and not (isinstance(b, int) and m == 0 and b == 0):
                pe.wait_ge(s_ssm_y, HC * (m * B + b))
            pe.wait_ge(s_ssm_hC, q + 1)
            for n in range(NB):
                last = nc.tensor.matmul(bank[6 + c][:, 0:S], ident[:, :], ssm_hC_buf[:, j % 2, n * S:(n + 1) * S],
                                        start=(g == 0 and n == 0), stop=(g == GB - 1 and n == NB - 1))
            last.then_inc(s_ssm_sum, 1)

        def ssm_reduce_dve(dve, m, b, j):
            c = j % HC
            q = b * GB * HC + j
            dve.wait_ge(s_ssm_hC, m * GROUPS + q + 1)
            if not (isinstance(b, int) and b == 0 and j == 0):
                dve.wait_ge(s_ssm_red_y, q)
            nc.vector.tensor_reduce(ssm_part[:, :], ssm_hC_buf[:, j % 2, :].rearrange("p (n l) -> p l n", n=NB),
                                    AX_X, ALU.add).then_inc(s_ssm_red, 1)
            dve.wait_ge(s_ssm_red, q + 1)
            row = ssm_y[:, m, ds(b, 1), c, :].rearrange("p a l -> p (a l)")
            nc.vector.tensor_tensor(row, row, ssm_part[:, :], ALU.add).then_inc(s_ssm_red_y, 1)

        def ssm_sum_dve(dve, m, b):
            dve.wait_ge(s_ssm_sum, m * GROUPS + (b + 1) * GB * HC)
            for c in range(HC):
                row = ssm_y[:, m, ds(b, 1), c, :].rearrange("p a l -> p (a l)")
                nc.vector.tensor_tensor(row, row, bank[6 + c][:, 0:S], ALU.add).then_inc(s_ssm_y, 1)

        z_gate = y
        s_z_silu = sem("s_z_silu")
        s_z_prod = sem("s_z_prod")
        s_z_t = sem("s_z_t")
        s_z_x = sem("s_z_x")

        def gated_act(act, m, k):
            for b in range(B):
                act.wait_ge(s_y, NT * k + TPB * (b + 1))
                nc.scalar.activation(z_gate[:, TPB * b:TPB * (b + 1), :], y[:, TPB * b:TPB * (b + 1), :],
                                     ACT.Silu).then_inc(s_z_silu, 1)

        def gated_dve(dve, m, k):
            norm_dve(dve, k)
            if m:
                dve.wait_ge(s_ssm_red_y, GROUPS)
            else:
                dve.wait_ge(s_ssm_y, B * HC)
            for b in range(B + 1):
                if b < B:
                    dve.wait_ge(s_z_silu, m * B + b + 1)
                    rows = z_gate[:, TPB * b:TPB * (b + 1), :]
                    nc.vector.tensor_tensor(rows, rows, ssm_y[:, m, b, :, :], ALU.mult).then_inc(s_z_prod, 1)
                if b:
                    dve.wait_ge(s_z_t, m * B + b)
                    rows = x[:, TPB * (b - 1):TPB * b, :].rearrange("p a n -> p (a n)")
                    nc.vector.scalar_tensor_tensor(out=rows, in0=bank[b % 2][:, :], scalar=tanh_g[:, 0, 2 * m + 1:2 * m + 2],
                                                   in1=rows, op0=ALU.mult, op1=ALU.add).then_inc(s_z_x, 1)

        def gated_pe(pe, m):
            for b in range(B):
                pe.wait_ge(s_z_prod, m * B + b + 1)
                if b >= 2:
                    pe.wait_ge(s_z_x, m * B + b - 1)
                for j in range(TPB):
                    for c in range(HC):
                        last = nc.tensor.transpose(bank[(b + 1) % 2][:, j * S + c * P:j * S + (c + 1) * P],
                                                   z_gate[:, TPB * b + c, j * P:(j + 1) * P], ident[:, :])
                last.then_inc(s_z_t, 1)

        att_q = area(0, T)
        att_k = area(T, T)
        att_e = area(2 * T, 2, TPB, S)
        att_T = area(2 * T + 2 * TPB * S, 2, TPB, S)
        att_top = sb("att_top", [P, 2, TPB])
        att_sum = sb("att_sum", [P, 2, TPB])
        att_inv = sb("att_inv", [P, 2, TPB])
        s_l0_qkp = sem("s_l0_qkp")
        s_l0_qk = sem("s_l0_qk")
        s_l0_energy = sem("s_l0_energy")
        s_l0_top = sem("s_l0_top")
        s_l0_exp = sem("s_l0_exp")
        s_l0_att = sem("s_l0_att")
        s_l0_attTp = sem("s_l0_attTp")
        s_l0_attT = sem("s_l0_attT")
        s_l0_out = sem("s_l0_out")
        s_l0_x = sem("s_l0_x")

        def l0x_pe(pe):
            pe.wait_ge(s_sp_pad, 4)
            for w in range(2):
                for h in range(2):
                    nc.tensor.matmul(bank[2 + 2 * w + h][:, :], wqkT[:, w, :], ctxT[:, h * HALF:(h + 1) * HALF],
                                     start=True, stop=True).then_inc(s_l0_qkp, 1)
            norm_pe(pe, 0, 0)
            pe.wait_ge(s_l0_qk, 4)
            for b in range(B):
                energy = bank[2 + b % 2]
                if b >= 2:
                    pe.wait_ge(s_l0_exp, TPB * (b - 1))
                for i in range(TPB):
                    last = nc.tensor.matmul(energy[:, i * S:(i + 1) * S],
                                            att_q[:, b * S + i * P:b * S + (i + 1) * P], att_k[:, b * S:(b + 1) * S],
                                            start=True, stop=True)
                last.then_inc(s_l0_energy, 1)
                if b >= 1:
                    l0x_pe_out(pe, b - 1)
            l0x_pe_out(pe, B - 1)

        def l0x_pe_out(pe, b):
            turned = bank[4 + b % 2]
            pe.wait_ge(s_l0_att, b + 1)
            if b >= 2:
                pe.wait_ge(s_l0_attT, b - 1)
            for j in range(TPB):
                for i in range(TPB):
                    last = nc.tensor.transpose(turned[:, j * S + i * P:j * S + (i + 1) * P],
                                               att_e[:, b % 2, i, j * P:(j + 1) * P], ident[:, :])
            last.then_inc(s_l0_attTp, 1)
            pe.wait_ge(s_l0_attT, b + 1)
            pe.wait_ge(s_yT, NT // 2)
            if b >= 2:
                pe.wait_ge(s_l0_x, b - 1)
            for i in range(TPB):
                for j in range(TPB):
                    last = nc.tensor.matmul(bank[b % 2][:, i * S:(i + 1) * S],
                                            yT[:, j, b * S + i * P:b * S + (i + 1) * P], att_T[:, b % 2, j, :],
                                            start=(j == 0), stop=(j == TPB - 1))
            last.then_inc(s_l0_out, 1)

        def l0x_act(act):
            for w in range(2):
                for h in range(2):
                    act.wait_ge(s_l0_qkp, 2 * w + h + 1)
                    dst = (att_q, att_k)[w][:, h * HALF:(h + 1) * HALF]
                    nc.scalar.activation(dst, bank[2 + 2 * w + h][:, :], ACT.Identity,
                                         bias=bqk[:, w:w + 1]).then_inc(s_l0_qk, 1)
            norm_act(act, 0)
            for b in range(B):
                act.wait_ge(s_l0_top, b + 1)
                if b >= 2:
                    act.wait_ge(s_l0_attTp, b - 1)
                for i in range(TPB):
                    nc.scalar.activation(att_e[:, b % 2, i, :], bank[2 + b % 2][:, i * S:(i + 1) * S], ACT.Exp,
                                         bias=att_top[:, b % 2, i:i + 1],
                                         accum_out=att_sum[:, b % 2, i:i + 1]).then_inc(s_l0_exp, 1)
                if b >= 1:
                    l0x_act_turn(act, b - 1)
            l0x_act_turn(act, B - 1)

        def l0x_act_turn(act, b):
            act.wait_ge(s_l0_attTp, b + 1)
            if b >= 2:
                act.wait_ge(s_l0_out, b - 1)
            nc.scalar.copy(att_T[:, b % 2, :, :].rearrange("p a b -> p (a b)"), bank[4 + b % 2][:, :]).then_inc(s_l0_attT, 1)

        def l0x_dve(dve):
            dve.wait_ge(s_ld_x, 16)
            dve.wait_ge(s_prep, 2)
            norm_dve(dve, 0)
            for b in range(B):
                dve.wait_ge(s_l0_energy, b + 1)
                if b >= 2:
                    dve.wait_ge(s_l0_exp, TPB * (b - 1))
                nc.vector.tensor_reduce(att_top[:, b % 2, :], bank[2 + b % 2][:, :].rearrange("p (i n) -> p i n", i=TPB),
                                        AX_X, ALU.max, negate=True).then_inc(s_l0_top, 1)
                dve.wait_ge(s_l0_exp, TPB * (b + 1))
                dve_link(nc.vector.reciprocal(att_inv[:, b % 2, :], att_sum[:, b % 2, :]))
                for i in range(TPB):
                    last = nc.vector.tensor_scalar(att_e[:, b % 2, i, :], att_e[:, b % 2, i, :],
                                                   att_inv[:, b % 2, i:i + 1], None, ALU.mult)
                last.then_inc(s_l0_att, 1)
                if b >= 1:
                    l0x_dve_add(dve, b - 1)
            l0x_dve_add(dve, B - 1)

        def l0x_dve_add(dve, b):
            dve.wait_ge(s_l0_out, b + 1)
            if b == 0:
                dve.wait_ge(s_gate, 1)
            rows = x[:, TPB * b:TPB * (b + 1), :].rearrange("p a b -> p (a b)")
            nc.vector.scalar_tensor_tensor(out=rows, in0=bank[b % 2][:, :], scalar=tanh_g[:, 0, 0:1], in1=rows,
                                           op0=ALU.mult, op1=ALU.add).then_inc(s_l0_x, 1)

        E0, K0, CAP, F0 = 64, 8, 128, 128
        PAIRS = E0 // 2
        RING, TURN = 4, 8
        slot_token = nc.dram_tensor("slot_token", [CAP * E0, 1], I32, kind="Internal").ap()
        y_rows = nc.dram_tensor("y_rows", [T, D], F32, kind="Internal").ap()
        slot_out = nc.dram_tensor("slot_out", [CAP * E0, D], F32, kind="Internal").ap()
        at = 0
        f0_prob = area(at, NT, E0); at += NT * E0
        f0_left = area(at, NT, E0); at += NT * E0
        f0_eq = area(at, K0, E0); at += K0 * E0
        F0_W = at
        assert F0_W == F0_W_AT
        f0_wg = area(at, RING, 2, D); at += RING * 2 * D
        f0_wu = area(at, RING, 2, D); at += RING * 2 * D
        f0_wd = area(at, RING, 2, D); at += RING * 2 * D
        f0_xg = area(at, RING, 2, D); at += RING * 2 * D
        f0_xgT = area(at, RING, 2 * D); at += RING * 2 * D
        f0_sg = area(at, RING, 2 * P); at += RING * 2 * P
        f0_hT = area(at, RING, 2 * P); at += RING * 2 * P
        f0_act = area(at, 2 * P); at += 2 * P
        f0_ye = area(at, RING, 2 * D); at += RING * 2 * D
        F0_END = at
        GR = 3 * RING * 2
        f0_back = area(F0_W, GR, D)
        f0_mask = sb("f0_mask", [P, NT, E0], BF16)
        tri = sb("tri", [P, P], BF16)
        ones_b = sb("ones_b", [P, P], BF16)
        iota_e = sb("iota_e", [P, E0])
        token_id = sb("token_id", [P, NT], I32)
        zero_slots = sb("zero_slots", [P, E0], I32)
        slots = sb("slots", [P, E0], I32)
        f0_top = sb("f0_top", [P, NT])
        f0_sum = sb("f0_sum", [P, NT])
        f0_w = sb("f0_w", [P, NT, K0])
        f0_i = sb("f0_i", [P, NT, K0], U32)
        f0_if = sb("f0_if", [P, NT, K0])
        f0_pos = sb("f0_pos", [P, NT, K0])
        f0_ok = sb("f0_ok", [P, NT, K0])
        f0_loc = sb("f0_loc", [P, NT, K0])
        f0_put = sb("f0_put", [P, NT, K0], I32)
        f0_get = sb("f0_get", [P, NT, K0], I32)
        s_f0_const = sem("s_f0_const")
        s_f0_logit = sem("s_f0_logit")
        s_f0_top = sem("s_f0_top")
        s_f0_exp = sem("s_f0_exp")
        s_f0_mask = sem("s_f0_mask")
        s_f0_rank = sem("s_f0_rank")
        s_f0_idx = sem("s_f0_idx")
        s_f0_zero = sem("s_f0_zero")
        s_f0_yrows = sem("s_f0_yrows")
        s_f0_put = sem("s_f0_put")
        s_f0_slots = sem("s_f0_slots")
        s_f0_w = [sem(f"s_f0_w{r}") for r in range(RING)]
        s_f0_xg = [sem(f"s_f0_xg{r}") for r in range(RING)]
        s_f0_T = sem("s_f0_T")
        s_f0_xgT = sem("s_f0_xgT")
        s_f0_gu = sem("s_f0_gu")
        s_f0_sg = sem("s_f0_sg")
        s_f0_h = sem("s_f0_h")
        s_f0_act = sem("s_f0_act")
        s_f0_d = sem("s_f0_d")
        s_f0_ye = sem("s_f0_ye")
        s_f0_st = [sem(f"s_f0_st{r}") for r in range(RING)]
        GB_ROWS = 3
        s_f0_back = [sem(f"s_f0_back{r}") for r in range(GR // GB_ROWS)]
        s_f0_x = sem("s_f0_x")

        def f0_const_pool(pool):
            pool_link(nc.gpsimd.memset(tri[:, :], 1.0))
            nc.gpsimd.affine_select(out=tri[:, :], in_=tri[:, :], compare_op=ALU.is_gt, fill=0.0, base=0,
                                    pattern=[[1, P]], channel_multiplier=-1)
            nc.gpsimd.memset(ones_b[:, :], 1.0)
            nc.gpsimd.memset(zero_slots[:, :], 0)
            nc.gpsimd.iota(iota_e[:, :], [[1, E0]], base=0, channel_multiplier=0, allow_small_or_imprecise_dtypes=True)
            nc.gpsimd.iota(token_id[:, :], [[P, NT]], base=0, channel_multiplier=1).then_inc(s_f0_const, 1)

        def f0_weights_sp(sp):
            def load(n, r):
                for m, (dst, name) in enumerate(((f0_wg, "L0_ffn_w_gate"), (f0_wu, "L0_ffn_w_up"), (f0_wd, "L0_ffn_w_down"))):
                    if m < 2:
                        src = A[name].rearrange("e (p h) f -> p e (h f)", h=HD)
                    else:
                        src = A[name].rearrange("e f d -> f e d")
                    sp.dma_start(dst[:, r, :, :], src[:, ds(2 * n, 2), :]).then_inc(s_f0_w[r], 16)
            return load

        def f0_sp(sp):
            load = f0_weights_sp(sp)
            sp.wait_ge(s_f0_const, 1)
            sp.dma_start(slot_token.rearrange("(p n) a -> p (n a)", p=P), zero_slots[:, :]).then_inc(s_f0_zero, 16)
            sp.wait_ge(s_l0_out, B)
            for n in range(RING):
                load(n, n)
            sp.wait_ge(s_y, 2 * NT)
            sp.dma_start(y_rows.rearrange("(i p) d -> p i d", p=P), y[:, :, :]).then_inc(s_f0_yrows, 16)
            ssm_bc_sp(sp, 0)
            for g in range(GB):
                ssm_load_sp(sp, 0, 0, g)

            def step(n, r):
                sp.wait_ge(s_f0_ye, n + 1)
                sp.dma_start(slot_out.rearrange("(c e) d -> c e d", e=E0)[:, ds(2 * n, 2), :],
                             f0_ye[:, r, :].rearrange("p (e d) -> p e d", e=2)).then_inc(s_f0_st[r], 16)

            def scan_load(b, j):
                n = (j - 1) // 2 + 2
                ssm_load_sp(sp, 0, b + n // GB, n % GB)

            for n in range(TURN):
                step(n, n % RING)
                load(n + RING, n % RING)
                if n >= TURN - 3 and n % 2:
                    scan_load(0, n)
            with sp.Fori(1, PAIRS // TURN - 1) as i:
                for j in range(TURN):
                    step(i * TURN + j, j % RING)
                    load(i * TURN + (j + RING), j % RING)
                    if j % 2:
                        scan_load(i, j)
            for n in range(PAIRS - TURN, PAIRS):
                step(n, n % RING)
                if n + RING < PAIRS:
                    load(n + RING, n % RING)
                if n in (PAIRS - TURN + 1, PAIRS - TURN + 3):
                    scan_load(B - 1, n % TURN)

        def f0_pool(pool):
            pool.wait_ge(s_f0_zero, 16)
            pool.wait_ge(s_f0_idx, 1)
            for i in range(NT):
                for k in range(K0):
                    nc.gpsimd.indirect_dma_start(
                        out=slot_token, out_offset=bass.IndirectOffsetOnAxis(ap=f0_put[:, i, k:k + 1], axis=0),
                        in_=token_id[:, i:i + 1], in_offset=None, bounds_check=CAP * E0 - 1,
                        oob_is_err=False).then_inc(s_f0_put, 16)
            pool.wait_ge(s_f0_put, 16 * NT * K0)
            pool.dma_start(slots[:, :], slot_token.rearrange("(c e) a -> c (e a)", e=E0)).then_inc(s_f0_slots, 16)
            pool.wait_ge(s_f0_slots, 16)
            pool.wait_ge(s_f0_yrows, 16)
            for n in range(PAIRS):
                if n >= RING:
                    pool.wait_ge(s_f0_T, n - RING + 1)
                for e in range(2):
                    nc.gpsimd.indirect_dma_start(
                        out=f0_xg[:, n % RING, e, :], out_offset=None, in_=y_rows,
                        in_offset=bass.IndirectOffsetOnAxis(ap=slots[:, 2 * n + e:2 * n + e + 1], axis=0),
                        bounds_check=T - 1, oob_is_err=True).then_inc(s_f0_xg[n % RING], 16)
            for r in range(RING):
                pool.wait_ge(s_f0_st[r], 16 * ((PAIRS - r + RING - 1) // RING))
            for m in range(NT * K0):
                if m >= GR:
                    pool.wait_ge(s_f0_x, m - GR + 1)
                nc.gpsimd.indirect_dma_start(
                    out=f0_back[:, m % GR, :], out_offset=None, in_=slot_out,
                    in_offset=bass.IndirectOffsetOnAxis(ap=f0_get[:, m // K0, m % K0:m % K0 + 1], axis=0),
                    bounds_check=CAP * E0 - 1, oob_is_err=True).then_inc(s_f0_back[m % GR // GB_ROWS], 16)

        def f0_pe(pe):
            norm_pe(pe, 1, 1)
            pe.wait_ge(s_yT, NT)
            for i in range(NT):
                for h in range(HD):
                    last = nc.tensor.matmul(bank[2][:, i * E0:(i + 1) * E0], yT[:, h, i * P:(i + 1) * P], gwT[:, h, :],
                                            start=(h == 0), stop=(h == HD - 1))
            last.then_inc(s_f0_logit, 1)
            pe.wait_ge(s_f0_mask, 1)
            pe.wait_ge(s_f0_const, 1)
            for i in range(NT):
                for j in range(i + 1):
                    last = nc.tensor.matmul(bank[3][:, i * E0:(i + 1) * E0], tri[:, :] if j == i else ones_b[:, :],
                                            f0_mask[:, j, :], start=(j == 0), stop=(j == i))
            last.then_inc(s_f0_rank, 1)

            def turn(n, r, m, tn):
                pe.wait_ge(s_f0_xg[r], tn * 32 + 32)
                if not (isinstance(n, int) and n < 2):
                    pe.wait_ge(s_f0_xgT, n - 1)
                for e in range(2):
                    for h in range(HD):
                        last = nc.tensor.transpose(bank[m][:, (2 * e + h) * P:(2 * e + h + 1) * P],
                                                   f0_xg[:, r, e, h:D:HD], ident[:, :])
                last.then_inc(s_f0_T, 1)

            def gate_up(n, r, m, tn):
                pe.wait_ge(s_f0_xgT, n + 1)
                pe.wait_ge(s_f0_w[r], tn * 48 + 48)
                if not (isinstance(n, int) and n < 2):
                    pe.wait_ge(s_f0_h, n - 1)
                for w, wt in enumerate((f0_wg, f0_wu)):
                    for e in range(2):
                        for h in range(HD):
                            last = nc.tensor.matmul(bank[2 + m][:, (2 * w + e) * P:(2 * w + e + 1) * P],
                                                    wt[:, r, e, h * P:(h + 1) * P],
                                                    f0_xgT[:, r, (2 * e + h) * P:(2 * e + h + 1) * P],
                                                    start=(h == 0), stop=(h == HD - 1))
                last.then_inc(s_f0_gu, 1)

            def down(n, r, m, tn):
                pe.wait_ge(s_f0_h, n + 1)
                if not (isinstance(n, int) and n < 2):
                    pe.wait_ge(s_f0_ye, n - 1)
                for e in range(2):
                    last = nc.tensor.matmul(bank[4 + m][:, e * D:(e + 1) * D], f0_hT[:, r, e * P:(e + 1) * P],
                                            f0_wd[:, r, e, :], start=True, stop=True)
                last.then_inc(s_f0_d, 1)

            def args(i, k):
                return i * TURN + k, k % RING, k % 2, i * (TURN // RING) + k // RING

            ssm_dt_pe(pe, 0)
            for j in range(GB * HC):
                ssm_pe(pe, 0, 0, j)
            turn(*args(0, 0))
            for k in range(TURN):
                turn(*args(0, k + 1))
                gate_up(*args(0, k))
                if k:
                    down(*args(0, k - 1))
            with pe.Fori(1, PAIRS // TURN - 1) as i:
                for k in range(TURN):
                    turn(*args(i, k + 1))
                    gate_up(*args(i, k))
                    down(*args(i, k - 1))
                    if k:
                        ssm_pe(pe, 0, i, k - 1)
                ssm_pe(pe, 0, i, TURN - 1)
            last_turn = PAIRS // TURN - 1
            for k in range(TURN):
                if k < TURN - 1:
                    turn(*args(last_turn, k + 1))
                gate_up(*args(last_turn, k))
                down(*args(last_turn, k - 1))
                if k:
                    ssm_pe(pe, 0, last_turn, k - 1)
            down(*args(last_turn, TURN - 1))
            ssm_pe(pe, 0, last_turn, TURN - 1)

        def f0_act_eng(act):
            norm_act(act, 1)
            act.wait_ge(s_f0_top, 1)
            for i in range(NT):
                last = nc.scalar.activation(f0_prob[:, i, :], bank[2][:, i * E0:(i + 1) * E0], ACT.Exp,
                                            bias=f0_top[:, i:i + 1], accum_out=f0_sum[:, i:i + 1])
            last.then_inc(s_f0_exp, 1)

            def step(n, r, m):
                act.wait_ge(s_f0_T, n + 1)
                if not (isinstance(n, int) and n < RING):
                    act.wait_ge(s_f0_gu, n - (RING - 1))
                nc.scalar.copy(f0_xgT[:, r, :], bank[m][:, :]).then_inc(s_f0_xgT, 1)

            def silu(n, r, m):
                act.wait_ge(s_f0_gu, n + 1)
                if not (isinstance(n, int) and n < RING):
                    act.wait_ge(s_f0_h, n - (RING - 1))
                nc.scalar.activation(f0_sg[:, r, :], bank[2 + m][:, 0:2 * P], ACT.Tanh,
                                     scale=0.5).then_inc(s_f0_sg, 1)

            ssm_dt_act(act, 0)
            for j in range(GB * HC):
                ssm_act(act, 0, 0, j)
            step(0, 0, 0)
            for n in range(TURN):
                step(n + 1, (n + 1) % RING, (n + 1) % 2)
                silu(n, n % RING, n % 2)
            with act.Fori(1, PAIRS // TURN - 1) as i:
                for k in range(TURN):
                    step(i * TURN + (k + 1), (k + 1) % RING, (k + 1) % 2)
                    silu(i * TURN + k, k % RING, k % 2)
                    ssm_act(act, 0, i, k)
            for n in range(PAIRS - TURN, PAIRS):
                if n + 1 < PAIRS:
                    step(n + 1, (n + 1) % RING, (n + 1) % 2)
                silu(n, n % RING, n % 2)
                ssm_act(act, 0, B - 1, n % TURN)

        def f0_dve(dve):
            dve.wait_ge(s_l0_x, B)
            norm_dve(dve, 1)
            dve.wait_ge(s_f0_logit, 1)
            nc.vector.tensor_reduce(f0_top[:, :], bank[2][:, :].rearrange("p (i e) -> p i e", i=NT), AX_X, ALU.max,
                                    negate=True).then_inc(s_f0_top, 1)
            dve.wait_ge(s_f0_exp, 1)
            dve_link(nc.vector.reciprocal(f0_sum[:, :], f0_sum[:, :]))
            dve_link(nc.vector.tensor_tensor(f0_prob[:, :, :], f0_prob[:, :, :],
                                             f0_sum[:, :].unsqueeze(2).to_broadcast([P, NT, E0]), ALU.mult))
            for i in range(NT):
                last = nc.vector.max(f0_w[:, i, :], f0_prob[:, i, :])
            dve_link(last)
            for i in range(NT):
                nc.vector.match_replace(f0_left[:, i, :], f0_w[:, i, :], f0_prob[:, i, :], -1.0)
                last = nc.vector.max_index(f0_i[:, i, :], f0_w[:, i, :], f0_prob[:, i, :])
            dve_link(last)
            nc.vector.tensor_tensor(f0_mask[:, :, :], f0_left[:, :, :], f0_prob[:, :, :],
                                    ALU.not_equal).then_inc(s_f0_mask, 1)
            dve_link(nc.vector.tensor_copy(f0_if[:, :, :], f0_i[:, :, :]))
            dve.wait_ge(s_f0_const, 1)
            dve.wait_ge(s_f0_rank, 1)
            for i in range(NT):
                dve_link(nc.vector.tensor_tensor(f0_eq, iota_e[:, :].unsqueeze(1).to_broadcast([P, K0, E0]),
                                                 f0_if[:, i, :].unsqueeze(2).to_broadcast([P, K0, E0]), ALU.is_equal))
                dve_link(nc.vector.tensor_tensor(
                    f0_eq, f0_eq, bank[3][:, i * E0:(i + 1) * E0].unsqueeze(1).to_broadcast([P, K0, E0]), ALU.mult))
                dve_link(nc.vector.tensor_reduce(f0_pos[:, i, :], f0_eq, AX_X, ALU.add))
            dve_link(nc.vector.tensor_scalar(f0_ok[:, :, :], f0_pos[:, :, :], float(CAP), None, ALU.is_lt))
            dve_link(nc.vector.tensor_tensor(f0_w[:, :, :], f0_w[:, :, :], f0_ok[:, :, :], ALU.mult))
            dve_link(nc.vector.tensor_scalar(f0_w[:, :, :], f0_w[:, :, :], tanh_g[:, 1, 0:1], None, ALU.mult))
            dve_link(nc.vector.tensor_scalar(f0_pos[:, :, :], f0_pos[:, :, :], float(CAP - 1), float(E0), ALU.min, ALU.mult))
            dve_link(nc.vector.tensor_tensor(f0_loc[:, :, :], f0_pos[:, :, :], f0_if[:, :, :], ALU.add))
            dve_link(nc.vector.tensor_copy(f0_get[:, :, :], f0_loc[:, :, :]))
            dve_link(nc.vector.tensor_scalar(f0_ok[:, :, :], f0_ok[:, :, :], -float(CAP * E0), float(CAP * E0),
                                             ALU.mult, ALU.add))
            nc.vector.tensor_tensor(f0_put[:, :, :], f0_loc[:, :, :], f0_ok[:, :, :], ALU.add).then_inc(s_f0_idx, 1)

            def mult(n, r, m):
                dve.wait_ge(s_f0_sg, n + 1)
                if not (isinstance(n, int) and n < RING):
                    dve.wait_ge(s_f0_d, n - (RING - 1))
                if not (isinstance(n, int) and n < 1):
                    dve.wait_ge(s_f0_h, n)
                nc.vector.scalar_tensor_tensor(out=f0_act, in0=f0_sg[:, r, :], scalar=1.0, in1=bank[2 + m][:, 0:2 * P],
                                               op0=ALU.add, op1=ALU.mult).then_inc(s_f0_act, 1)
                dve.wait_ge(s_f0_act, n + 1)
                nc.vector.scalar_tensor_tensor(out=f0_hT[:, r, :], in0=f0_act, scalar=0.5, in1=bank[2 + m][:, 2 * P:4 * P],
                                               op0=ALU.mult, op1=ALU.mult).then_inc(s_f0_h, 1)

            def evict(n, r, m, tn):
                dve.wait_ge(s_f0_d, n + 1)
                if not (isinstance(n, int) and n < RING):
                    dve.wait_ge(s_f0_st[r], tn * 16)
                nc.vector.tensor_copy(f0_ye[:, r, :], bank[4 + m][:, :]).then_inc(s_f0_ye, 1)

            ssm_dt_dve(dve, 0)
            for j in range(GB * HC):
                ssm_dve(dve, 0, 0, j)
            for n in range(TURN):
                mult(n, n % RING, n % 2)
                if n:
                    evict(n - 1, (n - 1) % RING, (n - 1) % 2, (n - 1) // RING)
            with dve.Fori(1, PAIRS // TURN) as i:
                for k in range(TURN):
                    mult(i * TURN + k, k % RING, k % 2)
                    evict(i * TURN + (k - 1), (k - 1) % RING, (k - 1) % 2, i * (TURN // RING) + (k - 1) // RING)
                    ssm_dve(dve, 0, i, k)
            n = PAIRS - 1
            evict(n, n % RING, n % 2, n // RING)
            ssm_sum_dve(dve, 0, B - 1)
            for m in range(NT * K0):
                i, k = m // K0, m % K0
                if m == 4:
                    ssm_in_dve(dve, 1)
                if m == 20:
                    ssm_dt_dve(dve, 1)
                if m % GB_ROWS == 0:
                    fetched = min(GB_ROWS, NT * K0 - m) + GB_ROWS * (m // GR)
                    dve.wait_ge(s_f0_back[m % GR // GB_ROWS], 16 * fetched)
                if m:
                    dve.wait_ge(s_f0_x, m)
                nc.vector.scalar_tensor_tensor(out=x[:, i, :], in0=f0_back[:, m % GR, :], scalar=f0_w[:, i, k:k + 1],
                                               in1=x[:, i, :], op0=ALU.mult, op1=ALU.add).then_inc(s_f0_x, 1)

        A1, R1, K1 = 64, 16, 4
        AR = A1 * R1
        CH = AR // P
        l1_back_end = F0_W + GR * D
        l1_AT = area(l1_back_end, HD, AR)
        l1_BT = area(l1_back_end + 2048, CH, D)
        l1_raw = l1_back_end + 4096
        l1_Arows = area(l1_raw, CH, D)
        l1_Brows = area(l1_raw + 2048, HD, AR)
        l1_Wrows = area(0, HD, D)
        l1_WT = area(512, HD, D)
        l1_sq = area(l1_raw, AR)
        l1_mv = area(l1_raw + 1024, AR)
        l1_P = area(l1_raw + 2048, 2, AR)
        l1_free = F0_W + NT * S
        l1_PT = area(l1_free, 2, AR)
        l1_eq = area(l1_free + 2 * AR, K1 * A1)
        assert l1_free + 2 * AR + K1 * A1 <= l1_back_end
        l1_arrow = sb("l1_arrow", [P, A1])
        l1_top = sb("l1_top", [P, 8])
        l1_idx = sb("l1_idx", [P, 8], U32)
        l1_idxf = sb("l1_idxf", [P, 8])
        l1_mask = sb("l1_mask", [P, 2, A1])
        l1_v = sb("l1_v", [P, 2, R1])
        l1_bias = sb("l1_bias", [1, D])
        ones_row = sb("ones_row", [1, P])
        ones_col = sb("ones_col", [P, 1])
        s_l1_ld = sem("s_l1_ld")
        s_l1_pt = sem("s_l1_pt")
        s_l1_prep = sem("s_l1_prep")
        s_l1_vec = sem("s_l1_vec")
        s_l1_sq = sem("s_l1_sq")
        s_l1_mv = sem("s_l1_mv")
        s_l1_v = sem("s_l1_v")
        s_l1_P = sem("s_l1_P")
        s_l1_Pt = sem("s_l1_Pt")
        s_l1_PT = sem("s_l1_PT")
        s_l1_out = sem("s_l1_out")
        s_l1_x = sem("s_l1_x")
        s_ones = sem("s_ones")
        l1_groups = [([l1_Arows[:, 4 * q + i, h * P:(h + 1) * P] for i in range(4)], l1_AT[:, h, q * HALF:(q + 1) * HALF])
                     for h in range(HD) for q in range(2)]
        l1_groups += [([l1_Brows[:, jh, (2 * q + i) * P:(2 * q + i + 1) * P] for i in range(2) for jh in range(HD)],
                       l1_BT[:, 2 * q:2 * q + 2, :].rearrange("p a b -> p (a b)")) for q in range(CH // 2)]
        l1_groups += [([l1_Wrows[:, jh, h * P:(h + 1) * P] for h in range(HD) for jh in range(HD)],
                       l1_WT.rearrange("p a b -> p (a b)"))]

        def l1_loads_sp(sp):
            sp.wait_ge(s_f0_ye, PAIRS)
            for r in range(RING):
                sp.wait_ge(s_f0_st[r], 16 * (PAIRS // RING))
            sp.dma_start(l1_Brows.rearrange("p h (a r) -> p h a r", r=R1)[:, 0, :, :],
                         A["L1_ffn_B"].rearrange("a (h p) r -> p h a r", p=P)[:, 0, :, :]).then_inc(s_l1_ld, 16)
            sp.dma_start(l1_Brows.rearrange("p h (a r) -> p h a r", r=R1)[:, 1, :, :],
                         A["L1_ffn_B"].rearrange("a (h p) r -> p h a r", p=P)[:, 1, :, :]).then_inc(s_l1_ld, 16)
            sp.dma_start(l1_Arows, A["L1_ffn_A"].rearrange("a r h -> (a r) h").rearrange("(c p) h -> p c h", p=P)).then_inc(s_l1_ld, 16)
            sp.dma_start(l1_Wrows, A["L1_ffn_W"].rearrange("(c p) h -> p c h", p=P)).then_inc(s_l1_ld, 16)
            sp.dma_start(l1_bias[:, :], A["L1_ffn_bias"].rearrange("(a n) -> a n", a=1)).then_inc(s_l1_ld, 16)

        def turn_pe(pe, groups, banks, written, copied):
            for n, (blocks, dst) in enumerate(groups):
                if n >= 2:
                    pe.wait_ge(copied[0], copied[1] + n - 1)
                at = 0
                for src in blocks:
                    rows = src.shape[0]
                    last = nc.tensor.transpose(bank[banks[n % 2]][0:src.shape[1], at:at + rows], src, ident[0:rows, 0:rows])
                    at += rows
                last.then_inc(written[0], 1)

        def turn_act(act, groups, banks, written, copied):
            for n, (blocks, dst) in enumerate(groups):
                act.wait_ge(written[0], written[1] + n + 1)
                nc.scalar.copy(dst, bank[banks[n % 2]][0:dst.shape[0], 0:dst.shape[1]]).then_inc(copied[0], 1)

        def l1_prep_pe(pe):
            pe.wait_ge(s_l1_ld, 16 * 5)
            turn_pe(pe, l1_groups, (2, 3), (s_l1_pt, 0), (s_l1_prep, 0))

        def l1_prep_act(act):
            turn_act(act, l1_groups, (2, 3), (s_l1_pt, 0), (s_l1_prep, 0))

        def l1_pe(pe):
            norm_pe(pe, 3, 2)
            pe.wait_ge(s_yT, 3 * NT // 2)
            pe.wait_ge(s_l1_prep, len(l1_groups))
            pe.wait_ge(s_ones, 1)

            def vectors(i):
                if i >= 2:
                    pe.wait_ge(s_l1_mv, i - 1)
                for q in range(2):
                    for h in range(HD):
                        last = nc.tensor.matmul(bank[2 + 2 * (i % 2) + q][:, :], yT[:, h, i * P:(i + 1) * P],
                                                l1_AT[:, h, q * HALF:(q + 1) * HALF], start=(h == 0), stop=(h == HD - 1))
                last.then_inc(s_l1_vec, 1)

            vectors(0)
            for i in range(NT):
                if i + 1 < NT:
                    vectors(i + 1)
                dst = bank[i % 2][:, 0:D]
                if i >= 2:
                    pe.wait_ge(s_l1_x, i - 1)
                for h in range(HD):
                    nc.tensor.matmul(dst, yT[:, h, i * P:(i + 1) * P], l1_WT[:, h, :], start=(h == 0), stop=False)
                nc.tensor.matmul(dst, ones_row[0:1, :], l1_bias[0:1, :], start=False, stop=False)
                pe.wait_ge(s_l1_P, i + 1)
                if i:
                    pe.wait_ge(s_l1_PT, i)
                for c in range(CH):
                    last = nc.tensor.transpose(bank[6 + c // 4][:, (c % 4) * P:(c % 4 + 1) * P],
                                               l1_P[:, i % 2, c * P:(c + 1) * P], ident[:, :])
                last.then_inc(s_l1_Pt, 1)
                pe.wait_ge(s_l1_PT, i + 1)
                for c in range(CH):
                    last = nc.tensor.matmul(dst, l1_PT[:, i % 2, c * P:(c + 1) * P], l1_BT[:, c, :],
                                            start=False, stop=(c == CH - 1))
                last.then_inc(s_l1_out, 1)

        def l1_act(act):
            norm_act(act, 2)

            def squares(i):
                act.wait_ge(s_l1_vec, i + 1)
                if i:
                    act.wait_ge(s_l1_mv, i)
                for q in range(2):
                    last = nc.scalar.activation(l1_sq[:, q * HALF:(q + 1) * HALF], bank[2 + 2 * (i % 2) + q][:, :], ACT.Square)
                last.then_inc(s_l1_sq, 1)

            squares(0)
            for i in range(NT):
                ssm_act(act, 1, 0, i)
                if i + 1 < NT:
                    squares(i + 1)
                act.wait_ge(s_l1_Pt, i + 1)
                if i >= 2:
                    act.wait_ge(s_l1_out, i - 1)
                for q in range(2):
                    last = nc.scalar.copy(l1_PT[:, i % 2, q * HALF:(q + 1) * HALF], bank[6 + q][:, :])
                last.then_inc(s_l1_PT, 1)

        def l1_dve(dve):
            V = nc.vector
            dve.wait_ge(s_z_x, B)
            norm_dve(dve, 3)

            def choose(i):
                dve.wait_ge(s_l1_sq, i + 1)
                dve_link(V.tensor_reduce(l1_arrow[:, :], l1_sq.rearrange("p (a r) -> p a r", r=R1), AX_X, ALU.add))
                dve_link(V.max(l1_top[:, :], l1_arrow[:, :]))
                dve_link(V.max_index(l1_idx[:, :], l1_top[:, :], l1_arrow[:, :]))
                dve_link(V.tensor_copy(l1_idxf[:, :], l1_idx[:, :]))
                eq = l1_eq.rearrange("p (k a) -> p k a", k=K1)
                dve_link(V.tensor_tensor(eq, iota_e[:, :].unsqueeze(1).to_broadcast([P, K1, A1]),
                                         l1_idxf[:, 0:K1].unsqueeze(2).to_broadcast([P, K1, A1]), ALU.is_equal))
                if i >= 2:
                    dve.wait_ge(s_l1_P, i - 1)
                dve_link(V.tensor_reduce(l1_mask[:, i % 2, :], l1_eq.rearrange("p (k a) -> p a k", k=K1), AX_X, ALU.add))
                for q in range(2):
                    half = A1 // 2
                    last = V.tensor_tensor(l1_mv[:, q * HALF:(q + 1) * HALF].rearrange("p (a r) -> p a r", r=R1),
                                           bank[2 + 2 * (i % 2) + q][:, :].rearrange("p (a r) -> p a r", r=R1),
                                           l1_mask[:, i % 2, q * half:(q + 1) * half].unsqueeze(2).to_broadcast([P, half, R1]),
                                           ALU.mult)
                last.then_inc(s_l1_mv, 1)
                dve.wait_ge(s_l1_mv, i + 1)
                dve_link(V.tensor_reduce(l1_v[:, i % 2, :], l1_mv.rearrange("p (a r) -> p r a", r=R1), AX_X, ALU.add))
                V.tensor_scalar(l1_v[:, i % 2, :], l1_v[:, i % 2, :], 1.0 / (K1 * K1), None, ALU.mult).then_inc(s_l1_v, 1)

            def add(i):
                dve.wait_ge(s_l1_out, i + 1)
                V.scalar_tensor_tensor(out=x[:, i, :], in0=bank[i % 2][:, 0:D], scalar=tanh_g[:, 1, 1:2], in1=x[:, i, :],
                                       op0=ALU.mult, op1=ALU.add).then_inc(s_l1_x, 1)

            choose(0)
            for i in range(NT):
                ssm_dve(dve, 1, 0, i, pool=True)
                if i + 1 < NT:
                    choose(i + 1)
                if i:
                    ssm_reduce_dve(dve, 1, 0, i - 1)
                add(i)
            ssm_reduce_dve(dve, 1, 0, NT - 1)

        def l1_pool(pool):
            nc.gpsimd.memset(ones_col[:, :], 1.0)
            nc.gpsimd.memset(ones_row[:, :], 1.0).then_inc(s_ones, 1)
            for i in range(NT):
                pool.wait_ge(s_l1_v, i + 1)
                if i >= 2:
                    pool.wait_ge(s_l1_Pt, i - 1)
                if i < 2:
                    pool.wait_ge(s_l1_prep, len(l1_groups))
                nc.gpsimd.tensor_tensor(l1_P[:, i % 2, :].rearrange("p (a r) -> p a r", r=R1),
                                        l1_mask[:, i % 2, :].unsqueeze(2).to_broadcast([P, A1, R1]),
                                        l1_v[:, i % 2, :].unsqueeze(1).to_broadcast([P, A1, R1]),
                                        ALU.mult).then_inc(s_l1_P, 1)
                ssm_hC(pool, nc.gpsimd, 1, 0, i)

        H, HB = 16, 4
        L2_SCALE_EPS = EPS * P
        at = l1_free + 2 * AR + K1 * A1
        x_wq = area(at, 2, HD * P); at += 2 * HD * P
        x_wkv = area(at, 2, 2 * P); at += 2 * 2 * P
        x_wo = area(at, 2, D); at += 2 * D
        x_kT = area(at, 2, T); at += 2 * T
        x_qT = area(at, 2, T); at += 2 * T
        x_qsq = area(at, T); at += T
        x_P = area(at, 2, TPB * S); at += 2 * TPB * S
        x_PT = area(at, 2, TPB * S); at += 2 * TPB * S
        x_OT = area(at, 2, T); at += 2 * T
        assert at <= SSM_AT
        x_kv = area(0, 2 * NT, 2 * P)
        x_ksq = area(2 * NT * 2 * P, NT, P)
        assert 2 * NT * 2 * P + NT * P <= l1_free + 2 * AR + K1 * A1
        x_gqk = sb("x_gqk", [P, 2])
        x_kve = sb("x_kve", [P, NT])
        x_rk = sb("x_rk", [P, NT])
        x_qve = sb("x_qve", [P, NT])
        x_rq = sb("x_rq", [P, 2, NT])
        x_top = sb("x_top", [P, 2, TPB])
        x_nb = sb("x_nb", [P, 2, TPB])
        x_sum = sb("x_sum", [P, 2, TPB])
        x_inv = sb("x_inv", [P, 2, TPB])
        s_x_g = sem("s_x_g")
        s_x_gqk = sem("s_x_gqk")
        s_x_w = [sem(f"s_x_w{r}") for r in range(2)]
        s_x_wo_ld = sem("s_x_wo_ld")
        (s_x_kv, s_x_kvc, s_x_ksum, s_x_ksq, s_x_kve, s_x_rk, s_x_khat, s_x_kt, s_x_kTc, s_x_q, s_x_qc, s_x_qsq, s_x_ss,
         s_x_qve, s_x_rq, s_x_S, s_x_top, s_x_max, s_x_exp, s_x_inv, s_x_P, s_x_Pt, s_x_PTc, s_x_O, s_x_Oc, s_x_wo,
         s_x_add) = (sem("s_x_" + n) for n in (
             "kv kvc ksum ksq kve rk khat kt kTc q qc qsq ss qve rq S top max exp inv P Pt PTc O Oc wo add").split())

        def after(eng, sem_, value):
            if not (isinstance(value, int) and value <= 0):
                eng.wait_ge(sem_, value)

        def x_sp(sp):
            sp.dma_start(x_gqk[:, 0:1], A["L2_xattn_gq"].rearrange("(p a) -> p a", a=1)).then_inc(s_x_g, 16)
            sp.dma_start(x_gqk[:, 1:2], A["L2_xattn_gk"].rearrange("(p a) -> p a", a=1)).then_inc(s_x_g, 16)
            wq = A["L2_xattn_Wq"].rearrange("(h p) n -> p h n", h=HD)
            sp.wait_ge(s_f0_x, NT * K0)

            def load(h, r):
                sp.dma_start(x_wq[:, r, :].rearrange("p (h n) -> p h n", h=HD), wq[:, :, ds(h * P, P)]).then_inc(s_x_w[r], 16)
                sp.dma_start(x_wkv[:, r, 0:P], A["L2_xattn_Wk"][:, ds(h * P, P)]).then_inc(s_x_w[r], 16)
                sp.dma_start(x_wkv[:, r, P:2 * P], A["L2_xattn_Wv"][:, ds(h * P, P)]).then_inc(s_x_w[r], 16)

            def load_wo(u):
                sp.dma_start(x_wo, A["L2_xattn_Wo"].rearrange("(h p) n -> p h n", p=P)[:, ds(2 * u, 2), :]).then_inc(s_x_wo_ld, 16)

            load(0, 0)
            load(1, 1)
            load_wo(0)

            def head(i, k):
                h = i * HB + k
                if not (isinstance(h, int) and h >= H - 2):
                    sp.wait_ge(s_x_kv, 4 * h + 4)
                    sp.wait_ge(s_x_q, 2 * h + 2)
                    load(h + 2, k % 2)
                if k % 2 == 0 and not (isinstance(h, int) and h < 2):
                    sp.wait_ge(s_x_wo, 2 * h)
                    load_wo(i * (HB // 2) + k // 2)

            for k in range(HB):
                head(0, k)
            with sp.Fori(1, H // HB - 1) as i:
                for k in range(HB):
                    ssm_load_sp(sp, 1, i, k)
                    head(i, k)
            for k in range(HB):
                ssm_load_sp(sp, 1, H // HB - 1, k)
                head(H // HB - 1, k)

        def x_pe(pe):
            norm_pe(pe, 4, 3)
            pe.wait_ge(s_yT, 4 * NT // 2)

            def kv(h, r, p, turns):
                if p == 0:
                    pe.wait_ge(s_x_w[r], turns * 48 + 48)
                after(pe, s_x_kvc, 4 * h + p - 1)
                if p < 2:
                    after(pe, s_x_kTc, 2 * h)
                for t in range(2):
                    last = nc.tensor.matmul(bank[p % 2][:, t * 2 * P:(t + 1) * 2 * P],
                                            ctxT[:, (2 * p + t) * P:(2 * p + t + 1) * P], x_wkv[:, r, :], start=True, stop=True)
                last.then_inc(s_x_kv, 1)

            def q(h, r, n, turns):
                if n == 0:
                    after(pe, s_x_qve, h)
                after(pe, s_x_qc, 2 * h + n - 1)
                for c in range(HD):
                    last = nc.tensor.matmul(bank[2 + n][:, :], x_wq[:, r, c * P:(c + 1) * P],
                                            yT[:, c, n * HALF:(n + 1) * HALF], start=(c == 0), stop=(c == HD - 1))
                last.then_inc(s_x_q, 1)

            def ss(h):
                pe.wait_ge(s_x_qsq, 2 * h + 2)
                for t in range(NT):
                    last = nc.tensor.matmul(bank[2][:, t:t + 1], x_qsq[:, t * P:(t + 1) * P], ones_col[:, :],
                                            start=True, stop=True)
                last.then_inc(s_x_ss, 1)

            def kt(h, r):
                pe.wait_ge(s_x_khat, h + 1)
                for n in range(2):
                    for t in range(4):
                        last = nc.tensor.transpose(bank[n][:, t * P:(t + 1) * P], x_kv[:, NT * r + 4 * n + t, 0:P], ident[:, :])
                    last.then_inc(s_x_kt, 1)

            def piece(h, r, b, turns):
                if b == 0:
                    kv(h, r, 0, turns)
                    kv(h, r, 1, turns)
                elif b == 1:
                    kv(h, r, 2, turns)
                    kv(h, r, 3, turns)
                    q(h, r, 0, turns)
                elif b == 2:
                    q(h, r, 1, turns)
                else:
                    ss(h)
                    kt(h, r)

            def project_out(u, p, to):
                if p == 0:
                    pe.wait_ge(s_x_wo_ld, u * 16 + 16)
                    pe.wait_ge(s_x_Oc, 8 * u + 8)
                for t in range(2):
                    for e in range(2):
                        last = nc.tensor.matmul(bank[to][:, t * D:(t + 1) * D], x_OT[:, e, (2 * p + t) * P:(2 * p + t + 1) * P],
                                                x_wo[:, e, :], start=(e == 0), stop=(e == 1))
                last.then_inc(s_x_wo, 1)

            def turned(s, par):
                pe.wait_ge(s_x_P, s + 1)
                after(pe, s_x_PTc, s)
                for j in range(TPB):
                    for i in range(TPB):
                        last = nc.tensor.transpose(bank[6][:, j * S + i * P:j * S + (i + 1) * P],
                                                   x_P[:, par, i * S + j * P:i * S + (j + 1) * P], ident[:, :])
                last.then_inc(s_x_Pt, 1)

            def values(s, r, b):
                pe.wait_ge(s_x_PTc, s + 1)
                after(pe, s_x_Oc, s)
                for j in range(TPB):
                    last = nc.tensor.matmul(bank[7][:, 0:S], x_kv[:, NT * r + TPB * b + j, P:2 * P],
                                            x_PT[:, b % 2, j * S:(j + 1) * S], start=(j == 0), stop=(j == TPB - 1))
                last.then_inc(s_x_O, 1)

            def step(i, k, b, first=False, final=False):
                h = i * HB + k
                s = i * (HB * B) + (k * B + b)
                if b == 0:
                    pe.wait_ge(s_x_qc, 2 * h + 2)
                    pe.wait_ge(s_x_kTc, 2 * h + 2)
                after(pe, s_x_exp, s - 1)
                for t in range(TPB):
                    last = nc.tensor.matmul(bank[4 + b % 2][:, t * S:(t + 1) * S],
                                            x_qT[:, k % 2, b * S + t * P:b * S + (t + 1) * P],
                                            x_kT[:, k % 2, b * S:(b + 1) * S], start=True, stop=True)
                last.then_inc(s_x_S, 1)
                if not first:
                    turned(s - 1, (b - 1) % 2)
                wo = k % 2 == 0 and not (isinstance(h, int) and h < 2)
                if not final:
                    if wo and b:
                        pe.wait_ge(s_x_add, 2 * h - 4 + (1, 2, 4)[b - 1])
                    piece(h + 1, (k + 1) % 2, b, i * (HB // 2) + (k + 1) // 2)
                if not first:
                    values(s - 1, (k if b else k - 1) % 2, (b - 1) % B)
                if wo:
                    u = i * (HB // 2) + (k // 2 - 1)
                    if b < 2:
                        if b == 0:
                            pe.wait_ge(s_x_qve, h + 1)
                        project_out(u, b, 2 + b)
                    elif b == 2:
                        pe.wait_ge(s_x_kvc, 4 * h + 8)
                        project_out(u, 2, 0)
                        project_out(u, 3, 1)

            for b in range(B):
                piece(0, 0, b, 0)
            for k in range(HB):
                for b in range(B):
                    step(0, k, b, first=(k == 0 and b == 0))
            with pe.Fori(1, H // HB - 1) as i:
                for k in range(HB):
                    for b in range(B):
                        step(i, k, b)
            for k in range(HB):
                for b in range(B):
                    step(H // HB - 1, k, b, final=(k == HB - 1))
            turned(H * B - 1, 1)
            values(H * B - 1, 1, B - 1)
            for p in range(4):
                project_out(H // 2 - 1, p, p)

        def x_act(act):
            norm_act(act, 3)

            def ksq(h, r, p):
                act.wait_ge(s_x_kvc, 4 * h + p + 1)
                after(act, s_x_kve, h)
                nc.scalar.activation(x_ksq[:, 2 * p:2 * p + 2, :], x_kv[:, NT * r + 2 * p:NT * r + 2 * p + 2, 0:P],
                                     ACT.Square).then_inc(s_x_ksq, 1)

            def qcopy(h, r, n):
                act.wait_ge(s_x_q, 2 * h + n + 1)
                after(act, s_x_S, 4 * h - 4)
                nc.scalar.copy(x_qT[:, r, n * HALF:(n + 1) * HALF], bank[2 + n][:, :]).then_inc(s_x_qc, 1)
                act.wait_ge(s_x_qc, 2 * h + n + 1)
                after(act, s_x_ss, h)
                nc.scalar.activation(x_qsq[:, n * HALF:(n + 1) * HALF], x_qT[:, r, n * HALF:(n + 1) * HALF],
                                     ACT.Square).then_inc(s_x_qsq, 1)

            def kcopy(h, r):
                if isinstance(h, int) and h == 0:
                    act.wait_ge(s_x_gqk, 1)
                for n in range(2):
                    act.wait_ge(s_x_kt, 2 * h + n + 1)
                    after(act, s_x_S, 4 * h - 4)
                    nc.scalar.activation(x_kT[:, r, n * HALF:(n + 1) * HALF], bank[n][:, :], ACT.Copy,
                                         scale=x_gqk[:, 0:1]).then_inc(s_x_kTc, 1)

            def piece(h, r, b):
                if b == 0:
                    ksq(h, r, 0)
                    ksq(h, r, 1)
                elif b == 1:
                    ksq(h, r, 2)
                    ksq(h, r, 3)
                    qcopy(h, r, 0)
                elif b == 2:
                    qcopy(h, r, 1)
                else:
                    kcopy(h, r)

            def ptcopy(s, par):
                act.wait_ge(s_x_Pt, s + 1)
                after(act, s_x_O, s - 1)
                nc.scalar.copy(x_PT[:, par, :], bank[6][:, :]).then_inc(s_x_PTc, 1)

            def step(i, k, b, first=False, final=False, scan=True):
                h = i * HB + k
                s = i * (HB * B) + (k * B + b)
                if not first:
                    ptcopy(s - 1, (b - 1) % 2)
                act.wait_ge(s_x_max, s + 1)
                after(act, s_x_Pt, s - 1)
                for t in range(TPB):
                    last = nc.scalar.activation(x_P[:, b % 2, t * S:(t + 1) * S], bank[4 + b % 2][:, t * S:(t + 1) * S], ACT.Exp,
                                                bias=x_nb[:, b % 2, t:t + 1], scale=x_rq[:, k % 2, TPB * b + t:TPB * b + t + 1],
                                                accum_out=x_sum[:, b % 2, t:t + 1])
                last.then_inc(s_x_exp, 1)
                if scan and b % 2:
                    ssm_act(act, 1, i, 2 * k + b // 2)
                if not final:
                    piece(h + 1, (k + 1) % 2, b)

            for b in range(B):
                piece(0, 0, b)
            for k in range(HB):
                for b in range(B):
                    step(0, k, b, first=(k == 0 and b == 0), scan=False)
            with act.Fori(1, H // HB - 1) as i:
                for k in range(HB):
                    for b in range(B):
                        step(i, k, b)
            for k in range(HB):
                for b in range(B):
                    step(H // HB - 1, k, b, final=(k == HB - 1))
            ptcopy(H * B - 1, 1)

        def x_dve(dve):
            V = nc.vector
            dve.wait_ge(s_x_g, 32)
            V.tensor_tensor(x_gqk[:, 0:1], x_gqk[:, 0:1], x_gqk[:, 1:2], ALU.mult).then_inc(s_x_gqk, 1)
            dve.wait_ge(s_l1_x, NT)
            norm_dve(dve, 4)

            def kvcopy(h, r, p):
                dve.wait_ge(s_x_kv, 4 * h + p + 1)
                after(dve, s_x_O, 4 * h - 4)
                V.tensor_copy(x_kv[:, NT * r + 2 * p:NT * r + 2 * p + 2, :],
                              bank[p % 2][:, :].rearrange("p (t n) -> p t n", t=2)).then_inc(s_x_kvc, 1)

            def krms(h):
                dve.wait_ge(s_x_ksq, 4 * h + 4)
                after(dve, s_x_rk, h)
                V.tensor_reduce(x_kve[:, :], x_ksq, AX_X, ALU.add).then_inc(s_x_ksum, 1)
                dve.wait_ge(s_x_ksum, h + 1)
                V.tensor_scalar(x_kve[:, :], x_kve[:, :], 1.0 / P, EPS, ALU.mult, ALU.add).then_inc(s_x_kve, 1)

            def khat(h, r):
                dve.wait_ge(s_x_rk, h + 1)
                rows = x_kv[:, NT * r:NT * (r + 1), 0:P]
                V.tensor_tensor(rows, rows, x_rk[:, :].unsqueeze(2).to_broadcast([P, NT, P]), ALU.mult).then_inc(s_x_khat, 1)

            def qrms(h):
                dve.wait_ge(s_x_ss, h + 1)
                after(dve, s_x_rq, h)
                V.tensor_scalar(x_qve[:, :], bank[2][:, 0:NT], L2_SCALE_EPS, None, ALU.add).then_inc(s_x_qve, 1)

            def ocopy(s, r, b):
                dve.wait_ge(s_x_O, s + 1)
                V.tensor_copy(x_OT[:, r, b * S:(b + 1) * S], bank[7][:, 0:S]).then_inc(s_x_Oc, 1)

            def add(n, p, at_bank):
                dve.wait_ge(s_x_wo, n + 1)
                after(dve, s_x_add, n)
                rows = x[:, 2 * p:2 * p + 2, :].rearrange("p a n -> p (a n)")
                V.scalar_tensor_tensor(out=rows, in0=bank[at_bank][:, :], scalar=tanh_g[:, 0, 2:3], in1=rows,
                                       op0=ALU.mult, op1=ALU.add).then_inc(s_x_add, 1)

            def step(i, k, b, first=False, final=False, scan=True):
                h = i * HB + k
                s = i * (HB * B) + (k * B + b)
                par = b % 2
                if b == 0:
                    dve.wait_ge(s_x_rq, h + 1)
                dve.wait_ge(s_x_S, s + 1)
                after(dve, s_x_exp, s - 1)
                V.tensor_reduce(x_top[:, par, :], bank[4 + par][:, :].rearrange("p (t n) -> p t n", t=TPB), AX_X, ALU.max,
                                negate=True).then_inc(s_x_top, 1)
                dve.wait_ge(s_x_top, s + 1)
                V.tensor_tensor(x_nb[:, par, :], x_top[:, par, :], x_rq[:, k % 2, TPB * b:TPB * (b + 1)], ALU.mult).then_inc(s_x_max, 1)
                if scan and par:
                    ssm_dve(dve, 1, i, 2 * k + b // 2, pool=True)
                dve.wait_ge(s_x_exp, s + 1)
                V.reciprocal(x_inv[:, par, :], x_sum[:, par, :]).then_inc(s_x_inv, 1)
                dve.wait_ge(s_x_inv, s + 1)
                for t in range(TPB):
                    last = V.tensor_scalar(x_P[:, par, t * S:(t + 1) * S], x_P[:, par, t * S:(t + 1) * S],
                                           x_inv[:, par, t:t + 1], None, ALU.mult)
                last.then_inc(s_x_P, 1)
                if not first:
                    r, pb = (k if b else k - 1) % 2, (b - 1) % B
                    u = i * (HB // 2) + (k if b else k - 1) // 2
                    after(dve, s_x_wo, 4 * u + (pb - 3))
                    ocopy(s - 1, r, pb)
                if not final:
                    n, r = h + 1, (k + 1) % 2
                    if b < 2:
                        kvcopy(n, r, 2 * b)
                        kvcopy(n, r, 2 * b + 1)
                    elif b == 2:
                        krms(n)
                        khat(n, r)
                    else:
                        qrms(n)
                if k % 2 == 0 and not (isinstance(h, int) and h < 2):
                    u4 = 2 * h - 4
                    if b < 2:
                        add(u4 + b, b, 2 + b)
                    elif b == 2:
                        add(u4 + 2, 2, 0)
                        add(u4 + 3, 3, 1)
                if scan and par:
                    ssm_reduce_dve(dve, 1, i, 2 * k + b // 2)

            kvcopy(0, 0, 0)
            kvcopy(0, 0, 1)
            kvcopy(0, 0, 2)
            kvcopy(0, 0, 3)
            krms(0)
            khat(0, 0)
            qrms(0)
            for k in range(HB):
                for b in range(B):
                    step(0, k, b, first=(k == 0 and b == 0), scan=False)
            with dve.Fori(1, H // HB - 1) as i:
                for k in range(HB):
                    for b in range(B):
                        step(i, k, b)
            for k in range(HB):
                for b in range(B):
                    step(H // HB - 1, k, b, final=(k == HB - 1))
            after(dve, s_x_wo, 2 * H - 4)
            ocopy(H * B - 1, 1, B - 1)
            for p in range(4):
                add(2 * H - 4 + p, p, p)

        def x_pool(pool):
            def rms(n):
                pool.wait_ge(s_x_kve, n + 1)
                after(pool, s_x_khat, n)
                nc.gpsimd.tensor_tensor(x_rk[:, :], x_kve[:, :], minus_half[:, :], ALU.pow).then_inc(s_x_rk, 1)

            def qrms(n, r):
                pool.wait_ge(s_x_qve, n + 1)
                after(pool, s_x_exp, 4 * n - 4)
                nc.gpsimd.tensor_tensor(x_rq[:, r, :], x_qve[:, :], minus_half[:, :], ALU.pow).then_inc(s_x_rq, 1)

            def head(i, k, final=False, scan=True):
                h = i * HB + k
                if scan:
                    ssm_hC(pool, nc.gpsimd, 1, i, 2 * k)
                if not final:
                    rms(h + 1)
                    qrms(h + 1, (k + 1) % 2)
                if scan:
                    ssm_hC(pool, nc.gpsimd, 1, i, 2 * k + 1)

            rms(0)
            qrms(0, 0)
            for k in range(HB):
                head(0, k, scan=False)
            with pool.Fori(1, H // HB - 1) as i:
                for k in range(HB):
                    head(i, k)
            for k in range(HB):
                head(H // HB - 1, k, final=(k == HB - 1))

        E2, F2, FS2, K2 = 8, 176, 352, 2
        RC = E2 * F2 // P
        g_rows = [P] * RC + [min(P, FS2 - i * P) for i in range(-(-FS2 // P))]
        GC = len(g_rows)
        at = 0
        g_gT = area(at, GC * D); at += GC * D
        g_uT = area(at, GC * D); at += GC * D
        g_dT = area(at, GC, D); at += GC * D
        g_wbc = area(at, RC, T); at += RC * T
        g_raw = ARENA - (2 * GC * D + HD * (E2 * F2 + FS2))
        assert at <= g_raw and SSM_AT <= g_raw
        g_raw_g = area(g_raw, GC, D)
        g_raw_u = area(g_raw + GC * D, GC, D)
        g_raw_d = area(g_raw + 2 * GC * D, HD, E2 * F2 + FS2)
        g_sg = area(g_raw, 2, HALF)
        g_m = area(g_raw + 2 * HALF, HALF)
        g_hT = area(g_raw + 3 * HALF, 4, HALF)
        g_wr = sb("g_wr", [E2, D])
        e_gw = sb("e_gw", [32, D])
        e_gwT = sb("e_gwT", [P, HD, 32])
        g_wrT = sb("g_wrT", [P, HD, E2])
        g_p = sb("g_p", [P, NT, E2])
        g_top = sb("g_top", [P, NT])
        g_sum = sb("g_sum", [P, NT])
        g_best = sb("g_best", [P, NT, 8])
        g_idx = sb("g_idx", [P, NT, 8], U32)
        g_idxf = sb("g_idxf", [P, NT, 8])
        g_eq = sb("g_eq", [P, NT, 2, E2])
        g_w = sb("g_w", [P, NT, E2])
        g_wT = ssm_y[0:E2, 0, :, :, :].rearrange(
            "p b c l -> p (b c l)")[:, 0:T]
        w_rows = nc.dram_tensor("w_rows", [E2, T], F32, kind="Internal").ap()

        def wait(eng, signal, value):
            eng.wait_ge(signal[0], signal[1] + value)

        s_g_ld = (s_l1_ld, 16 * 5)
        s_g_pt = (s_l1_pt, len(l1_groups))
        s_g_prep = (s_l1_prep, len(l1_groups))
        s_g_logit = (s_l1_vec, NT)
        s_g_top = (s_l1_sq, NT)
        s_g_exp = (s_l1_mv, NT)
        s_g_w = (s_l1_v, NT)
        s_g_wt = (s_l1_Pt, NT)
        s_g_wT = (s_l1_PT, NT)
        s_g_rows = (s_x_g, 32)
        s_g_bc = (s_x_wo_ld, 16 * H // 2)
        s_g_gu = (s_l1_P, NT)
        s_g_sg = (s_x_ksq, 4 * H)
        s_g_h = (s_x_kvc, 4 * H)
        s_g_d = (s_l1_out, NT)
        s_g_x = (s_l1_x, NT)
        GL = 11
        g_groups = [([g_wr[:, h * P:(h + 1) * P] for h in range(HD)], g_wrT[:, :, :].rearrange("p h e -> p (h e)"))]
        g_groups.append(([e_gw[:, h * P:(h + 1) * P] for h in range(HD)], e_gwT[:, :, :].rearrange("p h e -> p (h e)")))
        for raw, dst in ((g_raw_g, g_gT), (g_raw_u, g_uT)):
            for c in range(0, GC, 2):
                cols = sum(HD * g_rows[k] for k in (c, c + 1))
                g_groups.append(([raw[0:g_rows[k], k, h * P:(h + 1) * P] for k in (c, c + 1) for h in range(HD)],
                                 dst[:, c * D:c * D + cols]))
        for cs in [(c, c + 1) for c in range(0, GC - 2, 2)] + [(GC - 2,), (GC - 1,)]:
            rows = g_rows[cs[0]]
            g_groups.append(([g_raw_d[:, jh, c * P:c * P + rows] for c in cs for jh in range(HD)],
                             g_dT[0:rows, cs[0]:cs[-1] + 1, :].rearrange("p c n -> p (c n)")))
        g_spans = []
        for e in range(E2):
            f = e * F2
            while f < (e + 1) * F2:
                stop = min((f // P + 1) * P, (e + 1) * F2)
                g_spans.append((f // P, f % P, stop - f // P * P, e))
                f = stop

        def g_sp(sp):
            sp.wait_ge(s_ssm_red_y, GROUPS)
            pad = FS2 // P * P
            for dst, name, shared in ((g_raw_g, "Wg", "Wsg"), (g_raw_u, "Wu", "Wsu")):
                sp.dma_start(dst[:, 0:RC, :], A["L2_ffn_" + name].rearrange("e f d -> (e f) d").rearrange(
                    "(c p) d -> p c d", p=P)).then_inc(s_g_ld[0], 16)
                sp.dma_start(dst[:, RC:GC - 1, :], A["L2_ffn_" + shared][0:pad, :].rearrange("(c p) d -> p c d", p=P)
                             ).then_inc(s_g_ld[0], 16)
                sp.dma_start(dst[0:FS2 - pad, GC - 1, :], A["L2_ffn_" + shared][pad:FS2, :]).then_inc(s_g_ld[0], 16)
            for jh in range(HD):
                sp.dma_start(g_raw_d[:, jh, 0:E2 * F2].rearrange("p (e f) -> p e f", e=E2),
                             A["L2_ffn_Wd"].rearrange("e (h p) f -> p h e f", p=P)[:, jh, :, :]).then_inc(s_g_ld[0], 16)
            sp.dma_start(g_raw_d[:, :, E2 * F2:], A["L2_ffn_Wsd"].rearrange("(h p) f -> p h f", p=P)).then_inc(s_g_ld[0], 16)
            sp.dma_start(g_wr[:, :], A["L2_ffn_Wr"]).then_inc(s_g_ld[0], 16)
            sp.dma_start(e_gw[:, :], A["L3_ffn_gate_w"]).then_inc(s_g_ld[0], 16)
            wait(sp, s_g_wT, 2)
            sp.dma_start(w_rows, g_wT[:, :]).then_inc(s_g_rows[0], 16)
            wait(sp, s_g_rows, 16)
            for c, p0, p1, e in g_spans:
                sp.dma_start(g_wbc[p0:p1, c, :], w_rows[e:e + 1, :].to_broadcast([p1 - p0, T])).then_inc(s_g_bc[0], 16)

        g_steps = [(n, c) for n in range(2) for c in list(range(RC, GC)) + list(range(RC))]

        def g_pe(pe):
            wait(pe, s_g_ld, 16 * GL)
            turn_pe(pe, g_groups, (4, 5), s_g_pt, s_g_prep)
            norm_pe(pe, 5, 4)
            pe.wait_ge(s_yT, 5 * NT // 2)
            wait(pe, s_g_prep, len(g_groups))
            for i in range(NT):
                for h in range(HD):
                    last = nc.tensor.matmul(bank[6][:, i * E2:(i + 1) * E2], yT[:, h, i * P:(i + 1) * P], g_wrT[:, h, :],
                                            start=(h == 0), stop=(h == HD - 1))
            last.then_inc(s_g_logit[0], 1)

            def gate_up(t):
                n, c = g_steps[t]
                rows = g_rows[c]
                if t >= 2:
                    wait(pe, s_g_h, t - 1)
                for w, wt in enumerate((g_gT, g_uT)):
                    for h in range(HD):
                        last = nc.tensor.matmul(bank[2 * (t % 2) + w][0:rows, :], wt[:, c * D + h * rows:c * D + (h + 1) * rows],
                                                yT[:, h, n * HALF:(n + 1) * HALF], start=(h == 0), stop=(h == HD - 1))
                last.then_inc(s_g_gu[0], 1)

            def down(t):
                n, c = g_steps[t]
                rows = g_rows[c]
                wait(pe, s_g_h, t + 1)
                for i in range(NT // 2):
                    last = nc.tensor.matmul(bank[4 + 2 * n + i // 2][:, i % 2 * D:(i % 2 + 1) * D],
                                            g_hT[0:rows, t % 4, i * P:(i + 1) * P], g_dT[0:rows, c, :],
                                            start=(t % GC == 0 and i % 2 == 0), stop=(t % GC == GC - 1),
                                            skip_group_check=True)
                last.then_inc(s_g_d[0], 1)

            gate_up(0)
            gate_up(1)
            wait(pe, s_g_w, 1)
            for q in range(2):
                for i in range(4):
                    last = nc.tensor.transpose(bank[6 + q][0:E2, i * P:(i + 1) * P], g_w[:, 4 * q + i, :], ident[:, :])
            last.then_inc(s_g_wt[0], 1)
            for t in range(2 * GC):
                if t == GC:
                    wait(pe, s_g_wT, 2)
                if t + 1 < 2 * GC and t:
                    gate_up(t + 1)
                down(t)

        def g_act(act):
            act.wait_ge(s_x_add, 2 * H)
            turn_act(act, g_groups, (4, 5), s_g_pt, s_g_prep)
            norm_act(act, 4)
            wait(act, s_g_top, 1)
            for i in range(NT):
                last = nc.scalar.activation(g_p[:, i, :], bank[6][:, i * E2:(i + 1) * E2], ACT.Exp,
                                            bias=g_top[:, i:i + 1], accum_out=g_sum[:, i:i + 1])
            last.then_inc(s_g_exp[0], 1)
            for t in range(2 * GC):
                if t == 2:
                    wait(act, s_g_wt, 1)
                    for q in range(2):
                        nc.scalar.copy(g_wT[:, q * HALF:(q + 1) * HALF], bank[6 + q][0:E2, :]).then_inc(s_g_wT[0], 1)
                rows = g_rows[g_steps[t][1]]
                wait(act, s_g_gu, t + 1)
                if t >= 2:
                    wait(act, s_g_h, t - 1)
                nc.scalar.activation(g_sg[0:rows, t % 2, :], bank[2 * (t % 2)][0:rows, :], ACT.Silu).then_inc(s_g_sg[0], 1)

        def g_dve(dve):
            V = nc.vector
            dve.wait_ge(s_x_add, 2 * H)
            norm_dve(dve, 5)
            wait(dve, s_g_logit, 1)
            V.tensor_reduce(g_top[:, :], bank[6][:, 0:NT * E2].rearrange("p (i e) -> p i e", i=NT), AX_X, ALU.max,
                            negate=True).then_inc(s_g_top[0], 1)
            wait(dve, s_g_exp, 1)
            dve_link(V.reciprocal(g_sum[:, :], g_sum[:, :]))
            dve_link(V.tensor_tensor(g_p[:, :, :], g_p[:, :, :], g_sum[:, :].unsqueeze(2).to_broadcast([P, NT, E2]), ALU.mult))
            for i in range(NT):
                last = V.max(g_best[:, i, :], g_p[:, i, :])
            dve_link(last)
            for i in range(NT):
                last = V.max_index(g_idx[:, i, :], g_best[:, i, :], g_p[:, i, :])
            dve_link(last)
            dve_link(V.tensor_copy(g_idxf[:, :, :], g_idx[:, :, :]))
            for i in range(NT):
                last = V.tensor_tensor(g_eq[:, i, :, :], iota_e[:, 0:E2].unsqueeze(1).to_broadcast([P, K2, E2]),
                                       g_idxf[:, i, 0:K2].unsqueeze(2).to_broadcast([P, K2, E2]), ALU.is_equal)
            dve_link(last)
            dve_link(V.tensor_tensor(g_w[:, :, :], g_eq[:, :, 0, :], g_eq[:, :, 1, :], ALU.add))
            V.tensor_tensor(g_w[:, :, :], g_w[:, :, :], g_p[:, :, :], ALU.mult).then_inc(s_g_w[0], 1)

            def add(n):
                wait(dve, s_g_d, GC * (n + 1))
                for i in range(2):
                    rows = x[:, 4 * n + 2 * i:4 * n + 2 * i + 2, :].rearrange("p a n -> p (a n)")
                    V.scalar_tensor_tensor(out=rows, in0=bank[4 + 2 * n + i][:, :], scalar=tanh_g[:, 1, 2:3], in1=rows,
                                           op0=ALU.mult, op1=ALU.add).then_inc(s_g_x[0], 1)

            for t in range(2 * GC):
                n, c = g_steps[t]
                rows = g_rows[c]
                wait(dve, s_g_sg, t + 1)
                if t >= 4:
                    wait(dve, s_g_d, t - 3)
                if t:
                    wait(dve, s_g_h, t)
                h = g_hT[0:rows, t % 4, :]
                if c >= RC:
                    V.tensor_tensor(h, g_sg[0:rows, t % 2, :], bank[2 * (t % 2) + 1][0:rows, :], ALU.mult).then_inc(s_g_h[0], 1)
                else:
                    if t == GC - RC:
                        wait(dve, s_g_bc, 16 * len(g_spans))
                    dve_link(V.tensor_tensor(g_m, g_sg[:, t % 2, :], bank[2 * (t % 2) + 1][:, :], ALU.mult))
                    V.tensor_tensor(h, g_m, g_wbc[:, c, n * HALF:(n + 1) * HALF], ALU.mult).then_inc(s_g_h[0], 1)
                if t == GC:
                    add(0)
            add(1)

        E3, F3, K3, GROUP3 = 32, 96, 4, 2
        E3S, F3S, SMALL = E3 // GROUP3, 128, 0.05
        TILES = T * K3 // P + E3
        assert TILES == E0 and F3S == P
        at = 0
        e_w = arena[:, at:at + E3 * HD * 2 * F3].rearrange(
            "p (e h n) -> p e h n", e=E3, h=HD); at += E3 * HD * 2 * F3
        e_cw = arena[:, at:at + E3S * HD * 2 * F3S].rearrange("p (e h n) -> p e h n", e=E3S, h=HD); at += E3S * HD * 2 * F3S
        e_wd = area(at, E3, D); at += E3 * D
        e_cwd = area(at, E3S, D); at += E3S * D
        assert at <= ARENA
        e_back = area(0, NT * K3, D)
        scan_y = ssm_y[:, :, :, :, :].rearrange("p m b c l -> p (m b c l)")
        e_xg = scan_y[:, 0:4 * D].rearrange("p (r n) -> p r n", r=4)
        e_xgT = scan_y[:, 4 * D:8 * D].rearrange("p (r n) -> p r n", r=4)
        e_sg = scan_y[:, 8 * D:10 * D].rearrange("p (r n) -> p r n", r=2)
        e_h = scan_y[:, 10 * D:12 * D].rearrange("p (r n) -> p r n", r=2)
        e_hT = scan_y[:, 12 * D:14 * D].rearrange("p (r n) -> p r n", r=2)
        e_ye = ctxT[:, :].rearrange("p (r n) -> p r n", r=4)
        e_eq = yT[:, 0, :].rearrange("p (i k e) -> p i k e", i=NT, k=K3)
        e_eq2 = yT[:, 1, :].rearrange("p (i k e) -> p i k e", i=NT, k=K3)
        e_cmp = yT[:, :, :].rearrange("p h n -> p (h n)").rearrange("p (t e) -> p t e", e=E3)
        e_mask = f0_mask[:, :, 0:E3]
        e_p = sb("e_p", [P, NT, E3])
        e_sig = sb("e_sig", [P, NT, E3])
        e_pos = sb("e_pos", [P, NT, E3])
        e_top = sb("e_top", [P, NT])
        e_sum = sb("e_sum", [P, NT])
        e_wk = sb("e_wk", [P, NT, K3])
        e_wsum = sb("e_wsum", [P, NT])
        e_locf = sb("e_locf", [P, NT, K3])
        e_loc = sb("e_loc", [P, NT, K3], I32)
        e_low = sb("e_low", [P, NT, K3], I32)
        e_tot = sb("e_tot", [P, E3])
        e_ge = sb("e_ge", [P, E3, NT])
        e_tiles = sb("e_tiles", [P, E3])
        e_cum = sb("e_cum", [P, E3])
        e_base = sb("e_base", [P, E3])
        e_tabf = e_sig[:, :, :].rearrange("p i e -> p (i e)")[:, 0:2 * TILES].rearrange("p (a t) -> p a t", a=2)
        e_tab = sb("e_tab", [P, 2, TILES], I32)
        s_e_new = sem("s_e_new")
        s_e_tab = sem("s_e_tab")
        s_e_pad = sem("s_e_pad")
        s_e_logit, s_e_top, s_e_exp, s_e_mask, s_e_rank, s_e_idx = (
            (s, 1) for s in (s_f0_logit, s_f0_top, s_f0_exp, s_f0_mask, s_f0_rank, s_f0_idx))
        s_e_zero, s_e_yrows, s_e_slots = (s_f0_zero, 16), (s_f0_yrows, 16), (s_f0_slots, 16)
        s_e_put = (s_f0_put, 16 * NT * K0)
        s_e_xg = [(s, 2 * 16 * PAIRS // RING) for s in s_f0_xg]
        s_e_T, s_e_xgT, s_e_gu, s_e_sg, s_e_mul, s_e_Ht, s_e_d, s_e_ye = (
            (s, PAIRS) for s in (s_f0_T, s_f0_xgT, s_f0_gu, s_f0_sg, s_f0_h, s_f0_act, s_f0_d, s_f0_ye))
        s_e_hTc = (s_x_O, H * B)
        s_e_st = [(s, 16 * PAIRS // RING) for s in s_f0_st]
        s_e_ld = (s_x_w[0], 48 * H // 2)
        s_e_back = [(s, 16 * len([m for m in range(NT * K0) if m % GR // GB_ROWS == g])) for g, s in enumerate(s_f0_back)]
        s_e_x = (s_f0_x, NT * K0)
        EL = 10

        def e_sp(sp):
            sp.dma_start(slot_token.rearrange("(p n) a -> p (n a)", p=P), zero_slots[:, :]).then_inc(s_e_zero[0], 16)
            wait(sp, s_g_x, 4)
            for dst, n, name in ((e_w, F3, "W"), (e_cw, F3S, "cW")):
                for w, kind in enumerate("gu"):
                    src = A["L3_ffn_" + name + kind].rearrange("e (h p) i -> p h e i", p=P)
                    for h in range(HD):
                        sp.dma_start(dst[:, :, h, w * n:(w + 1) * n], src[:, h, :, :]).then_inc(s_e_ld[0], 16)
            sp.dma_start(e_wd[0:F3, :, :], A["L3_ffn_Wd"].rearrange("e i n -> i e n")).then_inc(s_e_ld[0], 16)
            sp.dma_start(e_cwd, A["L3_ffn_cWd"].rearrange("e i n -> i e n")).then_inc(s_e_ld[0], 16)
            sp.wait_ge(s_y, 8 * NT)
            sp.dma_start(y_rows.rearrange("(i p) d -> p i d", p=P), y[:, :, :]).then_inc(s_e_yrows[0], 16)

            def store(t, r):
                wait(sp, s_e_ye, t + 1)
                sp.dma_start(slot_out.rearrange("(c t) d -> c t d", t=TILES)[:, ds(t, 1), :],
                             e_ye[:, r, :].unsqueeze(1)).then_inc(s_e_st[r][0], 16)

            with sp.Fori(0, TILES // 4) as i:
                for k in range(4):
                    store(i * 4 + k, k)

        def e_pool(pool):
            norm_pool(pool, 7)
            wait(pool, s_e_zero, 16)
            wait(pool, s_e_idx, 1)
            for i in range(NT):
                for k in range(K3):
                    nc.gpsimd.indirect_dma_start(
                        out=slot_token, out_offset=bass.IndirectOffsetOnAxis(ap=e_loc[:, i, k:k + 1], axis=0),
                        in_=token_id[:, i:i + 1], in_offset=None, bounds_check=CAP * E0 - 1,
                        oob_is_err=True).then_inc(s_e_put[0], 16)
            wait(pool, s_e_put, 16 * NT * K3)
            pool.dma_start(slots[:, :], slot_token.rearrange("(c t) a -> c (t a)", t=TILES)).then_inc(s_e_slots[0], 16)
            wait(pool, s_e_slots, 16)
            wait(pool, s_e_yrows, 16)
            for t in range(TILES):
                if t >= 4:
                    wait(pool, s_e_T, t - 3)
                nc.gpsimd.indirect_dma_start(
                    out=e_xg[:, t % 4, :], out_offset=None, in_=y_rows,
                    in_offset=bass.IndirectOffsetOnAxis(ap=slots[:, t:t + 1], axis=0),
                    bounds_check=T - 1, oob_is_err=True).then_inc(s_e_xg[t % 4][0], 16)
            for r in range(4):
                wait(pool, s_e_st[r], 16 * TILES // 4)
            for m in range(NT * K3):
                nc.gpsimd.indirect_dma_start(
                    out=e_back[:, m, :], out_offset=None, in_=slot_out,
                    in_offset=bass.IndirectOffsetOnAxis(ap=e_loc[:, m // K3, m % K3:m % K3 + 1], axis=0),
                    bounds_check=CAP * E0 - 1, oob_is_err=True).then_inc(s_e_back[m // K3][0], 16)

        def e_route_pe(pe):
            norm_pe(pe, 7, 5)
            pe.wait_ge(s_yT, 6 * NT // 2)
            for i in range(NT):
                for h in range(HD):
                    last = nc.tensor.matmul(bank[2][:, i * E3:(i + 1) * E3], yT[:, h, i * P:(i + 1) * P], e_gwT[:, h, :],
                                            start=(h == 0), stop=(h == HD - 1))
            last.then_inc(s_e_logit[0], 1)
            wait(pe, s_e_mask, 1)
            for j in range(NT):
                nc.tensor.matmul(bank[4][:, 0:E3], ones_b[:, :], e_mask[:, j, :], start=(j == 0), stop=(j == NT - 1))
            for i in range(NT):
                for j in range(i + 1):
                    last = nc.tensor.matmul(bank[3][:, i * E3:(i + 1) * E3], tri[:, :] if j == i else ones_b[:, :],
                                            e_mask[:, j, :], start=(j == 0), stop=(j == i))
            last.then_inc(s_e_rank[0], 1)

        def e_steps(eng, step):
            turns = TILES // 4
            for k in range(4):
                step(k, k)
            with eng.Fori(1, turns - 1) as i:
                for k in range(4):
                    step(i * 4 + k, k)
            for t in range(TILES - 4, TILES + 2):
                step(t, t % 4)

        def static(t):
            return isinstance(t, int)

        def e_pe(pe):
            e_route_pe(pe)

            def turn(t, r, turns):
                wait(pe, s_e_xg[r], turns * 16 + 16)
                if not (static(t) and t < 2):
                    wait(pe, s_e_xgT, t - 1)
                for h in range(HD):
                    last = nc.tensor.transpose(bank[t_bank(r)][:, h * P:(h + 1) * P], e_xg[:, r, h * P:(h + 1) * P], ident[:, :])
                last.then_inc(s_e_T[0], 1)

            def t_bank(r):
                return r % 2

            def experts(t):
                e = pe.value_load(e_tab[0:1, 0, ds(t, 1)], min_val=0, max_val=E3 - 1)
                c = pe.value_load(e_tab[0:1, 1, ds(t, 1)], min_val=0, max_val=E3S - 1)
                return e, c

            def gate_up(t, r):
                e, c = experts(t)
                wait(pe, s_e_xgT, t + 1)
                if not (static(t) and t < 2):
                    wait(pe, s_e_mul, t - 1)
                to = bank[2 + r % 2][:, :].rearrange("p (w n) -> p w n", w=2)
                for src, which, dst in ((e_w, e, to[:, :, 0:F3]), (e_cw, c, to[:, :, P:2 * P])):
                    for h in range(HD):
                        last = nc.tensor.matmul(dst, e_xgT[:, r, h * P:(h + 1) * P],
                                                src[:, ds(which, 1), h, :].rearrange("p a (w n) -> p (a w) n", w=2),
                                                start=(h == 0), stop=(h == HD - 1))
                last.then_inc(s_e_gu[0], 1)

            def h_turn(t, r):
                wait(pe, s_e_mul, t + 1)
                if not (static(t) and t < 2):
                    wait(pe, s_e_hTc, t - 1)
                for w in range(2):
                    last = nc.tensor.transpose(bank[4 + r % 2][:, w * P:(w + 1) * P], e_h[:, r % 2, w * P:(w + 1) * P], ident[:, :])
                last.then_inc(s_e_Ht[0], 1)

            def down(t, r):
                e, c = experts(t)
                wait(pe, s_e_hTc, t + 1)
                if not (static(t) and t < 2):
                    wait(pe, s_e_ye, t - 1)
                nc.tensor.matmul(bank[6 + r % 2][:, 0:D], e_hT[0:F3, r % 2, 0:P],
                                 e_wd[0:F3, ds(e, 1), :].rearrange("p a n -> p (a n)"), start=True, stop=False)
                nc.tensor.matmul(bank[6 + r % 2][:, 0:D], e_hT[:, r % 2, P:2 * P],
                                 e_cwd[:, ds(c, 1), :].rearrange("p a n -> p (a n)"), start=False, stop=True
                                 ).then_inc(s_e_d[0], 1)

            wait(pe, s_e_ld, 16 * EL)
            pe.wait_ge(s_e_new, 2)
            pe.wait_ge(s_e_tab, 1)
            pe.wait_ge(s_e_pad, 1)
            turn(0, 0, 0)

            def step(t, k):
                if not (static(t) and t + 1 >= TILES):
                    turn(t + 1, (k + 1) % 4, (t + 1) // 4 if static(t) else turns_of(t, k))
                if not (static(t) and t >= TILES):
                    gate_up(t, k)
                if not (static(t) and not 0 <= t - 1 < TILES):
                    h_turn(t - 1, (k - 1) % 4)
                if not (static(t) and t < 2):
                    down(t - 2, (k - 2) % 4)

            turn_no = {}

            def turns_of(t, k):
                return turn_no["i"] + (1 if k == 3 else 0)

            for k in range(4):
                step(k, k)
            with pe.Fori(1, TILES // 4 - 1) as i:
                turn_no["i"] = i
                for k in range(4):
                    step(i * 4 + k, k)
            for t in range(TILES - 4, TILES + 2):
                step(t, t % 4)

        def e_act(act):
            norm_act(act, 5)
            act.wait_ge(s_e_new, 1)
            nc.scalar.activation(e_p[:, :, :], e_p[:, :, :], ACT.Exp)
            nc.scalar.activation(e_sig[:, :, :], bank[2][:, 0:NT * E3].rearrange("p (i e) -> p i e", i=NT), ACT.Exp,
                                 scale=-1.0).then_inc(s_e_exp[0], 1)
            wait(act, s_e_ld, 16 * EL)
            flat = e_cwd.rearrange("p c n -> p (c n)")
            nc.scalar.mul(flat, flat, SMALL).then_inc(s_e_new, 1)

            def xgT_copy(t, r):
                wait(act, s_e_T, t + 1)
                if not (static(t) and t < 4):
                    wait(act, s_e_gu, t - 3)
                nc.scalar.copy(e_xgT[:, r, :], bank[r % 2][:, 0:2 * P]).then_inc(s_e_xgT[0], 1)

            def silu(t, r):
                wait(act, s_e_gu, t + 1)
                if not (static(t) and t < 2):
                    wait(act, s_e_mul, t - 1)
                nc.scalar.activation(e_sg[:, r % 2, :], bank[2 + r % 2][:, 0:2 * P], ACT.Silu).then_inc(s_e_sg[0], 1)

            def hT_copy(t, r):
                wait(act, s_e_Ht, t + 1)
                if not (static(t) and t < 2):
                    wait(act, s_e_d, t - 1)
                nc.scalar.copy(e_hT[:, r % 2, :], bank[4 + r % 2][:, 0:2 * P]).then_inc(s_e_hTc[0], 1)

            xgT_copy(0, 0)

            def step(t, k):
                if not (static(t) and t + 1 >= TILES):
                    xgT_copy(t + 1, (k + 1) % 4)
                if not (static(t) and t >= TILES):
                    silu(t, k)
                if not (static(t) and not 0 <= t - 1 < TILES):
                    hT_copy(t - 1, (k - 1) % 4)

            e_steps(act, step)

        def e_dve(dve):
            V = nc.vector
            dve.wait_ge(s_z_x, 2 * B)
            norm_dve(dve, 7)
            wait(dve, s_e_logit, 1)
            logits = bank[2][:, 0:NT * E3].rearrange("p (i e) -> p i e", i=NT)
            dve_link(V.tensor_reduce(e_top[:, :], logits, AX_X, ALU.max))
            V.tensor_tensor(e_p[:, :, :], logits, e_top[:, :].unsqueeze(2).to_broadcast([P, NT, E3]),
                            ALU.subtract).then_inc(s_e_new, 1)
            wait(dve, s_e_exp, 1)
            dve_link(V.tensor_scalar(e_sig[:, :, :], e_sig[:, :, :], 1.0, None, ALU.add))
            dve_link(V.reciprocal(e_sig[:, :, :], e_sig[:, :, :]))
            for i in range(NT):
                last = V.max(g_best[:, i, :], e_sig[:, i, :])
            dve_link(last)
            for i in range(NT):
                last = V.max_index(g_idx[:, i, :], g_best[:, i, :], e_sig[:, i, :])
            dve_link(last)
            dve_link(V.tensor_copy(g_idxf[:, :, :], g_idx[:, :, :]))
            for i in range(NT):
                last = V.tensor_tensor(e_eq[:, i, :, :], iota_e[:, 0:E3].unsqueeze(1).to_broadcast([P, K3, E3]),
                                       g_idxf[:, i, 0:K3].unsqueeze(2).to_broadcast([P, K3, E3]), ALU.is_equal)
            dve_link(last)
            dve_link(V.tensor_reduce(e_pos[:, :, :], e_eq.rearrange("p i k e -> p i e k"), AX_X, ALU.add))
            V.tensor_copy(e_mask, e_pos[:, :, :]).then_inc(s_e_mask[0], 1)
            dve_link(V.tensor_reduce(e_sum[:, :], e_p[:, :, :], AX_X, ALU.add))
            dve_link(V.reciprocal(e_sum[:, :], e_sum[:, :]))
            dve_link(V.tensor_tensor(e_p[:, :, :], e_p[:, :, :], e_sum[:, :].unsqueeze(2).to_broadcast([P, NT, E3]), ALU.mult))
            for i in range(NT):
                last = V.tensor_tensor(e_eq2[:, i, :, :], e_eq[:, i, :, :], e_p[:, i, :].unsqueeze(1).to_broadcast([P, K3, E3]),
                                       ALU.mult)
            dve_link(last)
            dve_link(V.tensor_reduce(e_wk[:, :, :], e_eq2, AX_X, ALU.add))
            dve_link(V.tensor_reduce(e_wsum[:, :], e_wk[:, :, :], AX_X, ALU.add))
            dve_link(V.reciprocal(e_wsum[:, :], e_wsum[:, :]))
            dve_link(V.tensor_tensor(e_wk[:, :, :], e_wk[:, :, :], e_wsum[:, :].unsqueeze(2).to_broadcast([P, NT, K3]), ALU.mult))
            dve_link(V.tensor_scalar(e_wk[:, :, :], e_wk[:, :, :], tanh_g[:, 1, 3:4], None, ALU.mult))
            wait(dve, s_e_rank, 1)
            dve_link(V.tensor_scalar(e_tot[:, :], bank[4][:, 0:E3], 1.0 / P, None, ALU.mult))
            dve_link(V.tensor_tensor(e_ge[:, :, :], e_tot[:, :].unsqueeze(2).to_broadcast([P, E3, NT]),
                                     iota_e[:, 0:NT].unsqueeze(1).to_broadcast([P, E3, NT]), ALU.is_gt))
            V.memset(e_base[:, :], 1.0)
            dve_link(V.tensor_reduce(e_tiles[:, :], e_ge[:, :, :], AX_X, ALU.add))
            dve_link(V.tensor_tensor_scan(e_cum[:, :], e_base[:, :], e_tiles[:, :], 0.0, ALU.mult, ALU.add))
            dve_link(V.tensor_tensor(e_base[:, :], e_cum[:, :], e_tiles[:, :], ALU.subtract))
            dve_link(V.tensor_scalar(e_base[:, :], e_base[:, :], float(P), None, ALU.mult))
            dve_link(V.tensor_tensor(e_pos[:, :, :], bank[3][:, 0:NT * E3].rearrange("p (i e) -> p i e", i=NT),
                                     e_base[:, :].unsqueeze(1).to_broadcast([P, NT, E3]), ALU.add))
            for i in range(NT):
                last = V.tensor_tensor(e_eq2[:, i, :, :], e_eq[:, i, :, :], e_pos[:, i, :].unsqueeze(1).to_broadcast([P, K3, E3]),
                                       ALU.mult)
            dve_link(last)
            dve_link(V.tensor_reduce(e_locf[:, :, :], e_eq2, AX_X, ALU.add))
            dve_link(V.tensor_copy(e_loc[:, :, :], e_locf[:, :, :]))
            dve_link(V.tensor_scalar(e_low[:, :, :], e_loc[:, :, :], P - 1, TILES.bit_length() - 1, ALU.bitwise_and,
                                     ALU.logical_shift_left))
            dve_link(V.tensor_scalar(e_loc[:, :, :], e_loc[:, :, :], P.bit_length() - 1, None, ALU.logical_shift_right))
            V.tensor_tensor(e_loc[:, :, :], e_loc[:, :, :], e_low[:, :, :], ALU.bitwise_or).then_inc(s_e_idx[0], 1)
            row = e_cmp[0:1]
            dve_link(V.tensor_tensor(row, iota_e[0:1, 0:TILES].unsqueeze(2).to_broadcast([1, TILES, E3]),
                                     e_cum[0:1, :].unsqueeze(1).to_broadcast([1, TILES, E3]), ALU.is_ge))
            V.tensor_reduce(e_tabf[0:1, 0, :], row, AX_X, ALU.add)
            dve_link(V.tensor_reduce(e_tabf[0:1, 1, :], row[:, :, 1:E3:GROUP3], AX_X, ALU.add))
            V.tensor_scalar(e_tabf[0:1, 0, :], e_tabf[0:1, 0, :], float(E3 - 1), None, ALU.min)
            dve_link(V.tensor_scalar(e_tabf[0:1, 1, :], e_tabf[0:1, 1, :], float(E3S - 1), None, ALU.min))
            V.tensor_copy(e_tab[0:1, :, :], e_tabf[0:1, :, :]).then_inc(s_e_tab, 1)
            for b in (2, 3):
                last = V.memset(bank[b][:, :].rearrange("p (w n) -> p w n", w=2)[:, :, F3:P], 0.0)
            last.then_inc(s_e_pad, 1)

            def mult(t, r):
                wait(dve, s_e_sg, t + 1)
                if not (static(t) and t < 2):
                    wait(dve, s_e_Ht, t - 1)
                V.tensor_tensor(e_h[:, r % 2, :], e_sg[:, r % 2, :], bank[2 + r % 2][:, 2 * P:4 * P], ALU.mult).then_inc(s_e_mul[0], 1)

            def evict(t, r, turns):
                wait(dve, s_e_d, t + 1)
                if not (static(t) and t < 4):
                    wait(dve, s_e_st[r], turns * 16)
                V.tensor_copy(e_ye[:, r, :], bank[6 + r % 2][:, 0:D]).then_inc(s_e_ye[0], 1)

            def step(t, k, turns):
                if not (static(t) and t >= TILES):
                    mult(t, k)
                if not (static(t) and t < 2):
                    evict(t - 2, (k - 2) % 4, turns - 1 if k < 2 else turns)

            for k in range(4):
                step(k, k, 0)
            with dve.Fori(1, TILES // 4 - 1) as i:
                for k in range(4):
                    step(i * 4 + k, k, i)
            for t in range(TILES - 4, TILES + 2):
                step(t, t % 4, t // 4)
            for m in range(NT * K3):
                i, k = m // K3, m % K3
                if k == 0:
                    wait(dve, s_e_back[i], 16 * K3)
                if m:
                    wait(dve, s_e_x, m)
                V.scalar_tensor_tensor(out=x[:, i, :], in0=e_back[:, m, :], scalar=e_wk[:, i, k:k + 1],
                                       in1=x[:, i, :], op0=ALU.mult, op1=ALU.add).then_inc(s_e_x[0], 1)

        s_out = sem("s_out")

        def store_sp(sp):
            wait(sp, s_e_x, NT * K3)
            sp.dma_start(out.rearrange("b (h p) d -> p (b h) d", p=P), x[:, :, :]).then_inc(s_out, 16)
            sp.wait_ge(s_out, 16)

        dve_link, pool_link, act_link = Link(nc.vector, s_dve), Link(nc.gpsimd, s_pool), Link(nc.scalar, s_act)
        block = ctx.enter_context(nc.Block())

        @block.sync
        def _(sp):
            prep_sp(sp)
            f0_sp(sp)
            l1_loads_sp(sp)
            ssm_bc_sp(sp, 1)
            for g in range(GB):
                ssm_load_sp(sp, 1, 0, g)
            x_sp(sp)
            g_sp(sp)
            e_sp(sp)
            store_sp(sp)

        @block.gpsimd
        def _(pool):
            prep_pool(pool)
            f0_const_pool(pool)
            norm_pool(pool, 0)
            norm_pool(pool, 1)
            f0_pool(pool)
            norm_pool(pool, 2)
            norm_pool(pool, 3)
            l1_pool(pool)
            norm_pool(pool, 4)
            x_pool(pool)
            norm_pool(pool, 5)
            norm_pool(pool, 6)
            e_pool(pool)

        @block.scalar
        def _(act):
            prep_act(act)
            ssm_A_act(act)
            ssm_in_act(act, 0)
            l0x_act(act)
            f0_act_eng(act)
            ssm_in_act(act, 1)
            ssm_dt_act(act, 1)
            l1_prep_act(act)
            gated_act(act, 0, 2)
            l1_act(act)
            x_act(act)
            g_act(act)
            gated_act(act, 1, 6)
            e_act(act)

        @block.vector
        def _(dve):
            ssm_in_dve(dve, 0)
            l0x_dve(dve)
            f0_dve(dve)
            dve.wait_ge(s_f0_x, NT * K0)
            gated_dve(dve, 0, 2)
            l1_dve(dve)
            x_dve(dve)
            g_dve(dve)
            wait(dve, s_g_x, 4)
            gated_dve(dve, 1, 6)
            e_dve(dve)

        @block.tensor
        def _(pe):
            prep_pe(pe)
            ssm_in_pe(pe, 0)
            l0x_pe(pe)
            f0_pe(pe)
            ssm_in_pe(pe, 1)
            ssm_dt_pe(pe, 1)
            l1_prep_pe(pe)
            gated_pe(pe, 0)
            l1_pe(pe)
            x_pe(pe)
            g_pe(pe)
            gated_pe(pe, 1)
            e_pe(pe)


_OUTS = [((B, S, D), 'float32')]


def kernel(**inputs):
    import numpy as _np
    import concourse.bacc as _bacc
    from concourse import mybir as _mybir
    from concourse.bass_utils import run_bass_kernel_spmd as _run

    nc = _bacc.Bacc("TRN2", target_bir_lowering=False, num_devices=1)
    arrays, args = {}, {}
    for name in inputs:
        a = _np.ascontiguousarray(inputs[name])
        arrays[f"in_{name}_dram"] = a
        args[name] = nc.dram_tensor(f"in_{name}_dram", a.shape, _mybir.dt.from_np(a.dtype), kind="ExternalInput").ap()
    outs = []
    for i, (shape, dtype) in enumerate(_OUTS):
        dt = _mybir.dt.from_np(_np.dtype(dtype))
        outs.append(nc.dram_tensor(f"out_{i}_dram", shape, dt, kind="ExternalOutput").ap())
    flamingo_kernel(nc, args, outs[0])
    r = _run(nc, [arrays], core_ids=[0])
    return r.results[0]["out_0_dram"]
```

```python
from contextlib import ExitStack

import concourse.bass as bass
from concourse import mybir

F32 = mybir.dt.float32
BF16 = mybir.dt.bfloat16
I32 = mybir.dt.int32
U32 = mybir.dt.uint32
ALU = mybir.AluOpType
ACT = mybir.ActivationFunctionType
AX_X = mybir.AxisListType.X
ds = bass.ds

P = 128
B, S, D = 4, 256, 256
C = 128
T = B * S
NT = T // P
HD = D // P
TPB = S // P
HALF = 512
EPS = 1e-5
LAYERS = 4
F0_W_AT = 1536
SSM_AT = 16800
ARENA = 32768


class Link:

    def __init__(self, eng, sem):
        self.eng, self.sem, self.base, self.i, self.per, self.n = eng, sem, 0, None, 0, 0

    def enter(self, i, per):
        self.i, self.per, self.n = i, per, 0

    def leave(self, turns):
        assert self.n == self.per, (self.n, self.per)
        self.base += turns * self.per
        self.i = None

    def __call__(self, ins):
        ins.then_inc(self.sem, 1)
        if self.i is None:
            self.base += 1
            self.eng.wait_ge(self.sem, self.base)
        else:
            self.n += 1
            self.eng.wait_ge(self.sem, self.i * self.per + (self.base + self.n))


def flamingo_kernel(nc, A, out):
    with ExitStack() as ctx:
        def sb(name, shape, dt=F32):
            return ctx.enter_context(nc.sbuf_tensor(name, shape, dt))

        def sem(name):
            return ctx.enter_context(nc.semaphore(name))

        ctx.enter_context(nc.allow_non_contiguous_dma(reason="small parameters, loaded once"))
        bank = [ctx.enter_context(nc.psum_tensor(f"bank{i}", [P, HALF], F32)) for i in range(8)]

        x = sb("x", [P, NT, D])
        y = sb("y", [P, NT, D])
        yT = sb("yT", [P, HD, T])
        ctxT = sb("ctxT", [P, T])
        ident = sb("ident", [P, P])
        stats = sb("stats", [P, NT, 6])
        moments = sb("moments", [P, NT, 2])
        var_eps = sb("var_eps", [P, NT])
        rstd = sb("rstd", [P, NT])
        minus_half = sb("minus_half", [P, NT])
        gates = sb("gates", [P, 2, LAYERS])
        tanh_g = sb("tanh_g", [P, 2, LAYERS])
        arena = sb("arena", [P, ARENA])

        def area(at, *shape):
            n = 1
            for k in shape:
                n *= k
            assert at + n <= ARENA, (at, n)
            v = arena[:, at:at + n]
            if len(shape) == 2:
                v = v.rearrange("p (a b) -> p a b", a=shape[0])
            elif len(shape) == 3:
                v = v.rearrange("p (a b c) -> p a b c", a=shape[0], b=shape[1])
            return v

        s_dve = sem("s_dve")
        s_act = sem("s_act")
        s_pool = sem("s_pool")

        ctx_rows = y[:, :, 0:C]
        wqk_rows = sb("wqk_rows", [P, 2, C])
        gw_rows = sb("gw_rows", [64, D])
        wqkT = sb("wqkT", [P, 2, P])
        gwT = sb("gwT", [P, HD, 64])
        bqk = sb("bqk", [P, 2])
        s_ld_ctx = sem("s_ld_ctx")
        s_ld_w0 = sem("s_ld_w0")
        s_ld_x = sem("s_ld_x")
        s_ld_g = sem("s_ld_g")
        s_const = sem("s_const")
        s_prep_t = sem("s_prep_t")
        s_prep = sem("s_prep")
        s_gate = sem("s_gate")

        N_W0 = 5
        prep_groups = [
            ([ctx_rows[:, i, :] for i in range(4)], ctxT[:, 0:512]),
            ([ctx_rows[:, i, :] for i in range(4, 8)], ctxT[:, 512:1024]),
            ([wqk_rows[:, i, :] for i in range(2)], wqkT[:, :, :].rearrange("p a b -> p (a b)")),
            ([gw_rows[:, h * P:(h + 1) * P] for h in range(HD)], gwT[:, :, :].rearrange("p a b -> p (a b)")),
        ]

        def prep_sp(sp):
            sp.dma_start(ctx_rows, A["ctx_1024"].rearrange("b (h p) c -> p (b h) c", p=P)).then_inc(s_ld_ctx, 16)
            sp.dma_start(wqk_rows[:, 0, :], A["L0_xattn_Wq"]).then_inc(s_ld_w0, 16)
            sp.dma_start(wqk_rows[:, 1, :], A["L0_xattn_Wk"]).then_inc(s_ld_w0, 16)
            sp.dma_start(gw_rows[:, :], A["L0_ffn_gate_w"]).then_inc(s_ld_w0, 16)
            sp.dma_start(bqk[:, 0:1], A["L0_xattn_bq"].rearrange("(p a) -> p a", a=1)).then_inc(s_ld_w0, 16)
            sp.dma_start(bqk[:, 1:2], A["L0_xattn_bk"].rearrange("(p a) -> p a", a=1)).then_inc(s_ld_w0, 16)
            sp.dma_start(x[:, :, :], A["x"].rearrange("b (h p) d -> p (b h) d", p=P)).then_inc(s_ld_x, 16)
            sp.dma_start(gates[:, 0, :], A["g_xattn"].rearrange("(a n) -> a n", a=1).to_broadcast([P, LAYERS])).then_inc(s_ld_g, 16)
            sp.dma_start(gates[:, 1, :], A["g_ffn"].rearrange("(a n) -> a n", a=1).to_broadcast([P, LAYERS])).then_inc(s_ld_g, 16)
            ssm_loads_sp(sp)

        def prep_pool(pool):
            link = pool_link
            link(nc.gpsimd.memset(ident[:, :], 0.0))
            nc.gpsimd.affine_select(out=ident[:, :], in_=ident[:, :], compare_op=ALU.not_equal, fill=1.0, base=0,
                                    pattern=[[-1, P]], channel_multiplier=1).then_inc(s_const, 1)
            nc.gpsimd.memset(minus_half[:, :], -0.5).then_inc(s_const, 1)

        def prep_pe(pe, first, last_group):
            if first == 0:
                pe.wait_ge(s_const, 2)
            for n in range(first, last_group):
                blocks, dst = prep_groups[n]
                if n == 0:
                    pe.wait_ge(s_ld_ctx, 16)
                if n == 2:
                    pe.wait_ge(s_ld_w0, 16 * N_W0)
                if n == 4:
                    pe.wait_ge(s_ld_ssm, 16 * 16)
                    pe.wait_ge(s_yT, NT // 2)
                if n >= 2:
                    pe.wait_ge(s_prep, n - 1)
                at = 0
                for src in blocks:
                    rows = src.shape[0]
                    last = nc.tensor.transpose(bank[n % 2][0:src.shape[1], at:at + rows], src, ident[0:rows, 0:rows])
                    at += rows
                last.then_inc(s_prep_t, 1)

        def prep_act(act, first, last_group):
            for n in range(first, last_group):
                blocks, dst = prep_groups[n]
                act.wait_ge(s_prep_t, n + 1)
                nc.scalar.copy(dst, bank[n % 2][0:dst.shape[0], 0:dst.shape[1]]).then_inc(s_prep, 1)

        def gate_act(act):
            act.wait_ge(s_ld_g, 32)
            nc.scalar.activation(tanh_g[:, :, :], gates[:, :, :], ACT.Tanh).then_inc(s_gate, 1)

        s_var = sem("s_var")
        s_rstd = sem("s_rstd")
        s_y = sem("s_y")
        s_yT_t = sem("s_yT_t")
        s_yT = sem("s_yT")
        norms = {"n": 0, "t": 0}

        def norm_stats(dve, tiles, updated, count):
            dve.wait_ge(updated, count)
            for i in tiles:
                last = nc.vector.bn_stats(stats[:, i, :], x[:, i, :])
            dve_link(last)

        def norm_dve(dve, k):
            for i in range(NT):
                last = nc.vector.bn_aggr(moments[:, i, :], stats[:, i, :])
            dve_link(last)
            nc.vector.tensor_scalar(var_eps[:, :], moments[:, :, 1], EPS, None, ALU.add).then_inc(s_var, 1)
            dve.wait_ge(s_rstd, k + 1)
            for i in range(NT):
                nc.vector.tensor_scalar(y[:, i, :], x[:, i, :], moments[:, i, 0:1], rstd[:, i:i + 1],
                                        ALU.subtract, ALU.mult).then_inc(s_y, 1)

        def norm_pool(pool, k):
            pool.wait_ge(s_var, k + 1)
            nc.gpsimd.tensor_tensor(rstd[:, :], var_eps[:, :], minus_half[:, :], ALU.pow).then_inc(s_rstd, 1)

        def norm_pe(pe, k, t):
            for j in range(NT // 2):
                pe.wait_ge(s_y, NT * k + 2 * j + 2)
                m = t * NT // 2 + j
                if m >= 2:
                    pe.wait_ge(s_yT, m - 1)
                for h in range(HD):
                    for i in range(2):
                        last = nc.tensor.transpose(bank[m % 2][:, (2 * h + i) * P:(2 * h + i + 1) * P],
                                                   y[:, 2 * j + i, h * P:(h + 1) * P], ident[:, :])
                last.then_inc(s_yT_t, 1)

        def norm_act(act, t):
            for j in range(NT // 2):
                m = t * NT // 2 + j
                act.wait_ge(s_yT_t, m + 1)
                nc.scalar.copy(yT[:, :, 2 * j * P:(2 * j + 2) * P],
                               bank[m % 2][:, :].rearrange("p (h n) -> p h n", h=HD)).then_inc(s_yT, 1)

        SSM = ("L1_xattn_", "L3_xattn_")
        DI, DS, DR, DC = 256, 16, 8, 4
        HC = DI // P
        NB = 4
        GB = DS // NB
        GROUPS = B * GB * HC
        PAD = 4 + S
        bc_rows = nc.dram_tensor("bc_rows", [2, B, 2 * DS, S], F32, kind="Internal").ap()
        ssm_y = sb("ssm_y", [P, 2, B, HC, S])
        at = SSM_AT
        ssm_delta = area(at, HC, T); at += HC * T
        ssm_du = area(at, HC, T); at += HC * T
        ssm_tmp = at
        ssm_B = area(at, 2, NB * S); at += 2 * NB * S
        ssm_C = area(at, 2, NB * S); at += 2 * NB * S
        ssm_decay = area(at, 2, NB * S); at += 2 * NB * S
        ssm_h = area(at, 2, NB * S); at += 2 * NB * S
        ssm_hC_buf = area(at, 2, NB * S); at += 2 * NB * S
        ssm_in = area(at, NB * S); at += NB * S
        SSM_END = at
        at = ssm_tmp
        ssm_pad = area(at, HC * B, PAD); at += HC * B * PAD
        ssm_v = area(at, HC, T); at += HC * T
        ssm_u = area(at, HC, T); at += HC * T
        ssm_lin = area(at, HC, T); at += HC * T
        ssm_e = area(at, HC, T); at += HC * T
        assert at <= SSM_END
        ssm_w = ssm_v
        ssm_s = ssm_du
        win_rows = sb("win_rows", [P, 2, HC, C])
        xp_rows = sb("xp_rows", [DR + 2 * DS, 2, DI])
        dt_rows = sb("dt_rows", [P, 2, HC, DR])
        winT = sb("winT", [P, 2 * HC, P])
        xpT = sb("xpT", [P, 2 * HC, DR + 2 * DS])
        dtT = sb("dtT", [DR, 2 * HC, P])
        conv_w = sb("conv_w", [P, 2, HC, DC])
        ssm_par = sb("ssm_par", [P, 3, 2, HC])
        ssm_A = sb("ssm_A", [P, 2, HC, DS])
        x_dbl = sb("x_dbl", [DR + 2 * DS, T])
        s_ld_ssm = sem("s_ld_ssm")
        s_sp_xin = sem("s_sp_xin")
        s_sp_pad = sem("s_sp_pad")
        s_sp_v = sem("s_sp_v")
        s_sp_u = sem("s_sp_u")
        s_sp_dblp = sem("s_sp_dblp")
        s_sp_dbl = sem("s_sp_dbl")
        s_sp_bc = sem("s_sp_bc")
        s_sp_dtp = sem("s_sp_dtp")
        s_sp_e = sem("s_sp_e")
        s_sp_done = sem("s_sp_done")
        s_A = sem("s_A")
        s_ssm_B = [sem(f"s_ssm_B{r}") for r in range(2)]
        s_ssm_C = [sem(f"s_ssm_C{r}") for r in range(2)]
        s_ssm_decay = sem("s_ssm_decay")
        s_ssm_in = sem("s_ssm_in")
        s_ssm_go = sem("s_ssm_go")
        s_ssm_h = sem("s_ssm_h")
        s_ssm_hC = sem("s_ssm_hC")
        s_ssm_sum = sem("s_ssm_sum")
        s_ssm_y = sem("s_ssm_y")
        s_ssm_red = sem("s_ssm_red")
        s_ssm_red_y = sem("s_ssm_red_y")
        ssm_part = sb("ssm_part", [P, S])

        prep_groups += [
            ([win_rows[:, m, c, :] for m in range(2) for c in range(HC)], winT[:, :, :].rearrange("p a b -> p (a b)")),
            ([xp_rows[:, m, c * P:(c + 1) * P] for m in range(2) for c in range(HC)],
             xpT[:, :, :].rearrange("p a b -> p (a b)")),
            ([dt_rows[:, m, c, :] for m in range(2) for c in range(HC)], dtT[:, :, :].rearrange("p a b -> p (a b)")),
        ]

        def ssm_loads_sp(sp):
            for m, name in enumerate(SSM):
                loads = [
                    (win_rows[:, m, :, :], A[name + "in_proj_w"].rearrange("(c p) k -> p c k", p=P)),
                    (xp_rows[:, m, :], A[name + "x_proj_w"]),
                    (dt_rows[:, m, :, :], A[name + "dt_proj_w"].rearrange("(c p) r -> p c r", p=P)),
                    (conv_w[:, m, :, :], A[name + "conv_w"].rearrange("(c p) k -> p c k" if m == 0 else "(c p) a k -> p c (a k)", p=P)),
                    (ssm_par[:, 0, m, :], A[name + "conv_b"].rearrange("(c p) -> p c", p=P)),
                    (ssm_par[:, 1, m, :], A[name + "dt_proj_b"].rearrange("(c p) -> p c", p=P)),
                    (ssm_par[:, 2, m, :], A[name + "D"].rearrange("(c p) -> p c", p=P)),
                    (ssm_A[:, m, :, :], A[name + "A_log"].rearrange("(c p) n -> p c n", p=P)),
                ]
                for dst, src in loads:
                    sp.dma_start(dst, src).then_inc(s_ld_ssm, 16)

        def ssm_A_act(act):
            act.wait_ge(s_ld_ssm, 16 * 16)
            flat = ssm_A[:, :, :, :].rearrange("p m c n -> p (m c n)")
            act_link(nc.scalar.activation(flat, flat, ACT.Exp))
            nc.scalar.mul(flat, flat, -1.0).then_inc(s_A, 1)

        def ssm_bank(i):
            return bank[4 + i]

        def ssm_in_pe(pe, m):
            if m:
                pe.wait_ge(s_ssm_y, B * HC)
                pe.wait_ge(s_f0_ye, PAIRS)
            pe.wait_ge(s_prep, len(prep_groups))
            pe.wait_ge(s_l0_qk, 4)
            for c in range(HC):
                for h in range(2):
                    nc.tensor.matmul(ssm_bank(2 * c + h)[:, :], winT[:, HC * m + c, :], ctxT[:, h * HALF:(h + 1) * HALF],
                                     start=True, stop=True).then_inc(s_sp_xin, 1)

        def ssm_in_act(act, m):
            if m:
                act.wait_ge(s_ssm_sum, GROUPS)
                act.wait_ge(s_ssm_y, B * HC)
            for c in range(HC):
                for h in range(2):
                    act.wait_ge(s_sp_xin, 4 * m + 2 * c + h + 1)
                    nc.scalar.copy(ssm_pad[:, 4 * c + 2 * h:4 * c + 2 * h + 2, DC - 1:DC - 1 + S],
                                   ssm_bank(2 * c + h)[:, :].rearrange("p (b l) -> p b l", b=2)).then_inc(s_sp_pad, 1)

        def ssm_u_act(act, m):
            for c in range(HC):
                act.wait_ge(s_sp_v, HC * m + c + 1)
                nc.scalar.activation(ssm_u[:, c, :], ssm_v[:, c, :], ACT.Silu).then_inc(s_sp_u, 1)

        def ssm_in_dve(dve, m):
            if m:
                dve.wait_ge(s_ssm_sum, GROUPS)
            else:
                dve.wait_ge(s_ld_ssm, 16 * 16)
            dve_link(nc.vector.memset(ssm_pad[:, :, 0:DC - 1], 0.0))

        def ssm_conv_dve(dve, m, c, taps):
            dve.wait_ge(s_sp_pad, 4 * m + 2 * c + 2)
            v = ssm_v[:, c, :].rearrange("p (b l) -> p b l", b=B)
            for k in taps:
                tap = ssm_pad[:, B * c:B * (c + 1), k:k + S]
                if k == 0:
                    dve_link(nc.vector.tensor_scalar(v, tap, conv_w[:, m, c, 0:1], ssm_par[:, 0, m, c:c + 1],
                                                     ALU.mult, ALU.add))
                else:
                    last = nc.vector.scalar_tensor_tensor(out=v, in0=tap, scalar=conv_w[:, m, c, k:k + 1], in1=v,
                                                          op0=ALU.mult, op1=ALU.add)
                    if k < DC - 1:
                        dve_link(last)
                    else:
                        last.then_inc(s_sp_v, 1)

        def ssm_dt_pe(pe, m):
            pe.wait_ge(s_sp_u, HC * (m + 1))
            for h in range(2):
                for c in range(HC):
                    last = nc.tensor.matmul(ssm_bank(h)[0:DR + 2 * DS, :], xpT[:, HC * m + c, :],
                                            ssm_u[:, c, h * HALF:(h + 1) * HALF], start=(c == 0), stop=(c == HC - 1))
                last.then_inc(s_sp_dblp, 1)
            pe.wait_ge(s_sp_dbl, 2 * m + 2)
            for c in range(HC):
                for h in range(2):
                    nc.tensor.matmul(ssm_bank(2 * c + h)[:, :], dtT[:, HC * m + c, :],
                                     x_dbl[0:DR, h * HALF:(h + 1) * HALF], start=True, stop=True).then_inc(s_sp_dtp, 1)

        def ssm_dt_act(act, m):
            for h in range(2):
                act.wait_ge(s_sp_dblp, 2 * m + h + 1)
                if m:
                    act.wait_ge(s_sp_bc, 16)
                nc.scalar.copy(x_dbl[:, h * HALF:(h + 1) * HALF], ssm_bank(h)[0:DR + 2 * DS, :]).then_inc(s_sp_dbl, 1)
            for c in range(HC):
                nc.scalar.activation(ssm_y[:, m, :, c, :], ssm_u[:, c, :].rearrange("p (b l) -> p b l", b=B), ACT.Copy,
                                     scale=ssm_par[:, 2, m, c:c + 1])
                for h in range(2):
                    cols = slice(h * HALF, (h + 1) * HALF)
                    act.wait_ge(s_sp_dtp, 4 * m + 2 * c + h + 1)
                    bias = ssm_par[:, 1, m, c:c + 1]
                    nc.scalar.activation(ssm_lin[:, c, cols], ssm_bank(2 * c + h)[:, :], ACT.Relu, bias=bias)
                    act_link(nc.scalar.activation(ssm_e[:, c, cols], ssm_bank(2 * c + h)[:, :], ACT.Abs, bias=bias))
                    act_link(nc.scalar.activation(ssm_e[:, c, cols], ssm_e[:, c, cols], ACT.Exp, scale=-1.0))
                    nc.scalar.activation(ssm_delta[:, c, cols], ssm_e[:, c, cols], ACT.Copy, bias=2.0).then_inc(s_sp_e, 1)

        def ssm_bc_sp(sp, m):
            sp.wait_ge(s_sp_dbl, 2 * m + 2)
            sp.dma_start(bc_rows[m].rearrange("b n l -> n b l"),
                         x_dbl[DR:, :].rearrange("n (b l) -> n b l", b=B)).then_inc(s_sp_bc, 16)

        def ssm_dt_dve(dve, m, c):
            V = nc.vector
            e, s, w, t, lin, u = (z[:, c, :] for z in (ssm_e, ssm_s, ssm_w, ssm_delta, ssm_lin, ssm_u))
            dve.wait_ge(s_sp_e, 4 * m + 2 * c + 2)
            dve_link(V.reciprocal(t, t))
            dve_link(V.tensor_tensor(s, e, t, ALU.mult))
            dve_link(V.tensor_tensor(w, s, s, ALU.mult))
            c4, *rest = (0.14087329, 0.13980709, 0.20012427, 0.33333158)
            dve_link(V.tensor_scalar(t, w, c4, None, ALU.mult))
            for k in rest:
                dve_link(V.scalar_tensor_tensor(out=t, in0=t, scalar=k, in1=w, op0=ALU.add, op1=ALU.mult))
            dve_link(V.scalar_tensor_tensor(out=t, in0=t, scalar=1.0, in1=s, op0=ALU.add, op1=ALU.mult))
            dve_link(V.scalar_tensor_tensor(out=t, in0=t, scalar=2.0, in1=lin, op0=ALU.mult, op1=ALU.add))
            dve_link(V.tensor_tensor(s, t, u, ALU.mult))
            if c < HC - 1:
                return
            V.memset(ssm_decay.rearrange("p a (n l) -> p (a n) l", l=S)[:, :, 0:1], 0.0).then_inc(s_sp_done, 1)

        def ssm_load_sp(sp, m, b, g):
            n = m * B * GB + b * GB + g
            if not (isinstance(b, int) and m == 0 and b == 0 and g < 2):
                sp.wait_ge(s_ssm_in, HC * (n - 1))
                sp.wait_ge(s_ssm_hC, HC * (n - 1))
            if g == 0 and isinstance(b, int) and b == 0:
                sp.wait_ge(s_sp_bc, 16 * (m + 1))
                sp.wait_ge(s_sp_done, m + 1)
            for k, (dst, sems) in enumerate(((ssm_B, s_ssm_B), (ssm_C, s_ssm_C))):
                src = bc_rows[m][ds(b, 1), k * DS + g * NB:k * DS + (g + 1) * NB, :].rearrange("a n l -> a (n l)")
                sp.dma_start(dst[:, g % 2, :], src.to_broadcast([P, NB * S])).then_inc(sems[g % 2], 16)

        def ssm_act(act, m, b, j):
            g, c = j // HC, j % HC
            q = m * GROUPS + b * GB * HC + j
            if j == 0 and isinstance(b, int) and b == 0:
                act.wait_ge(s_A, 1)
                act.wait_ge(s_sp_done, m + 1)
            if not (isinstance(b, int) and m == 0 and b == 0 and j < 2):
                act.wait_ge(s_ssm_h, q - 1)
                act.sem_inc(s_ssm_go, 1)
            for n in range(NB):
                last = nc.scalar.activation(ssm_decay[:, j % 2, n * S + 1:(n + 1) * S], ssm_delta[:, c, ds(b * S + 1, S - 1)],
                                            ACT.Exp, scale=ssm_A[:, m, c, NB * g + n:NB * g + n + 1])
            last.then_inc(s_ssm_decay, 1)

        def ssm_in_product(dve, m, b, j):
            g, c = j // HC, j % HC
            q = m * GROUPS + b * GB * HC + j
            turns = (m * B + b) * (GB // 2) + g // 2
            dve.wait_ge(s_ssm_B[g % 2], turns * 16 + 16)
            if not (isinstance(b, int) and m == 0 and b == 0 and j < 1):
                dve.wait_ge(s_ssm_h, q)
            nc.vector.tensor_tensor(ssm_in.rearrange("p (n l) -> p n l", n=NB),
                                    ssm_B[:, g % 2, :].rearrange("p (n l) -> p n l", n=NB),
                                    ssm_du[:, c, ds(b * S, S)].unsqueeze(1).to_broadcast([P, NB, S]),
                                    ALU.mult).then_inc(s_ssm_in, 1)

        def ssm_scan(dve, m, b, j):
            q = m * GROUPS + b * GB * HC + j
            dve.wait_ge(s_ssm_in, q + 1)
            dve.wait_ge(s_ssm_decay, q + 1)
            if not (isinstance(b, int) and m == 0 and b == 0 and j < 2):
                dve.wait_ge(s_ssm_hC, q - 1)
            nc.vector.tensor_tensor_scan(ssm_h[:, j % 2, :], ssm_decay[:, j % 2, :], ssm_in, 0.0,
                                         ALU.mult, ALU.add).then_inc(s_ssm_h, 1)

        def ssm_dve(dve, m, b, j, pool=False):
            ssm_in_product(dve, m, b, j)
            ssm_scan(dve, m, b, j)
            if j == 1 and m == 0 and not (isinstance(b, int) and b == 0):
                ssm_sum_dve(dve, m, b - 1)
            if not pool:
                ssm_hC(dve, nc.vector, m, b, j)

        def ssm_hC(eng, ops, m, b, j):
            g = j // HC
            q = m * GROUPS + b * GB * HC + j
            turns = (m * B + b) * (GB // 2) + g // 2
            eng.wait_ge(s_ssm_h, q + 1)
            eng.wait_ge(s_ssm_C[g % 2], turns * 16 + 16)
            if not (isinstance(b, int) and b == 0 and j < 2):
                eng.wait_ge((s_ssm_sum, s_ssm_red)[m], b * GB * HC + (j - 1))
            ops.tensor_tensor(ssm_hC_buf[:, j % 2, :], ssm_h[:, j % 2, :], ssm_C[:, g % 2, :], ALU.mult).then_inc(s_ssm_hC, 1)

        def ssm_pe(pe, m, b, j):
            g, c = j // HC, j % HC
            q = m * GROUPS + b * GB * HC + j
            if g == 0 and not (isinstance(b, int) and m == 0 and b == 0):
                pe.wait_ge(s_ssm_y, HC * (m * B + b))
            pe.wait_ge(s_ssm_hC, q + 1)
            for n in range(NB):
                last = nc.tensor.matmul(bank[6 + c][:, 0:S], ident[:, :], ssm_hC_buf[:, j % 2, n * S:(n + 1) * S],
                                        start=(g == 0 and n == 0), stop=(g == GB - 1 and n == NB - 1))
            last.then_inc(s_ssm_sum, 1)

        def ssm_reduce_dve(dve, m, b, j):
            c = j % HC
            q = b * GB * HC + j
            dve.wait_ge(s_ssm_hC, m * GROUPS + q + 1)
            if not (isinstance(b, int) and b == 0 and j == 0):
                dve.wait_ge(s_ssm_red_y, q)
            nc.vector.tensor_reduce(ssm_part[:, :], ssm_hC_buf[:, j % 2, :].rearrange("p (n l) -> p l n", n=NB),
                                    AX_X, ALU.add).then_inc(s_ssm_red, 1)
            dve.wait_ge(s_ssm_red, q + 1)
            row = ssm_y[:, m, ds(b, 1), c, :].rearrange("p a l -> p (a l)")
            nc.vector.tensor_tensor(row, row, ssm_part[:, :], ALU.add).then_inc(s_ssm_red_y, 1)

        def ssm_sum_dve(dve, m, b):
            dve.wait_ge(s_ssm_sum, m * GROUPS + (b + 1) * GB * HC)
            for c in range(HC):
                row = ssm_y[:, m, ds(b, 1), c, :].rearrange("p a l -> p (a l)")
                nc.vector.tensor_tensor(row, row, bank[6 + c][:, 0:S], ALU.add).then_inc(s_ssm_y, 1)

        z_gate = y
        s_z_silu = sem("s_z_silu")
        s_z_prod = sem("s_z_prod")
        s_z_t = sem("s_z_t")
        s_z_x = sem("s_z_x")

        def gated_act(act, m, k):
            for b in range(B):
                act.wait_ge(s_y, NT * k + TPB * (b + 1))
                nc.scalar.activation(z_gate[:, TPB * b:TPB * (b + 1), :], y[:, TPB * b:TPB * (b + 1), :],
                                     ACT.Silu).then_inc(s_z_silu, 1)

        def gated_dve(dve, m, k):
            norm_dve(dve, k)
            if m:
                dve.wait_ge(s_ssm_red_y, GROUPS)
            else:
                dve.wait_ge(s_ssm_y, B * HC)
            for b in range(B + 1):
                if b < B:
                    dve.wait_ge(s_z_silu, m * B + b + 1)
                    rows = z_gate[:, TPB * b:TPB * (b + 1), :]
                    nc.vector.tensor_tensor(rows, rows, ssm_y[:, m, b, :, :], ALU.mult).then_inc(s_z_prod, 1)
                if b:
                    dve.wait_ge(s_z_t, m * B + b)
                    rows = x[:, TPB * (b - 1):TPB * b, :].rearrange("p a n -> p (a n)")
                    nc.vector.scalar_tensor_tensor(out=rows, in0=bank[b % 2][:, :], scalar=tanh_g[:, 0, 2 * m + 1:2 * m + 2],
                                                   in1=rows, op0=ALU.mult, op1=ALU.add).then_inc(s_z_x, 1)
                    norm_stats(dve, range(TPB * (b - 1), TPB * b), s_z_x, m * B + b)

        def gated_pe(pe, m):
            for b in range(B):
                pe.wait_ge(s_z_prod, m * B + b + 1)
                if b >= 2:
                    pe.wait_ge(s_z_x, m * B + b - 1)
                for j in range(TPB):
                    for c in range(HC):
                        last = nc.tensor.transpose(bank[(b + 1) % 2][:, j * S + c * P:j * S + (c + 1) * P],
                                                   z_gate[:, TPB * b + c, j * P:(j + 1) * P], ident[:, :])
                last.then_inc(s_z_t, 1)

        att_q = area(0, T)
        att_k = area(T, T)
        att_e = area(2 * T, 2, TPB, S)
        att_T = area(2 * T + 2 * TPB * S, 2, TPB, S)
        att_top = sb("att_top", [P, 2, TPB])
        att_sum = sb("att_sum", [P, 2, TPB])
        att_inv = sb("att_inv", [P, 2, TPB])
        s_l0_qkp = sem("s_l0_qkp")
        s_l0_qk = sem("s_l0_qk")
        s_l0_energy = sem("s_l0_energy")
        s_l0_top = sem("s_l0_top")
        s_l0_exp = sem("s_l0_exp")
        s_l0_att = sem("s_l0_att")
        s_l0_attTp = sem("s_l0_attTp")
        s_l0_attT = sem("s_l0_attT")
        s_l0_out = sem("s_l0_out")
        s_l0_x = sem("s_l0_x")

        def l0x_pe(pe):
            pe.wait_ge(s_prep, 4)
            for w in range(2):
                for h in range(2):
                    nc.tensor.matmul(bank[2 + 2 * w + h][:, :], wqkT[:, w, :], ctxT[:, h * HALF:(h + 1) * HALF],
                                     start=True, stop=True).then_inc(s_l0_qkp, 1)
            pe.wait_ge(s_l0_qk, 4)
            l0x_pe_energy(pe, 0)
            l0x_pe_energy(pe, 1)
            norm_pe(pe, 0, 0)
            prep_pe(pe, 4, len(prep_groups))
            ssm_in_pe(pe, 0)
            pe.wait_ge(s_sp_pad, 4)
            for b in range(B):
                if b >= 2:
                    l0x_pe_energy(pe, b)
                if b >= 1:
                    l0x_pe_out(pe, b - 1)
            l0x_pe_out(pe, B - 1)

        def l0x_pe_energy(pe, b):
            energy = bank[2 + b % 2]
            if b >= 2:
                pe.wait_ge(s_l0_exp, TPB * (b - 1))
            for i in range(TPB):
                last = nc.tensor.matmul(energy[:, i * S:(i + 1) * S],
                                        att_q[:, b * S + i * P:b * S + (i + 1) * P], att_k[:, b * S:(b + 1) * S],
                                        start=True, stop=True)
            last.then_inc(s_l0_energy, 1)

        def l0x_pe_out(pe, b):
            turned = bank[4 + b % 2]
            pe.wait_ge(s_l0_att, b + 1)
            if b >= 2:
                pe.wait_ge(s_l0_attT, b - 1)
            for j in range(TPB):
                for i in range(TPB):
                    last = nc.tensor.transpose(turned[:, j * S + i * P:j * S + (i + 1) * P],
                                               att_e[:, b % 2, i, j * P:(j + 1) * P], ident[:, :])
            last.then_inc(s_l0_attTp, 1)
            pe.wait_ge(s_l0_attT, b + 1)
            pe.wait_ge(s_yT, NT // 2)
            if b >= 2:
                pe.wait_ge(s_l0_x, b - 1)
            for i in range(TPB):
                for j in range(TPB):
                    last = nc.tensor.matmul(bank[b % 2][:, i * S:(i + 1) * S],
                                            yT[:, j, b * S + i * P:b * S + (i + 1) * P], att_T[:, b % 2, j, :],
                                            start=(j == 0), stop=(j == TPB - 1))
            last.then_inc(s_l0_out, 1)

        def l0x_act(act):
            for w in range(2):
                for h in range(2):
                    act.wait_ge(s_l0_qkp, 2 * w + h + 1)
                    dst = (att_q, att_k)[w][:, h * HALF:(h + 1) * HALF]
                    nc.scalar.activation(dst, bank[2 + 2 * w + h][:, :], ACT.Identity,
                                         bias=bqk[:, w:w + 1]).then_inc(s_l0_qk, 1)
            norm_act(act, 0)
            for b in range(B):
                act.wait_ge(s_l0_top, b + 1)
                if b >= 2:
                    act.wait_ge(s_l0_attTp, b - 1)
                for i in range(TPB):
                    nc.scalar.activation(att_e[:, b % 2, i, :], bank[2 + b % 2][:, i * S:(i + 1) * S], ACT.Exp,
                                         bias=att_top[:, b % 2, i:i + 1],
                                         accum_out=att_sum[:, b % 2, i:i + 1]).then_inc(s_l0_exp, 1)
                if b == 0:
                    prep_act(act, 4, len(prep_groups))
                    ssm_in_act(act, 0)
                if b >= 1:
                    l0x_act_turn(act, b - 1)
            l0x_act_turn(act, B - 1)
            ssm_u_act(act, 0)
            ssm_A_act(act)

        def l0x_act_turn(act, b):
            act.wait_ge(s_l0_attTp, b + 1)
            if b >= 2:
                act.wait_ge(s_l0_out, b - 1)
            nc.scalar.copy(att_T[:, b % 2, :, :].rearrange("p a b -> p (a b)"), bank[4 + b % 2][:, :]).then_inc(s_l0_attT, 1)

        def l0x_dve(dve):
            dve.wait_ge(s_ld_x, 16)
            dve.wait_ge(s_prep, 2)
            norm_stats(dve, range(NT), s_ld_x, 16)
            norm_dve(dve, 0)
            ssm_in_dve(dve, 0)
            for b in range(B):
                dve.wait_ge(s_l0_energy, b + 1)
                if b >= 2:
                    dve.wait_ge(s_l0_exp, TPB * (b - 1))
                nc.vector.tensor_reduce(att_top[:, b % 2, :], bank[2 + b % 2][:, :].rearrange("p (i n) -> p i n", i=TPB),
                                        AX_X, ALU.max, negate=True).then_inc(s_l0_top, 1)
                dve.wait_ge(s_l0_exp, TPB * (b + 1))
                dve_link(nc.vector.reciprocal(att_inv[:, b % 2, :], att_sum[:, b % 2, :]))
                for i in range(TPB):
                    last = nc.vector.tensor_scalar(att_e[:, b % 2, i, :], att_e[:, b % 2, i, :],
                                                   att_inv[:, b % 2, i:i + 1], None, ALU.mult)
                last.then_inc(s_l0_att, 1)
                ssm_conv_dve(dve, 0, b // 2, range(2 * (b % 2), 2 * (b % 2) + 2))
                if b >= 1:
                    l0x_dve_add(dve, b - 1)
            l0x_dve_add(dve, B - 1)

        def l0x_dve_add(dve, b):
            dve.wait_ge(s_l0_out, b + 1)
            if b == 0:
                dve.wait_ge(s_gate, 1)
            rows = x[:, TPB * b:TPB * (b + 1), :].rearrange("p a b -> p (a b)")
            nc.vector.scalar_tensor_tensor(out=rows, in0=bank[b % 2][:, :], scalar=tanh_g[:, 0, 0:1], in1=rows,
                                           op0=ALU.mult, op1=ALU.add).then_inc(s_l0_x, 1)
            norm_stats(dve, range(TPB * b, TPB * (b + 1)), s_l0_x, b + 1)

        E0, K0, CAP, F0 = 64, 8, 128, 128
        PAIRS = E0 // 2
        RING, TURN = 4, 8
        slot_token = nc.dram_tensor("slot_token", [CAP * E0, 1], I32, kind="Internal").ap()
        y_rows = nc.dram_tensor("y_rows", [T, D], F32, kind="Internal").ap()
        slot_out = nc.dram_tensor("slot_out", [CAP * E0, D], F32, kind="Internal").ap()
        at = 0
        f0_prob = area(at, NT, E0); at += NT * E0
        f0_left = area(at, NT, E0); at += NT * E0
        f0_eq = area(at, K0, E0); at += K0 * E0
        F0_W = at
        assert F0_W == F0_W_AT
        f0_wg = area(at, RING, 2, D); at += RING * 2 * D
        f0_wu = area(at, RING, 2, D); at += RING * 2 * D
        f0_wd = area(at, RING, 2, D); at += RING * 2 * D
        f0_xg = area(at, RING, 2, D); at += RING * 2 * D
        f0_xgT = area(at, RING, 2 * D); at += RING * 2 * D
        f0_sg = area(at, RING, 2 * P); at += RING * 2 * P
        f0_hT = area(at, RING, 2 * P); at += RING * 2 * P
        f0_act = area(at, 2 * P); at += 2 * P
        f0_ye = area(at, RING, 2 * D); at += RING * 2 * D
        F0_END = at
        GR = 3 * RING * 2
        f0_back = area(F0_W, GR, D)
        f0_mask = sb("f0_mask", [P, NT, E0], BF16)
        tri = sb("tri", [P, P], BF16)
        ones_b = sb("ones_b", [P, P], BF16)
        iota_e = sb("iota_e", [P, E0])
        token_id = sb("token_id", [P, NT], I32)
        zero_slots = sb("zero_slots", [P, E0], I32)
        slots = sb("slots", [P, E0], I32)
        f0_top = sb("f0_top", [P, NT])
        f0_sum = sb("f0_sum", [P, NT])
        f0_w = sb("f0_w", [P, NT, K0])
        f0_i = sb("f0_i", [P, NT, K0], U32)
        f0_if = sb("f0_if", [P, NT, K0])
        f0_pos = sb("f0_pos", [P, NT, K0])
        f0_ok = sb("f0_ok", [P, NT, K0])
        f0_loc = sb("f0_loc", [P, NT, K0])
        f0_put = sb("f0_put", [P, NT, K0], I32)
        f0_get = sb("f0_get", [P, NT, K0], I32)
        s_f0_const = sem("s_f0_const")
        s_f0_logit = sem("s_f0_logit")
        s_f0_top = sem("s_f0_top")
        s_f0_exp = sem("s_f0_exp")
        s_f0_mask = sem("s_f0_mask")
        s_f0_rank = sem("s_f0_rank")
        s_f0_idx = sem("s_f0_idx")
        s_f0_zero = sem("s_f0_zero")
        s_f0_yrows = sem("s_f0_yrows")
        s_f0_put = sem("s_f0_put")
        s_f0_slots = sem("s_f0_slots")
        s_f0_w = [sem(f"s_f0_w{r}") for r in range(RING)]
        s_f0_xg = [sem(f"s_f0_xg{r}") for r in range(RING)]
        s_f0_T = sem("s_f0_T")
        s_f0_xgT = sem("s_f0_xgT")
        s_f0_gu = sem("s_f0_gu")
        s_f0_sg = sem("s_f0_sg")
        s_f0_h = sem("s_f0_h")
        s_f0_act = sem("s_f0_act")
        s_f0_d = sem("s_f0_d")
        s_f0_ye = sem("s_f0_ye")
        s_f0_st = [sem(f"s_f0_st{r}") for r in range(RING)]
        GB_ROWS = 3
        s_f0_back = [sem(f"s_f0_back{r}") for r in range(GR // GB_ROWS)]
        s_f0_x = sem("s_f0_x")
        s_f0_diag = sem("s_f0_diag")
        s_f0_cmb = sem("s_f0_cmb")
        f0_diag = area(F0_W - 4 * P, 4, P)

        f0_order = [(2 * g + j, k) for g in range(NT // 2) for k in range(K0) for j in range(2)]

        def f0_const_pool(pool):
            pool_link(nc.gpsimd.memset(tri[:, :], 1.0))
            nc.gpsimd.affine_select(out=tri[:, :], in_=tri[:, :], compare_op=ALU.is_gt, fill=0.0, base=0,
                                    pattern=[[1, P]], channel_multiplier=-1)
            nc.gpsimd.memset(ones_b[:, :], 1.0)
            nc.gpsimd.memset(zero_slots[:, :], 0)
            nc.gpsimd.iota(iota_e[:, :], [[1, E0]], base=0, channel_multiplier=0, allow_small_or_imprecise_dtypes=True)
            nc.gpsimd.iota(token_id[:, :], [[P, NT]], base=0, channel_multiplier=1).then_inc(s_f0_const, 1)

        def f0_weights_sp(sp):
            def load(n, r):
                for m, (dst, name) in enumerate(((f0_wg, "L0_ffn_w_gate"), (f0_wu, "L0_ffn_w_up"), (f0_wd, "L0_ffn_w_down"))):
                    if m < 2:
                        src = A[name].rearrange("e (p h) f -> p e (h f)", h=HD)
                    else:
                        src = A[name].rearrange("e f d -> f e d")
                    sp.dma_start(dst[:, r, :, :], src[:, ds(2 * n, 2), :]).then_inc(s_f0_w[r], 16)
            return load

        def f0_sp(sp):
            load = f0_weights_sp(sp)
            sp.wait_ge(s_f0_const, 1)
            sp.dma_start(slot_token.rearrange("(p n) a -> p (n a)", p=P), zero_slots[:, :]).then_inc(s_f0_zero, 16)
            sp.wait_ge(s_l0_out, B)
            for n in range(RING):
                load(n, n)
            sp.wait_ge(s_y, 2 * NT)
            sp.dma_start(y_rows.rearrange("(i p) d -> p i d", p=P), y[:, :, :]).then_inc(s_f0_yrows, 16)
            ssm_bc_sp(sp, 0)
            for g in range(GB):
                ssm_load_sp(sp, 0, 0, g)

            def step(n, r):
                sp.wait_ge(s_f0_ye, n + 1)
                sp.dma_start(slot_out.rearrange("(c e) d -> c e d", e=E0)[:, ds(2 * n, 2), :],
                             f0_ye[:, r, :].rearrange("p (e d) -> p e d", e=2)).then_inc(s_f0_st[r], 16)

            def scan_load(b, j):
                n = (j - 1) // 2 + 2
                ssm_load_sp(sp, 0, b + n // GB, n % GB)

            for n in range(TURN):
                step(n, n % RING)
                load(n + RING, n % RING)
                if n >= TURN - 3 and n % 2:
                    scan_load(0, n)
            with sp.Fori(1, PAIRS // TURN - 1) as i:
                for j in range(TURN):
                    step(i * TURN + j, j % RING)
                    load(i * TURN + (j + RING), j % RING)
                    if j % 2:
                        scan_load(i, j)
            for n in range(PAIRS - TURN, PAIRS):
                step(n, n % RING)
                if n + RING < PAIRS:
                    load(n + RING, n % RING)
                if n in (PAIRS - TURN + 1, PAIRS - TURN + 3):
                    scan_load(B - 1, n % TURN)

        def f0_pool(pool):
            pool.wait_ge(s_f0_zero, 16)
            for i in range(NT):
                pool.wait_ge(s_f0_idx, i + 1)
                for k in range(K0):
                    nc.gpsimd.indirect_dma_start(
                        out=slot_token, out_offset=bass.IndirectOffsetOnAxis(ap=f0_put[:, i, k:k + 1], axis=0),
                        in_=token_id[:, i:i + 1], in_offset=None, bounds_check=CAP * E0 - 1,
                        oob_is_err=False).then_inc(s_f0_put, 16)
            pool.wait_ge(s_f0_put, 16 * NT * K0)
            pool.dma_start(slots[:, :], slot_token.rearrange("(c e) a -> c (e a)", e=E0)).then_inc(s_f0_slots, 16)
            pool.wait_ge(s_f0_slots, 16)
            pool.wait_ge(s_f0_yrows, 16)
            AHEAD = RING - 1
            for n in range(PAIRS):
                if n >= RING:
                    pool.wait_ge(s_f0_T, n - RING + 1)
                for e in range(2):
                    nc.gpsimd.indirect_dma_start(
                        out=f0_xg[:, n % RING, e, :], out_offset=None, in_=y_rows,
                        in_offset=bass.IndirectOffsetOnAxis(ap=slots[:, 2 * n + e:2 * n + e + 1], axis=0),
                        bounds_check=T - 1, oob_is_err=True).then_inc(s_f0_xg[n % RING], 16)
                if n - AHEAD >= TURN:
                    ssm_hC(pool, nc.gpsimd, 0, (n - AHEAD) // TURN, (n - AHEAD) % TURN)
            for n in range(PAIRS - AHEAD, PAIRS):
                ssm_hC(pool, nc.gpsimd, 0, n // TURN, n % TURN)
            for r in range(RING):
                pool.wait_ge(s_f0_st[r], 16 * ((PAIRS - r + RING - 1) // RING))
            for m, (i, k) in enumerate(f0_order):
                if m >= GR:
                    pool.wait_ge(s_f0_cmb, m - GR + 1)
                nc.gpsimd.indirect_dma_start(
                    out=f0_back[:, m % GR, :], out_offset=None, in_=slot_out,
                    in_offset=bass.IndirectOffsetOnAxis(ap=f0_get[:, i, k:k + 1], axis=0),
                    bounds_check=CAP * E0 - 1, oob_is_err=True).then_inc(s_f0_back[m % GR // GB_ROWS], 16)

        def f0_pe(pe):
            norm_pe(pe, 1, 1)
            pe.wait_ge(s_yT, NT)
            for i in range(NT):
                for h in range(HD):
                    last = nc.tensor.matmul(bank[2][:, i * E0:(i + 1) * E0], yT[:, h, i * P:(i + 1) * P], gwT[:, h, :],
                                            start=(h == 0), stop=(h == HD - 1))
            last.then_inc(s_f0_logit, 1)
            pe.wait_ge(s_f0_mask, 1)
            pe.wait_ge(s_f0_const, 1)
            for i in range(NT):
                for j in range(i + 1):
                    last = nc.tensor.matmul(bank[3][:, i * E0:(i + 1) * E0], tri[:, :] if j == i else ones_b[:, :],
                                            f0_mask[:, j, :], start=(j == 0), stop=(j == i))
            last.then_inc(s_f0_rank, 1)

            def turn(n, r, m, tn):
                pe.wait_ge(s_f0_xg[r], tn * 32 + 32)
                if not (isinstance(n, int) and n < 2):
                    pe.wait_ge(s_f0_xgT, n - 1)
                for e in range(2):
                    for h in range(HD):
                        last = nc.tensor.transpose(bank[m][:, (2 * e + h) * P:(2 * e + h + 1) * P],
                                                   f0_xg[:, r, e, h:D:HD], ident[:, :])
                last.then_inc(s_f0_T, 1)

            def gate_up(n, r, m, tn):
                pe.wait_ge(s_f0_xgT, n + 1)
                pe.wait_ge(s_f0_w[r], tn * 48 + 48)
                if not (isinstance(n, int) and n < 2):
                    pe.wait_ge(s_f0_h, n - 1)
                for w, wt in enumerate((f0_wg, f0_wu)):
                    for e in range(2):
                        for h in range(HD):
                            last = nc.tensor.matmul(bank[2 + m][:, (2 * w + e) * P:(2 * w + e + 1) * P],
                                                    wt[:, r, e, h * P:(h + 1) * P],
                                                    f0_xgT[:, r, (2 * e + h) * P:(2 * e + h + 1) * P],
                                                    start=(h == 0), stop=(h == HD - 1))
                last.then_inc(s_f0_gu, 1)

            def down(n, r, m, tn):
                pe.wait_ge(s_f0_h, n + 1)
                if not (isinstance(n, int) and n < 2):
                    pe.wait_ge(s_f0_ye, n - 1)
                for e in range(2):
                    last = nc.tensor.matmul(bank[4 + m][:, e * D:(e + 1) * D], f0_hT[:, r, e * P:(e + 1) * P],
                                            f0_wd[:, r, e, :], start=True, stop=True)
                last.then_inc(s_f0_d, 1)

            def args(i, k):
                return i * TURN + k, k % RING, k % 2, i * (TURN // RING) + k // RING

            ssm_dt_pe(pe, 0)
            lag = 2
            for j in range(GB * HC - lag):
                ssm_pe(pe, 0, 0, j)

            def sums(i, k):
                if k >= lag:
                    ssm_pe(pe, 0, i, k - lag)
                else:
                    ssm_pe(pe, 0, i - 1, TURN + k - lag)

            turn(*args(0, 0))
            for k in range(TURN):
                turn(*args(0, k + 1))
                gate_up(*args(0, k))
                if k:
                    down(*args(0, k - 1))
            with pe.Fori(1, PAIRS // TURN - 1) as i:
                for k in range(TURN):
                    turn(*args(i, k + 1))
                    gate_up(*args(i, k))
                    down(*args(i, k - 1))
                    sums(i, k)
            last_turn = PAIRS // TURN - 1
            for k in range(TURN):
                if k < TURN - 1:
                    turn(*args(last_turn, k + 1))
                gate_up(*args(last_turn, k))
                down(*args(last_turn, k - 1))
                sums(last_turn, k)
            down(*args(last_turn, TURN - 1))
            for j in range(TURN - lag, TURN):
                ssm_pe(pe, 0, last_turn, j)

        def f0_act_eng(act):
            norm_act(act, 1)
            act.wait_ge(s_f0_top, 1)
            for i in range(NT):
                last = nc.scalar.activation(f0_prob[:, i, :], bank[2][:, i * E0:(i + 1) * E0], ACT.Exp,
                                            bias=f0_top[:, i:i + 1], accum_out=f0_sum[:, i:i + 1])
            last.then_inc(s_f0_exp, 1)

            def step(n, r, m):
                act.wait_ge(s_f0_T, n + 1)
                if not (isinstance(n, int) and n < RING):
                    act.wait_ge(s_f0_gu, n - (RING - 1))
                nc.scalar.copy(f0_xgT[:, r, :], bank[m][:, :]).then_inc(s_f0_xgT, 1)

            def silu(n, r, m):
                act.wait_ge(s_f0_gu, n + 1)
                if not (isinstance(n, int) and n < RING):
                    act.wait_ge(s_f0_h, n - (RING - 1))
                nc.scalar.activation(f0_sg[:, r, :], bank[2 + m][:, 0:2 * P], ACT.Tanh,
                                     scale=0.5).then_inc(s_f0_sg, 1)

            ssm_dt_act(act, 0)
            for j in range(GB * HC):
                ssm_act(act, 0, 0, j)
            step(0, 0, 0)
            for n in range(TURN):
                step(n + 1, (n + 1) % RING, (n + 1) % 2)
                silu(n, n % RING, n % 2)
            with act.Fori(1, PAIRS // TURN - 1) as i:
                for k in range(TURN):
                    step(i * TURN + (k + 1), (k + 1) % RING, (k + 1) % 2)
                    silu(i * TURN + k, k % RING, k % 2)
                    ssm_act(act, 0, i, k)
            for n in range(PAIRS - TURN, PAIRS):
                if n + 1 < PAIRS:
                    step(n + 1, (n + 1) % RING, (n + 1) % 2)
                silu(n, n % RING, n % 2)
                ssm_act(act, 0, B - 1, n % TURN)

        def f0_dve(dve):
            dve.wait_ge(s_l0_x, B)
            norm_dve(dve, 1)
            dve.wait_ge(s_f0_logit, 1)
            nc.vector.tensor_reduce(f0_top[:, :], bank[2][:, :].rearrange("p (i e) -> p i e", i=NT), AX_X, ALU.max,
                                    negate=True).then_inc(s_f0_top, 1)
            dve.wait_ge(s_f0_exp, 1)
            dve_link(nc.vector.reciprocal(f0_sum[:, :], f0_sum[:, :]))
            dve_link(nc.vector.tensor_tensor(f0_prob[:, :, :], f0_prob[:, :, :],
                                             f0_sum[:, :].unsqueeze(2).to_broadcast([P, NT, E0]), ALU.mult))
            for i in range(NT):
                last = nc.vector.max(f0_w[:, i, :], f0_prob[:, i, :])
            dve_link(last)
            for i in range(NT):
                nc.vector.match_replace(f0_left[:, i, :], f0_w[:, i, :], f0_prob[:, i, :], -1.0)
                last = nc.vector.max_index(f0_i[:, i, :], f0_w[:, i, :], f0_prob[:, i, :])
            dve_link(last)
            nc.vector.tensor_tensor(f0_mask[:, :, :], f0_left[:, :, :], f0_prob[:, :, :],
                                    ALU.not_equal).then_inc(s_f0_mask, 1)
            dve_link(nc.vector.tensor_copy(f0_if[:, :, :], f0_i[:, :, :]))
            dve.wait_ge(s_f0_const, 1)
            dve.wait_ge(s_f0_rank, 1)
            for i in range(NT):
                dve_link(nc.vector.tensor_tensor(f0_eq, iota_e[:, :].unsqueeze(1).to_broadcast([P, K0, E0]),
                                                 f0_if[:, i, :].unsqueeze(2).to_broadcast([P, K0, E0]), ALU.is_equal))
                dve_link(nc.vector.tensor_tensor(
                    f0_eq, f0_eq, bank[3][:, i * E0:(i + 1) * E0].unsqueeze(1).to_broadcast([P, K0, E0]), ALU.mult))
                dve_link(nc.vector.tensor_reduce(f0_pos[:, i, :], f0_eq, AX_X, ALU.add))
                miss = f0_left[:, i, 0:K0]
                nc.vector.tensor_scalar(f0_ok[:, i, :], f0_pos[:, i, :], float(CAP), None, ALU.is_lt)
                dve_link(nc.vector.tensor_scalar(miss, f0_pos[:, i, :], float(CAP), float(CAP * E0), ALU.is_ge, ALU.mult))
                dve_link(nc.vector.tensor_scalar(f0_pos[:, i, :], f0_pos[:, i, :], float(CAP - 1), float(E0), ALU.min, ALU.mult))
                dve_link(nc.vector.tensor_tensor(f0_loc[:, i, :], f0_pos[:, i, :], f0_if[:, i, :], ALU.add))
                nc.vector.tensor_copy(f0_get[:, i, :], f0_loc[:, i, :])
                nc.vector.tensor_tensor(f0_put[:, i, :], f0_loc[:, i, :], miss, ALU.add).then_inc(s_f0_idx, 1)
            dve.wait_ge(s_f0_idx, NT)
            dve_link(nc.vector.tensor_tensor(f0_w[:, :, :], f0_w[:, :, :], f0_ok[:, :, :], ALU.mult))
            dve_link(nc.vector.tensor_scalar(f0_w[:, :, :], f0_w[:, :, :], tanh_g[:, 1, 0:1], None, ALU.mult))

            def mult(n, r, m):
                dve.wait_ge(s_f0_sg, n + 1)
                if not (isinstance(n, int) and n < RING):
                    dve.wait_ge(s_f0_d, n - (RING - 1))
                if not (isinstance(n, int) and n < 1):
                    dve.wait_ge(s_f0_h, n)
                nc.vector.scalar_tensor_tensor(out=f0_act, in0=f0_sg[:, r, :], scalar=1.0, in1=bank[2 + m][:, 0:2 * P],
                                               op0=ALU.add, op1=ALU.mult).then_inc(s_f0_act, 1)
                dve.wait_ge(s_f0_act, n + 1)
                nc.vector.scalar_tensor_tensor(out=f0_hT[:, r, :], in0=f0_act, scalar=0.5, in1=bank[2 + m][:, 2 * P:4 * P],
                                               op0=ALU.mult, op1=ALU.mult).then_inc(s_f0_h, 1)

            def evict(n, r, m, tn):
                dve.wait_ge(s_f0_d, n + 1)
                if not (isinstance(n, int) and n < RING):
                    dve.wait_ge(s_f0_st[r], tn * 16)
                nc.vector.tensor_copy(f0_ye[:, r, :], bank[4 + m][:, :]).then_inc(s_f0_ye, 1)

            for c in range(HC):
                ssm_dt_dve(dve, 0, c)
            for j in range(GB * HC):
                ssm_dve(dve, 0, 0, j)
            for n in range(TURN):
                mult(n, n % RING, n % 2)
                if n:
                    evict(n - 1, (n - 1) % RING, (n - 1) % 2, (n - 1) // RING)
            with dve.Fori(1, PAIRS // TURN) as i:
                for k in range(TURN):
                    mult(i * TURN + k, k % RING, k % 2)
                    evict(i * TURN + (k - 1), (k - 1) % RING, (k - 1) % 2, i * (TURN // RING) + (k - 1) // RING)
                    ssm_dve(dve, 0, i, k, pool=True)
            n = PAIRS - 1
            evict(n, n % RING, n % 2, n // RING)
            ssm_sum_dve(dve, 0, B - 1)
            def add(g):
                dve.wait_ge(s_f0_cmb, 2 * K0 * (g + 1))
                for i in (2 * g, 2 * g + 1):
                    nc.vector.tensor_tensor(x[:, i, :], x[:, i, :], f0_sum_bank(i)[:, 0:D], ALU.add).then_inc(s_f0_x, 1)
                norm_stats(dve, (2 * g, 2 * g + 1), s_f0_x, 2 * g + 2)

            ssm_in_dve(dve, 1)
            for c in range(HC):
                ssm_conv_dve(dve, 1, c, range(DC))
            ssm_dt_dve(dve, 1, 0)
            add(0)
            ssm_dt_dve(dve, 1, 1)
            for g in range(1, NT // 2):
                add(g)

        def f0_sum_bank(i):
            return bank[(0, 1, 6, 7, 4, 5, 0, 1)[i]]

        def f0_diag_act(act, first, stop):
            for m in range(first, stop):
                i, k = f0_order[m]
                if m >= 4:
                    act.wait_ge(s_f0_cmb, m - 3)
                nc.scalar.activation(f0_diag[:, m % 4, :], ident[:, :], ACT.Copy, scale=f0_w[:, i, k:k + 1]).then_inc(s_f0_diag, 1)

        def f0_combine_pe(pe, first, stop):
            for m in range(first, stop):
                i, k = f0_order[m]
                if m == 0:
                    pe.wait_ge(s_f0_xgT, PAIRS)
                if m == 2 * K0:
                    pe.wait_ge(s_sp_e, 8)
                if k == 0 and i >= 6:
                    pe.wait_ge(s_f0_x, i - 5)
                if m % GB_ROWS == 0:
                    fetched = min(GB_ROWS, NT * K0 - m) + GB_ROWS * (m // GR)
                    pe.wait_ge(s_f0_back[m % GR // GB_ROWS], 16 * fetched)
                pe.wait_ge(s_f0_diag, m + 1)
                nc.tensor.matmul(f0_sum_bank(i)[:, 0:D], f0_diag[:, m % 4, :], f0_back[:, m % GR, :], start=(k == 0),
                                 stop=(k == K0 - 1)).then_inc(s_f0_cmb, 1)

        A1, R1, K1 = 64, 16, 4
        AR = A1 * R1
        CH = AR // P
        l1_back_end = F0_W + GR * D
        l1_AT = area(l1_back_end, HD, AR)
        l1_BT = area(l1_back_end + 2048, CH, D)
        l1_raw = l1_back_end + 4096
        l1_Arows = area(l1_raw, CH, D)
        l1_Brows = area(l1_raw + 2048, HD, AR)
        l1_Wrows = area(0, HD, D)
        l1_WT = area(512, HD, D)
        l1_sq = area(l1_raw, AR)
        l1_mv = area(l1_raw + 1024, AR)
        l1_P = area(l1_raw + 2048, 2, AR)
        l1_free = F0_W + NT * S
        l1_PT = area(l1_free, 2, AR)
        l1_eq = area(l1_free + 2 * AR, K1 * A1)
        assert l1_free + 2 * AR + K1 * A1 <= l1_back_end
        l1_arrow = sb("l1_arrow", [P, A1])
        l1_top = sb("l1_top", [P, 8])
        l1_idx = sb("l1_idx", [P, 8], U32)
        l1_idxf = sb("l1_idxf", [P, 8])
        l1_mask = sb("l1_mask", [P, 2, A1])
        l1_v = sb("l1_v", [P, 2, R1])
        l1_bias = sb("l1_bias", [1, D])
        ones_row = sb("ones_row", [1, P])
        ones_col = sb("ones_col", [P, 1])
        s_l1_ld = sem("s_l1_ld")
        s_l1_pt = sem("s_l1_pt")
        s_l1_prep = sem("s_l1_prep")
        s_l1_vec = sem("s_l1_vec")
        s_l1_sq = sem("s_l1_sq")
        s_l1_mv = sem("s_l1_mv")
        s_l1_v = sem("s_l1_v")
        s_l1_P = sem("s_l1_P")
        s_l1_Pt = sem("s_l1_Pt")
        s_l1_PT = sem("s_l1_PT")
        s_l1_out = sem("s_l1_out")
        s_l1_x = sem("s_l1_x")
        s_ones = sem("s_ones")
        l1_groups = [([l1_Arows[:, 4 * q + i, h * P:(h + 1) * P] for i in range(4)], l1_AT[:, h, q * HALF:(q + 1) * HALF])
                     for h in range(HD) for q in range(2)]
        l1_groups += [([l1_Brows[:, jh, (2 * q + i) * P:(2 * q + i + 1) * P] for i in range(2) for jh in range(HD)],
                       l1_BT[:, 2 * q:2 * q + 2, :].rearrange("p a b -> p (a b)")) for q in range(CH // 2)]
        l1_groups += [([l1_Wrows[:, jh, h * P:(h + 1) * P] for h in range(HD) for jh in range(HD)],
                       l1_WT.rearrange("p a b -> p (a b)"))]

        def l1_loads_sp(sp):
            sp.wait_ge(s_f0_ye, PAIRS)
            for r in range(RING):
                sp.wait_ge(s_f0_st[r], 16 * (PAIRS // RING))
            sp.dma_start(l1_Brows.rearrange("p h (a r) -> p h a r", r=R1)[:, 0, :, :],
                         A["L1_ffn_B"].rearrange("a (h p) r -> p h a r", p=P)[:, 0, :, :]).then_inc(s_l1_ld, 16)
            sp.dma_start(l1_Brows.rearrange("p h (a r) -> p h a r", r=R1)[:, 1, :, :],
                         A["L1_ffn_B"].rearrange("a (h p) r -> p h a r", p=P)[:, 1, :, :]).then_inc(s_l1_ld, 16)
            sp.dma_start(l1_Arows, A["L1_ffn_A"].rearrange("a r h -> (a r) h").rearrange("(c p) h -> p c h", p=P)).then_inc(s_l1_ld, 16)
            sp.dma_start(l1_Wrows, A["L1_ffn_W"].rearrange("(c p) h -> p c h", p=P)).then_inc(s_l1_ld, 16)
            sp.dma_start(l1_bias[:, :], A["L1_ffn_bias"].rearrange("(a n) -> a n", a=1)).then_inc(s_l1_ld, 16)

        def turn_pe(pe, groups, banks, written, copied, loads={}):
            for n, (blocks, dst) in enumerate(groups):
                if n in loads:
                    (loaded, base), count = loads[n]
                    pe.wait_ge(loaded, base + count)
                if n >= 2:
                    pe.wait_ge(copied[0], copied[1] + n - 1)
                at = 0
                for src in blocks:
                    rows = src.shape[0]
                    last = nc.tensor.transpose(bank[banks[n % 2]][0:src.shape[1], at:at + rows], src, ident[0:rows, 0:rows])
                    at += rows
                last.then_inc(written[0], 1)

        def turn_act(act, groups, banks, written, copied):
            for n, (blocks, dst) in enumerate(groups):
                act.wait_ge(written[0], written[1] + n + 1)
                nc.scalar.copy(dst, bank[banks[n % 2]][0:dst.shape[0], 0:dst.shape[1]]).then_inc(copied[0], 1)

        def l1_prep_pe(pe):
            pe.wait_ge(s_l1_ld, 16 * 5)
            turn_pe(pe, l1_groups, (2, 3), (s_l1_pt, 0), (s_l1_prep, 0))

        def l1_prep_act(act):
            turn_act(act, l1_groups, (2, 3), (s_l1_pt, 0), (s_l1_prep, 0))

        def l1_pe(pe):
            norm_pe(pe, 3, 2)
            pe.wait_ge(s_yT, 3 * NT // 2)
            pe.wait_ge(s_l1_prep, len(l1_groups))
            pe.wait_ge(s_ones, 1)

            def vectors(i):
                if i >= 2:
                    pe.wait_ge(s_l1_mv, i - 1)
                for q in range(2):
                    for h in range(HD):
                        last = nc.tensor.matmul(bank[2 + 2 * (i % 2) + q][:, :], yT[:, h, i * P:(i + 1) * P],
                                                l1_AT[:, h, q * HALF:(q + 1) * HALF], start=(h == 0), stop=(h == HD - 1))
                last.then_inc(s_l1_vec, 1)

            vectors(0)
            for i in range(NT):
                if i + 1 < NT:
                    vectors(i + 1)
                dst = bank[i % 2][:, 0:D]
                if i >= 2:
                    pe.wait_ge(s_l1_x, i - 1)
                for h in range(HD):
                    nc.tensor.matmul(dst, yT[:, h, i * P:(i + 1) * P], l1_WT[:, h, :], start=(h == 0), stop=False)
                nc.tensor.matmul(dst, ones_row[0:1, :], l1_bias[0:1, :], start=False, stop=False)
                pe.wait_ge(s_l1_P, i + 1)
                if i:
                    pe.wait_ge(s_l1_PT, i)
                for c in range(CH):
                    last = nc.tensor.transpose(bank[6 + c // 4][:, (c % 4) * P:(c % 4 + 1) * P],
                                               l1_P[:, i % 2, c * P:(c + 1) * P], ident[:, :])
                last.then_inc(s_l1_Pt, 1)
                pe.wait_ge(s_l1_PT, i + 1)
                for c in range(CH):
                    last = nc.tensor.matmul(dst, l1_PT[:, i % 2, c * P:(c + 1) * P], l1_BT[:, c, :],
                                            start=False, stop=(c == CH - 1))
                last.then_inc(s_l1_out, 1)

        def l1_act(act):
            norm_act(act, 2)

            def squares(i):
                act.wait_ge(s_l1_vec, i + 1)
                if i:
                    act.wait_ge(s_l1_mv, i)
                for q in range(2):
                    last = nc.scalar.activation(l1_sq[:, q * HALF:(q + 1) * HALF], bank[2 + 2 * (i % 2) + q][:, :], ACT.Square)
                last.then_inc(s_l1_sq, 1)

            squares(0)
            for i in range(NT):
                ssm_act(act, 1, 0, i)
                if i + 1 < NT:
                    squares(i + 1)
                act.wait_ge(s_l1_Pt, i + 1)
                if i >= 2:
                    act.wait_ge(s_l1_out, i - 1)
                for q in range(2):
                    last = nc.scalar.copy(l1_PT[:, i % 2, q * HALF:(q + 1) * HALF], bank[6 + q][:, :])
                last.then_inc(s_l1_PT, 1)

        def l1_dve(dve):
            V = nc.vector
            dve.wait_ge(s_z_x, B)
            norm_dve(dve, 3)

            def choose(i):
                dve.wait_ge(s_l1_sq, i + 1)
                dve_link(V.tensor_reduce(l1_arrow[:, :], l1_sq.rearrange("p (a r) -> p a r", r=R1), AX_X, ALU.add))
                dve_link(V.max(l1_top[:, :], l1_arrow[:, :]))
                dve_link(V.max_index(l1_idx[:, :], l1_top[:, :], l1_arrow[:, :]))
                dve_link(V.tensor_copy(l1_idxf[:, :], l1_idx[:, :]))
                eq = l1_eq.rearrange("p (k a) -> p k a", k=K1)
                dve_link(V.tensor_tensor(eq, iota_e[:, :].unsqueeze(1).to_broadcast([P, K1, A1]),
                                         l1_idxf[:, 0:K1].unsqueeze(2).to_broadcast([P, K1, A1]), ALU.is_equal))
                if i >= 2:
                    dve.wait_ge(s_l1_P, i - 1)
                dve_link(V.tensor_reduce(l1_mask[:, i % 2, :], l1_eq.rearrange("p (k a) -> p a k", k=K1), AX_X, ALU.add))
                for q in range(2):
                    half = A1 // 2
                    last = V.tensor_tensor(l1_mv[:, q * HALF:(q + 1) * HALF].rearrange("p (a r) -> p a r", r=R1),
                                           bank[2 + 2 * (i % 2) + q][:, :].rearrange("p (a r) -> p a r", r=R1),
                                           l1_mask[:, i % 2, q * half:(q + 1) * half].unsqueeze(2).to_broadcast([P, half, R1]),
                                           ALU.mult)
                last.then_inc(s_l1_mv, 1)
                dve.wait_ge(s_l1_mv, i + 1)
                dve_link(V.tensor_reduce(l1_v[:, i % 2, :], l1_mv.rearrange("p (a r) -> p r a", r=R1), AX_X, ALU.add))
                V.tensor_scalar(l1_v[:, i % 2, :], l1_v[:, i % 2, :], 1.0 / (K1 * K1), None, ALU.mult).then_inc(s_l1_v, 1)

            def add(i):
                dve.wait_ge(s_l1_out, i + 1)
                V.scalar_tensor_tensor(out=x[:, i, :], in0=bank[i % 2][:, 0:D], scalar=tanh_g[:, 1, 1:2], in1=x[:, i, :],
                                       op0=ALU.mult, op1=ALU.add).then_inc(s_l1_x, 1)
                norm_stats(dve, (i,), s_l1_x, i + 1)

            choose(0)
            for i in range(NT):
                ssm_dve(dve, 1, 0, i, pool=True)
                if i + 1 < NT:
                    choose(i + 1)
                if i:
                    ssm_reduce_dve(dve, 1, 0, i - 1)
                add(i)

        def l1_pool(pool):
            nc.gpsimd.memset(ones_col[:, :], 1.0)
            nc.gpsimd.memset(ones_row[:, :], 1.0).then_inc(s_ones, 1)
            for i in range(NT):
                pool.wait_ge(s_l1_v, i + 1)
                if i >= 2:
                    pool.wait_ge(s_l1_Pt, i - 1)
                if i < 2:
                    pool.wait_ge(s_l1_prep, len(l1_groups))
                nc.gpsimd.tensor_tensor(l1_P[:, i % 2, :].rearrange("p (a r) -> p a r", r=R1),
                                        l1_mask[:, i % 2, :].unsqueeze(2).to_broadcast([P, A1, R1]),
                                        l1_v[:, i % 2, :].unsqueeze(1).to_broadcast([P, A1, R1]),
                                        ALU.mult).then_inc(s_l1_P, 1)
                ssm_hC(pool, nc.gpsimd, 1, 0, i)

        H, HB = 16, 4
        L2_SCALE_EPS = EPS * P
        at = l1_free + 2 * AR + K1 * A1
        x_wq = area(at, 2, HD * P); at += 2 * HD * P
        x_wkv = area(at, 2, 2 * P); at += 2 * 2 * P
        x_wo = area(at, 2, D); at += 2 * D
        x_kT = area(at, 2, T); at += 2 * T
        x_qT = area(at, 2, T); at += 2 * T
        x_qsq = area(at, T); at += T
        x_P = area(at, 2, TPB * S); at += 2 * TPB * S
        x_PT = area(at, 2, TPB * S); at += 2 * TPB * S
        x_OT = area(at, 2, T); at += 2 * T
        assert at <= SSM_AT
        x_kv = area(0, 2 * NT, 2 * P)
        x_ksq = area(2 * NT * 2 * P, NT, P)
        assert 2 * NT * 2 * P + NT * P <= l1_free + 2 * AR + K1 * A1
        x_gqk = sb("x_gqk", [P, 2])
        x_kss = sb("x_kss", [P, NT])
        x_kve = sb("x_kve", [P, NT])
        x_rk = sb("x_rk", [P, NT])
        x_qve = sb("x_qve", [P, NT])
        x_rq = sb("x_rq", [P, 2, NT])
        x_top = sb("x_top", [P, 2, TPB])
        x_nb = sb("x_nb", [P, 2, TPB])
        x_sum = sb("x_sum", [P, 2, TPB])
        x_inv = sb("x_inv", [P, 2, TPB])
        s_x_g = sem("s_x_g")
        s_x_gqk = sem("s_x_gqk")
        s_x_w = [sem(f"s_x_w{r}") for r in range(2)]
        s_x_wo_ld = sem("s_x_wo_ld")
        (s_x_kv, s_x_kvc, s_x_ksq, s_x_kve, s_x_rk, s_x_khat, s_x_kt, s_x_kTc, s_x_q, s_x_qc, s_x_qsq, s_x_ss,
         s_x_qve, s_x_rq, s_x_S, s_x_top, s_x_max, s_x_exp, s_x_inv, s_x_P, s_x_Pt, s_x_PTc, s_x_O, s_x_Oc, s_x_wo,
         s_x_add) = (sem("s_x_" + n) for n in (
             "kv kvc ksq kve rk khat kt kTc q qc qsq ss qve rq S top max exp inv P Pt PTc O Oc wo add").split())

        def after(eng, sem_, value):
            if not (isinstance(value, int) and value <= 0):
                eng.wait_ge(sem_, value)

        def x_sp(sp):
            sp.dma_start(x_gqk[:, 0:1], A["L2_xattn_gq"].rearrange("(p a) -> p a", a=1)).then_inc(s_x_g, 16)
            sp.dma_start(x_gqk[:, 1:2], A["L2_xattn_gk"].rearrange("(p a) -> p a", a=1)).then_inc(s_x_g, 16)
            wq = A["L2_xattn_Wq"].rearrange("(h p) n -> p h n", h=HD)
            sp.wait_ge(s_f0_x, NT)

            def load(h, r):
                sp.dma_start(x_wq[:, r, :].rearrange("p (h n) -> p h n", h=HD), wq[:, :, ds(h * P, P)]).then_inc(s_x_w[r], 16)
                sp.dma_start(x_wkv[:, r, 0:P], A["L2_xattn_Wk"][:, ds(h * P, P)]).then_inc(s_x_w[r], 16)
                sp.dma_start(x_wkv[:, r, P:2 * P], A["L2_xattn_Wv"][:, ds(h * P, P)]).then_inc(s_x_w[r], 16)

            def load_wo(u):
                sp.dma_start(x_wo, A["L2_xattn_Wo"].rearrange("(h p) n -> p h n", p=P)[:, ds(2 * u, 2), :]).then_inc(s_x_wo_ld, 16)

            load(0, 0)
            load(1, 1)
            load_wo(0)

            def head(i, k):
                h = i * HB + k
                if not (isinstance(h, int) and h >= H - 2):
                    sp.wait_ge(s_x_kv, 4 * h + 4)
                    sp.wait_ge(s_x_q, 2 * h + 2)
                    load(h + 2, k % 2)
                if k % 2 == 0 and not (isinstance(h, int) and h < 2):
                    sp.wait_ge(s_x_wo, 2 * h)
                    load_wo(i * (HB // 2) + k // 2)

            for k in range(HB):
                ssm_load_sp(sp, 1, 1, k)
                head(0, k)
            with sp.Fori(1, H // HB - 1) as i:
                for k in range(HB):
                    ssm_load_sp(sp, 1, i + 1, k)
                    head(i, k)
            for k in range(HB):
                head(H // HB - 1, k)

        def x_pe(pe):
            norm_pe(pe, 4, 3)
            pe.wait_ge(s_yT, 4 * NT // 2)

            def kv(h, r, p, turns):
                if p == 0:
                    pe.wait_ge(s_x_w[r], turns * 48 + 48)
                after(pe, s_x_kvc, 4 * h + p - 1)
                if p < 2:
                    after(pe, s_x_kTc, 2 * h)
                for t in range(2):
                    last = nc.tensor.matmul(bank[p % 2][:, t * 2 * P:(t + 1) * 2 * P],
                                            ctxT[:, (2 * p + t) * P:(2 * p + t + 1) * P], x_wkv[:, r, :], start=True, stop=True)
                last.then_inc(s_x_kv, 1)

            def q(h, r, n, turns):
                if n == 0:
                    after(pe, s_x_qve, h)
                after(pe, s_x_qc, 2 * h + n - 1)
                for c in range(HD):
                    last = nc.tensor.matmul(bank[2 + n][:, :], x_wq[:, r, c * P:(c + 1) * P],
                                            yT[:, c, n * HALF:(n + 1) * HALF], start=(c == 0), stop=(c == HD - 1))
                last.then_inc(s_x_q, 1)

            def ss(h):
                pe.wait_ge(s_x_qsq, 2 * h + 2)
                for t in range(NT):
                    last = nc.tensor.matmul(bank[2][:, t:t + 1], x_qsq[:, t * P:(t + 1) * P], ones_col[:, :],
                                            start=True, stop=True)
                last.then_inc(s_x_ss, 1)

            def kt(h, r):
                pe.wait_ge(s_x_khat, h + 1)
                for n in range(2):
                    for t in range(4):
                        last = nc.tensor.transpose(bank[n][:, t * P:(t + 1) * P], x_kv[:, NT * r + 4 * n + t, 0:P], ident[:, :])
                    last.then_inc(s_x_kt, 1)

            def piece(h, r, b, turns):
                if b == 0:
                    kv(h, r, 0, turns)
                    kv(h, r, 1, turns)
                elif b == 1:
                    kv(h, r, 2, turns)
                    kv(h, r, 3, turns)
                    q(h, r, 0, turns)
                elif b == 2:
                    q(h, r, 1, turns)
                else:
                    ss(h)
                    kt(h, r)

            def project_out(u, p, to):
                if p == 0:
                    pe.wait_ge(s_x_wo_ld, u * 16 + 16)
                    pe.wait_ge(s_x_Oc, 8 * u + 8)
                for t in range(2):
                    for e in range(2):
                        last = nc.tensor.matmul(bank[to][:, t * D:(t + 1) * D], x_OT[:, e, (2 * p + t) * P:(2 * p + t + 1) * P],
                                                x_wo[:, e, :], start=(e == 0), stop=(e == 1))
                last.then_inc(s_x_wo, 1)

            def turned(s, par):
                pe.wait_ge(s_x_P, s + 1)
                after(pe, s_x_PTc, s)
                for j in range(TPB):
                    for i in range(TPB):
                        last = nc.tensor.transpose(bank[6][:, j * S + i * P:j * S + (i + 1) * P],
                                                   x_P[:, par, i * S + j * P:i * S + (j + 1) * P], ident[:, :])
                last.then_inc(s_x_Pt, 1)

            def values(s, r, b):
                pe.wait_ge(s_x_PTc, s + 1)
                after(pe, s_x_Oc, s)
                for j in range(TPB):
                    last = nc.tensor.matmul(bank[7][:, 0:S], x_kv[:, NT * r + TPB * b + j, P:2 * P],
                                            x_PT[:, b % 2, j * S:(j + 1) * S], start=(j == 0), stop=(j == TPB - 1))
                last.then_inc(s_x_O, 1)

            def step(i, k, b, first=False, final=False):
                h = i * HB + k
                s = i * (HB * B) + (k * B + b)
                if b == 0:
                    pe.wait_ge(s_x_qc, 2 * h + 2)
                    pe.wait_ge(s_x_kTc, 2 * h + 2)
                after(pe, s_x_exp, s - 1)
                for t in range(TPB):
                    last = nc.tensor.matmul(bank[4 + b % 2][:, t * S:(t + 1) * S],
                                            x_qT[:, k % 2, b * S + t * P:b * S + (t + 1) * P],
                                            x_kT[:, k % 2, b * S:(b + 1) * S], start=True, stop=True)
                last.then_inc(s_x_S, 1)
                if not first:
                    turned(s - 1, (b - 1) % 2)
                wo = k % 2 == 0 and not (isinstance(h, int) and h < 2)
                if wo and b == 1:
                    project_out(i * (HB // 2) + (k // 2 - 1), 0, 3)
                if not final:
                    if b == 2:
                        after(pe, s_x_add, 2 * h - (3 if k % 2 == 0 else 2))
                    if b == 3 and wo:
                        pe.wait_ge(s_x_add, 2 * h - 1)
                    piece(h + 1, (k + 1) % 2, b, i * (HB // 2) + (k + 1) // 2)
                if not first:
                    values(s - 1, (k if b else k - 1) % 2, (b - 1) % B)
                if wo:
                    u = i * (HB // 2) + (k // 2 - 1)
                    if b == 2:
                        pe.wait_ge(s_x_kvc, 4 * h + 8)
                        project_out(u, 1, 0)
                        project_out(u, 2, 1)
                    elif b == 3:
                        pe.wait_ge(s_x_qc, 2 * h + 4)
                        project_out(u, 3, 3)

            for b in range(B):
                piece(0, 0, b, 0)
            for k in range(HB):
                for b in range(B):
                    step(0, k, b, first=(k == 0 and b == 0))
            with pe.Fori(1, H // HB - 1) as i:
                for k in range(HB):
                    for b in range(B):
                        step(i, k, b)
            for k in range(HB):
                for b in range(B):
                    step(H // HB - 1, k, b, final=(k == HB - 1))
            turned(H * B - 1, 1)
            values(H * B - 1, 1, B - 1)
            pe.wait_ge(s_x_add, 2 * H - 4)
            for p in range(4):
                project_out(H // 2 - 1, p, p)

        def x_act(act):
            norm_act(act, 3)

            def kvcopy(h, r, p):
                act.wait_ge(s_x_kv, 4 * h + p + 1)
                after(act, s_x_O, 4 * h - 4)
                nc.scalar.copy(x_kv[:, NT * r + 2 * p:NT * r + 2 * p + 2, :],
                               bank[p % 2][:, :].rearrange("p (t n) -> p t n", t=2)).then_inc(s_x_kvc, 1)

            def ksq(h, r, p):
                act.wait_ge(s_x_kvc, 4 * h + p + 1)
                after(act, s_x_kve, h)
                for t in (2 * p, 2 * p + 1):
                    last = nc.scalar.activation(x_ksq[:, t, :], x_kv[:, NT * r + t, 0:P], ACT.Square,
                                                accum_out=x_kss[:, t:t + 1])
                last.then_inc(s_x_ksq, 1)

            def qcopy(h, r, n):
                act.wait_ge(s_x_q, 2 * h + n + 1)
                after(act, s_x_S, 4 * h - 4)
                nc.scalar.copy(x_qT[:, r, n * HALF:(n + 1) * HALF], bank[2 + n][:, :]).then_inc(s_x_qc, 1)
                act.wait_ge(s_x_qc, 2 * h + n + 1)
                after(act, s_x_ss, h)
                nc.scalar.activation(x_qsq[:, n * HALF:(n + 1) * HALF], x_qT[:, r, n * HALF:(n + 1) * HALF],
                                     ACT.Square).then_inc(s_x_qsq, 1)

            def kcopy(h, r):
                if isinstance(h, int) and h == 0:
                    act.wait_ge(s_x_gqk, 1)
                for n in range(2):
                    act.wait_ge(s_x_kt, 2 * h + n + 1)
                    after(act, s_x_S, 4 * h - 4)
                    nc.scalar.activation(x_kT[:, r, n * HALF:(n + 1) * HALF], bank[n][:, :], ACT.Copy,
                                         scale=x_gqk[:, 0:1]).then_inc(s_x_kTc, 1)

            def piece(h, r, b):
                if b < 2:
                    for p in (2 * b, 2 * b + 1):
                        kvcopy(h, r, p)
                    for p in (2 * b, 2 * b + 1):
                        ksq(h, r, p)
                if b == 1:
                    qcopy(h, r, 0)
                elif b == 2:
                    qcopy(h, r, 1)
                elif b == 3:
                    kcopy(h, r)

            def ptcopy(s, par):
                act.wait_ge(s_x_Pt, s + 1)
                after(act, s_x_O, s - 1)
                nc.scalar.copy(x_PT[:, par, :], bank[6][:, :]).then_inc(s_x_PTc, 1)

            def step(i, k, b, first=False, final=False, scan=True):
                h = i * HB + k
                s = i * (HB * B) + (k * B + b)
                if not first:
                    ptcopy(s - 1, (b - 1) % 2)
                act.wait_ge(s_x_max, s + 1)
                after(act, s_x_Pt, s - 1)
                for t in range(TPB):
                    last = nc.scalar.activation(x_P[:, b % 2, t * S:(t + 1) * S], bank[4 + b % 2][:, t * S:(t + 1) * S], ACT.Exp,
                                                bias=x_nb[:, b % 2, t:t + 1], scale=x_rq[:, k % 2, TPB * b + t:TPB * b + t + 1],
                                                accum_out=x_sum[:, b % 2, t:t + 1])
                last.then_inc(s_x_exp, 1)
                if not final:
                    piece(h + 1, (k + 1) % 2, b)
                if scan and b % 2 == 0:
                    ssm_act(act, 1, i + 1, 2 * k + b // 2)

            for b in range(B):
                piece(0, 0, b)
            for k in range(HB):
                for b in range(B):
                    step(0, k, b, first=(k == 0 and b == 0))
            with act.Fori(1, H // HB - 1) as i:
                for k in range(HB):
                    for b in range(B):
                        step(i, k, b)
            for k in range(HB):
                for b in range(B):
                    step(H // HB - 1, k, b, final=(k == HB - 1), scan=False)
            ptcopy(H * B - 1, 1)

        def x_dve(dve):
            V = nc.vector
            dve.wait_ge(s_x_g, 32)
            V.tensor_tensor(x_gqk[:, 0:1], x_gqk[:, 0:1], x_gqk[:, 1:2], ALU.mult).then_inc(s_x_gqk, 1)
            norm_dve(dve, 4)

            def krms(h):
                dve.wait_ge(s_x_ksq, 4 * h + 4)
                after(dve, s_x_rk, h)
                V.tensor_scalar(x_kve[:, :], x_kss[:, :], 1.0 / P, EPS, ALU.mult, ALU.add).then_inc(s_x_kve, 1)

            def qrms(h):
                dve.wait_ge(s_x_ss, h + 1)
                after(dve, s_x_rq, h)
                V.tensor_scalar(x_qve[:, :], bank[2][:, 0:NT], L2_SCALE_EPS, None, ALU.add).then_inc(s_x_qve, 1)

            def ocopy(s, r, b):
                dve.wait_ge(s_x_O, s + 1)
                V.tensor_copy(x_OT[:, r, b * S:(b + 1) * S], bank[7][:, 0:S]).then_inc(s_x_Oc, 1)

            def add(n, p, at_bank):
                dve.wait_ge(s_x_wo, n + 1)
                after(dve, s_x_add, n)
                rows = x[:, 2 * p:2 * p + 2, :].rearrange("p a n -> p (a n)")
                V.scalar_tensor_tensor(out=rows, in0=bank[at_bank][:, :], scalar=tanh_g[:, 0, 2:3], in1=rows,
                                       op0=ALU.mult, op1=ALU.add).then_inc(s_x_add, 1)

            def step(i, k, b, first=False, final=False, scan=True):
                h = i * HB + k
                s = i * (HB * B) + (k * B + b)
                par = b % 2
                if b == 0:
                    dve.wait_ge(s_x_rq, h + 1)
                dve.wait_ge(s_x_S, s + 1)
                after(dve, s_x_exp, s - 1)
                V.tensor_reduce(x_top[:, par, :], bank[4 + par][:, :].rearrange("p (t n) -> p t n", t=TPB), AX_X, ALU.max,
                                negate=True).then_inc(s_x_top, 1)
                dve.wait_ge(s_x_top, s + 1)
                V.tensor_tensor(x_nb[:, par, :], x_top[:, par, :], x_rq[:, k % 2, TPB * b:TPB * (b + 1)], ALU.mult).then_inc(s_x_max, 1)
                if scan and par:
                    ssm_in_product(dve, 1, i + 1, 2 * k + b // 2)
                dve.wait_ge(s_x_exp, s + 1)
                V.reciprocal(x_inv[:, par, :], x_sum[:, par, :]).then_inc(s_x_inv, 1)
                dve.wait_ge(s_x_inv, s + 1)
                for t in range(TPB):
                    last = V.tensor_scalar(x_P[:, par, t * S:(t + 1) * S], x_P[:, par, t * S:(t + 1) * S],
                                           x_inv[:, par, t:t + 1], None, ALU.mult)
                last.then_inc(s_x_P, 1)
                if k % 2 == 0 and not (isinstance(h, int) and h < 2) and b == 1:
                    add(2 * h - 4, 0, 3)
                if not first:
                    r, pb = (k if b else k - 1) % 2, (b - 1) % B
                    u = i * (HB // 2) + (k if b else k - 1) // 2
                    after(dve, s_x_wo, 4 * u + (pb - 3))
                    ocopy(s - 1, r, pb)
                if not final:
                    n, r = h + 1, (k + 1) % 2
                    if b == 2:
                        krms(n)
                    elif b == 3:
                        qrms(n)
                if k % 2 == 0 and not (isinstance(h, int) and h < 2):
                    u4 = 2 * h - 4
                    if b == 2:
                        add(u4 + 1, 1, 0)
                        add(u4 + 2, 2, 1)
                    elif b == 3:
                        add(u4 + 3, 3, 3)
                if scan:
                    j = 2 * k + b // 2
                    if par:
                        ssm_scan(dve, 1, i + 1, j)
                    elif j:
                        ssm_reduce_dve(dve, 1, i + 1, j - 1)
                    else:
                        ssm_reduce_dve(dve, 1, i, GB * HC - 1)

            krms(0)
            qrms(0)
            for k in range(HB):
                for b in range(B):
                    step(0, k, b, first=(k == 0 and b == 0))
            with dve.Fori(1, H // HB - 1) as i:
                for k in range(HB):
                    for b in range(B):
                        step(i, k, b)
            ssm_reduce_dve(dve, 1, B - 1, GB * HC - 1)
            for k in range(HB):
                for b in range(B):
                    step(H // HB - 1, k, b, final=(k == HB - 1), scan=False)
            after(dve, s_x_wo, 2 * H - 4)
            ocopy(H * B - 1, 1, B - 1)
            for p in range(4):
                add(2 * H - 4 + p, p, p)
                norm_stats(dve, (2 * p, 2 * p + 1), s_x_add, 2 * H - 3 + p)

        def x_pool(pool):
            def rms(n, slot):
                pool.wait_ge(s_x_kve, n + 1)
                after(pool, s_x_khat, n)
                nc.gpsimd.tensor_tensor(x_rk[:, :], x_kve[:, :], minus_half[:, :], ALU.pow).then_inc(s_x_rk, 1)
                pool.wait_ge(s_x_rk, n + 1)
                rows = x_kv[:, NT * slot:NT * (slot + 1), 0:P]
                nc.gpsimd.tensor_tensor(rows, rows, x_rk[:, :].unsqueeze(2).to_broadcast([P, NT, P]),
                                        ALU.mult).then_inc(s_x_khat, 1)

            def qrms(n, r):
                pool.wait_ge(s_x_qve, n + 1)
                after(pool, s_x_exp, 4 * n - 4)
                nc.gpsimd.tensor_tensor(x_rq[:, r, :], x_qve[:, :], minus_half[:, :], ALU.pow).then_inc(s_x_rq, 1)

            def head(i, k, final=False, scan=True):
                h = i * HB + k
                if scan:
                    ssm_hC(pool, nc.gpsimd, 1, i + 1, 2 * k)
                if not final:
                    rms(h + 1, (k + 1) % 2)
                    qrms(h + 1, (k + 1) % 2)
                if scan:
                    ssm_hC(pool, nc.gpsimd, 1, i + 1, 2 * k + 1)

            rms(0, 0)
            qrms(0, 0)
            for k in range(HB):
                head(0, k)
            with pool.Fori(1, H // HB - 1) as i:
                for k in range(HB):
                    head(i, k)
            for k in range(HB):
                head(H // HB - 1, k, final=(k == HB - 1), scan=False)

        E2, F2, FS2, K2 = 8, 176, 352, 2
        RC = E2 * F2 // P
        g_rows = [P] * RC + [min(P, FS2 - i * P) for i in range(-(-FS2 // P))]
        GC = len(g_rows)
        at = 0
        g_gT = area(at, GC * D); at += GC * D
        g_uT = area(at, GC * D); at += GC * D
        g_dT = area(at, GC, D); at += GC * D
        g_wbc = area(at, RC, T); at += RC * T
        g_raw = ARENA - (2 * GC * D + HD * (E2 * F2 + FS2))
        assert at <= g_raw and SSM_AT <= g_raw
        g_raw_g = area(g_raw, GC, D)
        g_raw_u = area(g_raw + GC * D, GC, D)
        g_raw_d = area(g_raw + 2 * GC * D, HD, E2 * F2 + FS2)
        g_sg = area(g_raw, 2, HALF)
        g_m = area(g_raw + 2 * HALF, HALF)
        g_hT = area(g_raw + 3 * HALF, 4, HALF)
        g_wr = sb("g_wr", [E2, D])
        e_gw = sb("e_gw", [32, D])
        e_gwT = sb("e_gwT", [P, HD, 32])
        g_wrT = sb("g_wrT", [P, HD, E2])
        g_p = sb("g_p", [P, NT, E2])
        g_top = sb("g_top", [P, NT])
        g_sum = sb("g_sum", [P, NT])
        g_best = sb("g_best", [P, NT, 8])
        g_idx = sb("g_idx", [P, NT, 8], U32)
        g_idxf = sb("g_idxf", [P, NT, 8])
        g_eq = sb("g_eq", [P, NT, 2, E2])
        g_w = sb("g_w", [P, NT, E2])
        g_wT = ssm_y[0:E2, 0, :, :, :].rearrange(
            "p b c l -> p (b c l)")[:, 0:T]
        w_rows = nc.dram_tensor("w_rows", [E2, T], F32, kind="Internal").ap()

        def wait(eng, signal, value):
            eng.wait_ge(signal[0], signal[1] + value)

        s_g_ld = (s_l1_ld, 16 * 5)
        s_g_pt = (s_l1_pt, len(l1_groups))
        s_g_prep = (s_l1_prep, len(l1_groups))
        s_g_logit = (s_l1_vec, NT)
        s_g_top = (s_l1_sq, NT)
        s_g_exp = (s_l1_mv, NT)
        s_g_w = (s_l1_v, NT)
        s_g_wt = (s_l1_Pt, NT)
        s_g_wT = (s_l1_PT, NT)
        s_g_rows = (s_x_g, 32)
        s_g_bc = (s_x_wo_ld, 16 * H // 2)
        s_g_bc0 = (sem("s_g_bc0"), 0)
        FEW = 2
        s_g_gu = (s_l1_P, NT)
        s_g_sg = (s_x_ksq, 4 * H)
        s_g_h = (s_x_kvc, 4 * H)
        s_g_d = (s_l1_out, NT)
        s_g_x = (s_l1_x, NT)
        s_g_ldg, s_g_ldu, s_g_ldd = (sem("s_g_ldg"), 0), (sem("s_g_ldu"), 0), (sem("s_g_ldd"), 0)
        g_groups = [([g_wr[:, h * P:(h + 1) * P] for h in range(HD)], g_wrT[:, :, :].rearrange("p h e -> p (h e)"))]
        g_groups.append(([e_gw[:, h * P:(h + 1) * P] for h in range(HD)], e_gwT[:, :, :].rearrange("p h e -> p (h e)")))
        for raw, dst in ((g_raw_g, g_gT), (g_raw_u, g_uT)):
            for c in range(0, GC, 2):
                cols = sum(HD * g_rows[k] for k in (c, c + 1))
                g_groups.append(([raw[0:g_rows[k], k, h * P:(h + 1) * P] for k in (c, c + 1) for h in range(HD)],
                                 dst[:, c * D:c * D + cols]))
        for cs in [(c, c + 1) for c in range(0, GC - 2, 2)] + [(GC - 2,), (GC - 1,)]:
            rows = g_rows[cs[0]]
            g_groups.append(([g_raw_d[:, jh, c * P:c * P + rows] for c in cs for jh in range(HD)],
                             g_dT[0:rows, cs[0]:cs[-1] + 1, :].rearrange("p c n -> p (c n)")))
        g_spans = []
        for e in range(E2):
            f = e * F2
            while f < (e + 1) * F2:
                stop = min((f // P + 1) * P, (e + 1) * F2)
                g_spans.append((f // P, f % P, stop - f // P * P, e))
                f = stop

        def g_sp(sp):
            sp.wait_ge(s_ssm_red_y, GROUPS)
            pad = FS2 // P * P
            sp.dma_start(g_wr[:, :], A["L2_ffn_Wr"]).then_inc(s_g_ld[0], 16)
            sp.dma_start(e_gw[:, :], A["L3_ffn_gate_w"]).then_inc(s_g_ld[0], 16)
            for dst, name, shared, loaded in ((g_raw_g, "Wg", "Wsg", s_g_ldg), (g_raw_u, "Wu", "Wsu", s_g_ldu)):
                sp.dma_start(dst[:, 0:RC, :], A["L2_ffn_" + name].rearrange("e f d -> (e f) d").rearrange(
                    "(c p) d -> p c d", p=P)).then_inc(loaded[0], 16)
                sp.dma_start(dst[:, RC:GC - 1, :], A["L2_ffn_" + shared][0:pad, :].rearrange("(c p) d -> p c d", p=P)
                             ).then_inc(loaded[0], 16)
                sp.dma_start(dst[0:FS2 - pad, GC - 1, :], A["L2_ffn_" + shared][pad:FS2, :]).then_inc(loaded[0], 16)
            for jh in range(HD):
                sp.dma_start(g_raw_d[:, jh, 0:E2 * F2].rearrange("p (e f) -> p e f", e=E2),
                             A["L2_ffn_Wd"].rearrange("e (h p) f -> p h e f", p=P)[:, jh, :, :]).then_inc(s_g_ldd[0], 16)
            sp.dma_start(g_raw_d[:, :, E2 * F2:], A["L2_ffn_Wsd"].rearrange("(h p) f -> p h f", p=P)).then_inc(s_g_ldd[0], 16)
            wait(sp, s_g_wT, 2)
            sp.dma_start(w_rows, g_wT[:, :]).then_inc(s_g_rows[0], 16)
            wait(sp, s_g_rows, 16)
            for c, p0, p1, e in g_spans:
                sp.dma_start(g_wbc[p0:p1, c, :], w_rows[e:e + 1, :].to_broadcast([p1 - p0, T])
                             ).then_inc((s_g_bc0 if c < FEW else s_g_bc)[0], 16)

        g_steps = [(n, c) for n in range(2) for c in list(range(RC, GC)) + list(range(RC))]

        def g_pe(pe):
            turn_pe(pe, g_groups, (4, 5), s_g_pt, s_g_prep,
                    {0: (s_g_ld, 16 * 2), 2: (s_g_ldg, 16 * 3), 2 + GC // 2: (s_g_ldu, 16 * 3), 2 + GC: (s_g_ldd, 16 * 3)})
            norm_pe(pe, 5, 4)
            pe.wait_ge(s_yT, 5 * NT // 2)
            wait(pe, s_g_prep, len(g_groups))
            for i in range(NT):
                for h in range(HD):
                    last = nc.tensor.matmul(bank[6][:, i * E2:(i + 1) * E2], yT[:, h, i * P:(i + 1) * P], g_wrT[:, h, :],
                                            start=(h == 0), stop=(h == HD - 1))
            last.then_inc(s_g_logit[0], 1)

            def gate_up(t):
                n, c = g_steps[t]
                rows = g_rows[c]
                if t >= 2:
                    wait(pe, s_g_h, t - 1)
                for w, wt in enumerate((g_gT, g_uT)):
                    for h in range(HD):
                        last = nc.tensor.matmul(bank[2 * (t % 2) + w][0:rows, :], wt[:, c * D + h * rows:c * D + (h + 1) * rows],
                                                yT[:, h, n * HALF:(n + 1) * HALF], start=(h == 0), stop=(h == HD - 1))
                last.then_inc(s_g_gu[0], 1)

            def down(t):
                n, c = g_steps[t]
                rows = g_rows[c]
                wait(pe, s_g_h, t + 1)
                for i in range(NT // 2):
                    last = nc.tensor.matmul(bank[4 + 2 * n + i // 2][:, i % 2 * D:(i % 2 + 1) * D],
                                            g_hT[0:rows, t % 4, i * P:(i + 1) * P], g_dT[0:rows, c, :],
                                            start=(t % GC == 0 and i % 2 == 0), stop=(t % GC == GC - 1),
                                            skip_group_check=True)
                last.then_inc(s_g_d[0], 1)

            gate_up(0)
            wait(pe, s_g_w, 1)
            for q in range(2):
                for i in range(4):
                    last = nc.tensor.transpose(bank[6 + q][0:E2, i * P:(i + 1) * P], g_w[:, 4 * q + i, :], ident[:, :])
            last.then_inc(s_g_wt[0], 1)
            gate_up(1)
            for t in range(2 * GC):
                if t == GC:
                    wait(pe, s_g_wT, 2)
                if t + 1 < 2 * GC and t:
                    gate_up(t + 1)
                down(t)

        def g_act(act):
            act.wait_ge(s_x_add, 2 * H)
            turn_act(act, g_groups, (4, 5), s_g_pt, s_g_prep)
            norm_act(act, 4)
            wait(act, s_g_top, 1)
            for i in range(NT):
                last = nc.scalar.activation(g_p[:, i, :], bank[6][:, i * E2:(i + 1) * E2], ACT.Exp,
                                            bias=g_top[:, i:i + 1], accum_out=g_sum[:, i:i + 1])
            last.then_inc(s_g_exp[0], 1)
            for t in range(2 * GC):
                if t == 1:
                    wait(act, s_g_wt, 1)
                    for q in range(2):
                        nc.scalar.copy(g_wT[:, q * HALF:(q + 1) * HALF], bank[6 + q][0:E2, :]).then_inc(s_g_wT[0], 1)
                rows = g_rows[g_steps[t][1]]
                wait(act, s_g_gu, t + 1)
                if t >= 2:
                    wait(act, s_g_h, t - 1)
                nc.scalar.activation(g_sg[0:rows, t % 2, :], bank[2 * (t % 2)][0:rows, :], ACT.Silu).then_inc(s_g_sg[0], 1)

        def g_dve(dve):
            V = nc.vector
            dve.wait_ge(s_x_add, 2 * H)
            norm_dve(dve, 5)
            wait(dve, s_g_logit, 1)
            V.tensor_reduce(g_top[:, :], bank[6][:, 0:NT * E2].rearrange("p (i e) -> p i e", i=NT), AX_X, ALU.max,
                            negate=True).then_inc(s_g_top[0], 1)
            wait(dve, s_g_exp, 1)
            dve_link(V.reciprocal(g_sum[:, :], g_sum[:, :]))
            dve_link(V.tensor_tensor(g_p[:, :, :], g_p[:, :, :], g_sum[:, :].unsqueeze(2).to_broadcast([P, NT, E2]), ALU.mult))
            for i in range(NT):
                last = V.max(g_best[:, i, :], g_p[:, i, :])
            dve_link(last)
            for i in range(NT):
                last = V.max_index(g_idx[:, i, :], g_best[:, i, :], g_p[:, i, :])
            dve_link(last)
            dve_link(V.tensor_copy(g_idxf[:, :, :], g_idx[:, :, :]))
            for i in range(NT):
                last = V.tensor_tensor(g_eq[:, i, :, :], iota_e[:, 0:E2].unsqueeze(1).to_broadcast([P, K2, E2]),
                                       g_idxf[:, i, 0:K2].unsqueeze(2).to_broadcast([P, K2, E2]), ALU.is_equal)
            dve_link(last)
            dve_link(V.tensor_tensor(g_w[:, :, :], g_eq[:, :, 0, :], g_eq[:, :, 1, :], ALU.add))
            V.tensor_tensor(g_w[:, :, :], g_w[:, :, :], g_p[:, :, :], ALU.mult).then_inc(s_g_w[0], 1)

            def add(n):
                wait(dve, s_g_d, GC * (n + 1))
                for i in range(2):
                    rows = x[:, 4 * n + 2 * i:4 * n + 2 * i + 2, :].rearrange("p a n -> p (a n)")
                    V.scalar_tensor_tensor(out=rows, in0=bank[4 + 2 * n + i][:, :], scalar=tanh_g[:, 1, 2:3], in1=rows,
                                           op0=ALU.mult, op1=ALU.add).then_inc(s_g_x[0], 1)
                norm_stats(dve, range(4 * n, 4 * n + 4), s_g_x[0], s_g_x[1] + 2 * n + 2)

            for t in range(2 * GC):
                n, c = g_steps[t]
                rows = g_rows[c]
                wait(dve, s_g_sg, t + 1)
                if t >= 4:
                    wait(dve, s_g_d, t - 3)
                if t:
                    wait(dve, s_g_h, t)
                h = g_hT[0:rows, t % 4, :]
                if c >= RC:
                    V.tensor_tensor(h, g_sg[0:rows, t % 2, :], bank[2 * (t % 2) + 1][0:rows, :], ALU.mult).then_inc(s_g_h[0], 1)
                else:
                    few = len([s for s in g_spans if s[0] < FEW])
                    if t == GC - RC:
                        wait(dve, s_g_bc0, 16 * few)
                    if t == GC - RC + FEW:
                        wait(dve, s_g_bc, 16 * (len(g_spans) - few))
                    dve_link(V.tensor_tensor(g_m, g_sg[:, t % 2, :], bank[2 * (t % 2) + 1][:, :], ALU.mult))
                    V.tensor_tensor(h, g_m, g_wbc[:, c, n * HALF:(n + 1) * HALF], ALU.mult).then_inc(s_g_h[0], 1)
                if t == GC:
                    add(0)
            add(1)

        E3, F3, K3, GROUP3 = 32, 96, 4, 2
        E3S, F3S, SMALL = E3 // GROUP3, 128, 0.05
        TILES = T * K3 // P + E3
        assert TILES == E0 and F3S == P
        at = 0
        e_w = arena[:, at:at + E3 * HD * 2 * F3].rearrange(
            "p (e h n) -> p e h n", e=E3, h=HD); at += E3 * HD * 2 * F3
        e_cw = arena[:, at:at + E3S * HD * 2 * F3S].rearrange("p (e h n) -> p e h n", e=E3S, h=HD); at += E3S * HD * 2 * F3S
        e_wd = area(at, E3, D); at += E3 * D
        e_cwd = area(at, E3S, D); at += E3S * D
        assert at <= ARENA
        e_back = area(0, NT * K3, D)
        scan_y = ssm_y[:, :, :, :, :].rearrange("p m b c l -> p (m b c l)")
        XR = 8
        e_xg = y
        e_xgT = scan_y[:, 4 * D:8 * D].rearrange("p (r n) -> p r n", r=4)
        e_sg = scan_y[:, 8 * D:10 * D].rearrange("p (r n) -> p r n", r=2)
        e_h = scan_y[:, 10 * D:12 * D].rearrange("p (r n) -> p r n", r=2)
        e_hT = scan_y[:, 12 * D:14 * D].rearrange("p (r n) -> p r n", r=2)
        e_ye = ctxT[:, :].rearrange("p (r n) -> p r n", r=4)
        e_eq = yT[:, 0, :].rearrange("p (i k e) -> p i k e", i=NT, k=K3)
        e_eq2 = yT[:, 1, :].rearrange("p (i k e) -> p i k e", i=NT, k=K3)
        e_cmp = yT[:, :, :].rearrange("p h n -> p (h n)").rearrange("p (t e) -> p t e", e=E3)
        e_mask = f0_mask[:, :, 0:E3]
        e_p = sb("e_p", [P, NT, E3])
        e_sig = sb("e_sig", [P, NT, E3])
        e_pos = sb("e_pos", [P, NT, E3])
        e_top = sb("e_top", [P, NT])
        e_sum = sb("e_sum", [P, NT])
        e_wk = sb("e_wk", [P, NT, K3])
        e_wsum = sb("e_wsum", [P, NT])
        e_locf = sb("e_locf", [P, NT, K3])
        e_loc = sb("e_loc", [P, NT, K3], I32)
        e_low = sb("e_low", [P, NT, K3], I32)
        e_tot = sb("e_tot", [P, E3])
        e_ge = sb("e_ge", [P, E3, NT])
        e_tiles = sb("e_tiles", [P, E3])
        e_cum = sb("e_cum", [P, E3])
        e_base = sb("e_base", [P, E3])
        e_tabf = e_sig[:, :, :].rearrange("p i e -> p (i e)")[0:1, 0:TILES]
        e_tab = sb("e_tab", [1, TILES], I32)
        s_e_new = sem("s_e_new")
        s_e_tab = sem("s_e_tab")
        s_e_pad = sem("s_e_pad")
        s_e_logit, s_e_top, s_e_exp, s_e_mask, s_e_rank = (
            (s, 1) for s in (s_f0_logit, s_f0_top, s_f0_exp, s_f0_mask, s_f0_rank))
        s_e_idx = (s_f0_idx, NT)
        s_e_zero, s_e_yrows, s_e_slots = (s_f0_zero, 16), (s_f0_yrows, 16), (s_f0_slots, 16)
        s_e_put = (s_f0_put, 16 * NT * K0)
        s_e_xg = [(s, 2 * 16 * PAIRS // RING) for s in s_f0_xg] + [(sem(f"s_e_xg{r}"), 0) for r in range(4, XR)]
        s_e_T, s_e_xgT, s_e_gu, s_e_sg, s_e_mul, s_e_Ht, s_e_d, s_e_ye = (
            (s, PAIRS) for s in (s_f0_T, s_f0_xgT, s_f0_gu, s_f0_sg, s_f0_h, s_f0_act, s_f0_d, s_f0_ye))
        s_e_hTc = (s_x_O, H * B)
        s_e_st = [(s, 16 * PAIRS // RING) for s in s_f0_st]
        s_e_ld = (s_x_w[0], 48 * H // 2)
        s_e_back = [(s, 16 * len([m for m in range(NT * K0) if m % GR // GB_ROWS == g])) for g, s in enumerate(s_f0_back)]
        s_e_x = (s_f0_x, NT)
        EL = 10

        def e_sp(sp):
            sp.dma_start(slot_token.rearrange("(p n) a -> p (n a)", p=P), zero_slots[:, :]).then_inc(s_e_zero[0], 16)
            wait(sp, s_g_x, 4)
            for dst, n, name in ((e_w, F3, "W"), (e_cw, F3S, "cW")):
                for w, kind in enumerate("gu"):
                    src = A["L3_ffn_" + name + kind].rearrange("e (h p) i -> p h e i", p=P)
                    for h in range(HD):
                        sp.dma_start(dst[:, :, h, w * n:(w + 1) * n], src[:, h, :, :]).then_inc(s_e_ld[0], 16)
            sp.dma_start(e_wd[0:F3, :, :], A["L3_ffn_Wd"].rearrange("e i n -> i e n")).then_inc(s_e_ld[0], 16)
            sp.dma_start(e_cwd, A["L3_ffn_cWd"].rearrange("e i n -> i e n")).then_inc(s_e_ld[0], 16)
            sp.wait_ge(s_y, 8 * NT)
            sp.dma_start(y_rows.rearrange("(i p) d -> p i d", p=P), y[:, :, :]).then_inc(s_e_yrows[0], 16)

            def store(t, r):
                wait(sp, s_e_ye, t + 1)
                sp.dma_start(slot_out.rearrange("(c t) d -> c t d", t=TILES)[:, ds(t, 1), :],
                             e_ye[:, r, :].unsqueeze(1)).then_inc(s_e_st[r][0], 16)

            with sp.Fori(0, TILES // 4) as i:
                for k in range(4):
                    store(i * 4 + k, k)

        def e_pool(pool):
            norm_pool(pool, 7)
            wait(pool, s_e_zero, 16)
            for i in range(NT):
                wait(pool, s_e_idx, i + 1)
                for k in range(K3):
                    nc.gpsimd.indirect_dma_start(
                        out=slot_token, out_offset=bass.IndirectOffsetOnAxis(ap=e_loc[:, i, k:k + 1], axis=0),
                        in_=token_id[:, i:i + 1], in_offset=None, bounds_check=CAP * E0 - 1,
                        oob_is_err=True).then_inc(s_e_put[0], 16)
            wait(pool, s_e_put, 16 * NT * K3)
            pool.dma_start(slots[:, :], slot_token.rearrange("(c t) a -> c (t a)", t=TILES)).then_inc(s_e_slots[0], 16)
            wait(pool, s_e_slots, 16)
            wait(pool, s_e_yrows, 16)
            for t in range(TILES):
                if t >= XR:
                    wait(pool, s_e_T, t - XR + 1)
                nc.gpsimd.indirect_dma_start(
                    out=e_xg[:, t % XR, :], out_offset=None, in_=y_rows,
                    in_offset=bass.IndirectOffsetOnAxis(ap=slots[:, t:t + 1], axis=0),
                    bounds_check=T - 1, oob_is_err=True).then_inc(s_e_xg[t % XR][0], 16)
            for r in range(4):
                wait(pool, s_e_st[r], 16 * TILES // 4)
            for m in range(NT * K3):
                nc.gpsimd.indirect_dma_start(
                    out=e_back[:, m, :], out_offset=None, in_=slot_out,
                    in_offset=bass.IndirectOffsetOnAxis(ap=e_loc[:, m // K3, m % K3:m % K3 + 1], axis=0),
                    bounds_check=CAP * E0 - 1, oob_is_err=True).then_inc(s_e_back[m // K3][0], 16)

        def e_route_pe(pe):
            norm_pe(pe, 7, 5)
            pe.wait_ge(s_yT, 6 * NT // 2)
            for i in range(NT):
                for h in range(HD):
                    last = nc.tensor.matmul(bank[2][:, i * E3:(i + 1) * E3], yT[:, h, i * P:(i + 1) * P], e_gwT[:, h, :],
                                            start=(h == 0), stop=(h == HD - 1))
            last.then_inc(s_e_logit[0], 1)
            wait(pe, s_e_mask, 1)
            for j in range(NT):
                nc.tensor.matmul(bank[4][:, 0:E3], ones_b[:, :], e_mask[:, j, :], start=(j == 0), stop=(j == NT - 1))
            for i in range(NT):
                for j in range(i + 1):
                    last = nc.tensor.matmul(bank[3][:, i * E3:(i + 1) * E3], tri[:, :] if j == i else ones_b[:, :],
                                            e_mask[:, j, :], start=(j == 0), stop=(j == i))
            last.then_inc(s_e_rank[0], 1)

        def e_steps(eng, step):
            for k in range(XR):
                step(k, k, 0)
            with eng.Fori(1, TILES // XR - 1) as i:
                for k in range(XR):
                    step(i * XR + k, k, i)
            for t in range(TILES - XR, TILES + 2):
                step(t, t % XR, t // XR)

        def static(t):
            return isinstance(t, int)

        def e_pe(pe):
            e_route_pe(pe)

            def turn(t, r, turns):
                wait(pe, s_e_xg[r], turns * 16 + 16)
                if not (static(t) and t < 2):
                    wait(pe, s_e_xgT, t - 1)
                for h in range(HD):
                    last = nc.tensor.transpose(bank[t_bank(r)][:, h * P:(h + 1) * P], e_xg[:, r, h * P:(h + 1) * P], ident[:, :])
                last.then_inc(s_e_T[0], 1)

            def t_bank(r):
                return r % 2

            read = {}

            def experts(t, k):
                if k not in read:
                    e = pe.value_load(e_tab[0:1, ds(t, 1)], min_val=0, max_val=E3 - 1)
                    read[k] = e, e // GROUP3
                return read[k]

            def gate_up(t, r, k):
                e, c = experts(t, k)
                wait(pe, s_e_xgT, t + 1)
                if not (static(t) and t < 2):
                    wait(pe, s_e_mul, t - 1)
                to = bank[2 + r % 2][:, :].rearrange("p (w n) -> p w n", w=2)
                for src, which, dst in ((e_w, e, to[:, :, 0:F3]), (e_cw, c, to[:, :, P:2 * P])):
                    for h in range(HD):
                        last = nc.tensor.matmul(dst, e_xgT[:, r, h * P:(h + 1) * P],
                                                src[:, ds(which, 1), h, :].rearrange("p a (w n) -> p (a w) n", w=2),
                                                start=(h == 0), stop=(h == HD - 1))
                last.then_inc(s_e_gu[0], 1)

            def h_turn(t, r):
                wait(pe, s_e_mul, t + 1)
                if not (static(t) and t < 2):
                    wait(pe, s_e_hTc, t - 1)
                for w in range(2):
                    last = nc.tensor.transpose(bank[4 + r % 2][:, w * P:(w + 1) * P], e_h[:, r % 2, w * P:(w + 1) * P], ident[:, :])
                last.then_inc(s_e_Ht[0], 1)

            def down(t, r, k):
                e, c = experts(t, k)
                wait(pe, s_e_hTc, t + 1)
                if not (static(t) and t < 2):
                    wait(pe, s_e_ye, t - 1)
                nc.tensor.matmul(bank[6 + r % 2][:, 0:D], e_hT[0:F3, r % 2, 0:P],
                                 e_wd[0:F3, ds(e, 1), :].rearrange("p a n -> p (a n)"), start=True, stop=False)
                nc.tensor.matmul(bank[6 + r % 2][:, 0:D], e_hT[:, r % 2, P:2 * P],
                                 e_cwd[:, ds(c, 1), :].rearrange("p a n -> p (a n)"), start=False, stop=True
                                 ).then_inc(s_e_d[0], 1)

            wait(pe, s_e_ld, 16 * EL)
            pe.wait_ge(s_e_new, 2)
            pe.wait_ge(s_e_tab, 1)
            pe.wait_ge(s_e_pad, 1)
            turn(0, 0, 0)

            def step(t, k, turns):
                if k == 0:
                    read.clear()
                if not (static(t) and t + 1 >= TILES):
                    turn(t + 1, (k + 1) % XR, turns + (k + 1) // XR)
                if not (static(t) and t >= TILES):
                    gate_up(t, k % 4, k)
                if not (static(t) and not 0 <= t - 1 < TILES):
                    h_turn(t - 1, (k - 1) % 4)
                if not (static(t) and t < 2):
                    down(t - 2, (k - 2) % 4, k - 2)

            e_steps(pe, step)

        def e_act(act):
            norm_act(act, 5)
            act.wait_ge(s_e_new, 1)
            nc.scalar.activation(e_p[:, :, :], e_p[:, :, :], ACT.Exp)
            nc.scalar.activation(e_sig[:, :, :], bank[2][:, 0:NT * E3].rearrange("p (i e) -> p i e", i=NT), ACT.Exp,
                                 scale=-1.0).then_inc(s_e_exp[0], 1)
            wait(act, s_e_ld, 16 * EL)
            flat = e_cwd.rearrange("p c n -> p (c n)")
            nc.scalar.mul(flat, flat, SMALL).then_inc(s_e_new, 1)

            def xgT_copy(t, r):
                wait(act, s_e_T, t + 1)
                if not (static(t) and t < 4):
                    wait(act, s_e_gu, t - 3)
                nc.scalar.copy(e_xgT[:, r, :], bank[r % 2][:, 0:2 * P]).then_inc(s_e_xgT[0], 1)

            def silu(t, r):
                wait(act, s_e_gu, t + 1)
                if not (static(t) and t < 2):
                    wait(act, s_e_mul, t - 1)
                nc.scalar.activation(e_sg[:, r % 2, :], bank[2 + r % 2][:, 0:2 * P], ACT.Silu).then_inc(s_e_sg[0], 1)

            def hT_copy(t, r):
                wait(act, s_e_Ht, t + 1)
                if not (static(t) and t < 2):
                    wait(act, s_e_d, t - 1)
                nc.scalar.copy(e_hT[:, r % 2, :], bank[4 + r % 2][:, 0:2 * P]).then_inc(s_e_hTc[0], 1)

            xgT_copy(0, 0)

            def step(t, k, turns):
                if not (static(t) and t + 1 >= TILES):
                    xgT_copy(t + 1, (k + 1) % 4)
                if not (static(t) and t >= TILES):
                    silu(t, k % 4)
                if not (static(t) and not 0 <= t - 1 < TILES):
                    hT_copy(t - 1, (k - 1) % 4)

            e_steps(act, step)

        def e_dve(dve):
            V = nc.vector
            dve.wait_ge(s_z_x, 2 * B)
            norm_dve(dve, 7)
            wait(dve, s_e_logit, 1)
            logits = bank[2][:, 0:NT * E3].rearrange("p (i e) -> p i e", i=NT)
            dve_link(V.tensor_reduce(e_top[:, :], logits, AX_X, ALU.max))
            V.tensor_tensor(e_p[:, :, :], logits, e_top[:, :].unsqueeze(2).to_broadcast([P, NT, E3]),
                            ALU.subtract).then_inc(s_e_new, 1)
            wait(dve, s_e_exp, 1)
            dve_link(V.tensor_scalar(e_sig[:, :, :], e_sig[:, :, :], 1.0, None, ALU.add))
            dve_link(V.reciprocal(e_sig[:, :, :], e_sig[:, :, :]))
            for i in range(NT):
                last = V.max(g_best[:, i, :], e_sig[:, i, :])
            dve_link(last)
            for i in range(NT):
                last = V.max_index(g_idx[:, i, :], g_best[:, i, :], e_sig[:, i, :])
            dve_link(last)
            dve_link(V.tensor_copy(g_idxf[:, :, :], g_idx[:, :, :]))
            for i in range(NT):
                last = V.tensor_tensor(e_eq[:, i, :, :], iota_e[:, 0:E3].unsqueeze(1).to_broadcast([P, K3, E3]),
                                       g_idxf[:, i, 0:K3].unsqueeze(2).to_broadcast([P, K3, E3]), ALU.is_equal)
            dve_link(last)
            dve_link(V.tensor_reduce(e_pos[:, :, :], e_eq.rearrange("p i k e -> p i e k"), AX_X, ALU.add))
            V.tensor_copy(e_mask, e_pos[:, :, :]).then_inc(s_e_mask[0], 1)
            wait(dve, s_e_rank, 1)
            dve_link(V.tensor_scalar(e_tot[:, :], bank[4][:, 0:E3], 1.0 / P, None, ALU.mult))
            dve_link(V.tensor_tensor(e_ge[:, :, :], e_tot[:, :].unsqueeze(2).to_broadcast([P, E3, NT]),
                                     iota_e[:, 0:NT].unsqueeze(1).to_broadcast([P, E3, NT]), ALU.is_gt))
            V.memset(e_base[:, :], 1.0)
            dve_link(V.tensor_reduce(e_tiles[:, :], e_ge[:, :, :], AX_X, ALU.add))
            dve_link(V.tensor_tensor_scan(e_cum[:, :], e_base[:, :], e_tiles[:, :], 0.0, ALU.mult, ALU.add))
            dve_link(V.tensor_tensor(e_base[:, :], e_cum[:, :], e_tiles[:, :], ALU.subtract))
            dve_link(V.tensor_scalar(e_base[:, :], e_base[:, :], float(P), None, ALU.mult))
            dve_link(V.tensor_tensor(e_pos[:, :, :], bank[3][:, 0:NT * E3].rearrange("p (i e) -> p i e", i=NT),
                                     e_base[:, :].unsqueeze(1).to_broadcast([P, NT, E3]), ALU.add))
            for i in range(NT):
                dve_link(V.tensor_tensor(e_eq2[:, i, :, :], e_eq[:, i, :, :],
                                         e_pos[:, i, :].unsqueeze(1).to_broadcast([P, K3, E3]), ALU.mult))
                dve_link(V.tensor_reduce(e_locf[:, i, :], e_eq2[:, i, :, :], AX_X, ALU.add))
                dve_link(V.tensor_copy(e_loc[:, i, :], e_locf[:, i, :]))
                dve_link(V.tensor_scalar(e_low[:, i, :], e_loc[:, i, :], P - 1, TILES.bit_length() - 1, ALU.bitwise_and,
                                         ALU.logical_shift_left))
                dve_link(V.tensor_scalar(e_loc[:, i, :], e_loc[:, i, :], P.bit_length() - 1, None, ALU.logical_shift_right))
                V.tensor_tensor(e_loc[:, i, :], e_loc[:, i, :], e_low[:, i, :], ALU.bitwise_or).then_inc(s_e_idx[0], 1)
            wait(dve, s_e_idx, NT)
            dve_link(V.tensor_reduce(e_sum[:, :], e_p[:, :, :], AX_X, ALU.add))
            dve_link(V.reciprocal(e_sum[:, :], e_sum[:, :]))
            dve_link(V.tensor_tensor(e_p[:, :, :], e_p[:, :, :], e_sum[:, :].unsqueeze(2).to_broadcast([P, NT, E3]), ALU.mult))
            for i in range(NT):
                last = V.tensor_tensor(e_eq2[:, i, :, :], e_eq[:, i, :, :], e_p[:, i, :].unsqueeze(1).to_broadcast([P, K3, E3]),
                                       ALU.mult)
            dve_link(last)
            dve_link(V.tensor_reduce(e_wk[:, :, :], e_eq2, AX_X, ALU.add))
            dve_link(V.tensor_reduce(e_wsum[:, :], e_wk[:, :, :], AX_X, ALU.add))
            dve_link(V.reciprocal(e_wsum[:, :], e_wsum[:, :]))
            dve_link(V.tensor_tensor(e_wk[:, :, :], e_wk[:, :, :], e_wsum[:, :].unsqueeze(2).to_broadcast([P, NT, K3]), ALU.mult))
            dve_link(V.tensor_scalar(e_wk[:, :, :], e_wk[:, :, :], tanh_g[:, 1, 3:4], None, ALU.mult))
            row = e_cmp[0:1]
            dve_link(V.tensor_tensor(row, iota_e[0:1, 0:TILES].unsqueeze(2).to_broadcast([1, TILES, E3]),
                                     e_cum[0:1, :].unsqueeze(1).to_broadcast([1, TILES, E3]), ALU.is_ge))
            dve_link(V.tensor_reduce(e_tabf, row, AX_X, ALU.add))
            dve_link(V.tensor_scalar(e_tabf, e_tabf, float(E3 - 1), None, ALU.min))
            V.tensor_copy(e_tab[:, :], e_tabf).then_inc(s_e_tab, 1)
            for b in (2, 3):
                last = V.memset(bank[b][:, :].rearrange("p (w n) -> p w n", w=2)[:, :, F3:P], 0.0)
            last.then_inc(s_e_pad, 1)

            def mult(t, r):
                wait(dve, s_e_sg, t + 1)
                if not (static(t) and t < 2):
                    wait(dve, s_e_Ht, t - 1)
                V.tensor_tensor(e_h[:, r % 2, :], e_sg[:, r % 2, :], bank[2 + r % 2][:, 2 * P:4 * P], ALU.mult).then_inc(s_e_mul[0], 1)

            def evict(t, r, turns):
                wait(dve, s_e_d, t + 1)
                if not (static(t) and t < 4):
                    wait(dve, s_e_st[r], turns * 16)
                V.tensor_copy(e_ye[:, r, :], bank[6 + r % 2][:, 0:D]).then_inc(s_e_ye[0], 1)

            def step(t, k, turns):
                if not (static(t) and t >= TILES):
                    mult(t, k % 4)
                if not (static(t) and t < 2):
                    evict(t - 2, (k - 2) % 4, turns * (XR // 4) + (k - 2) // 4)

            e_steps(dve, step)
            for m in range(NT * K3):
                i, k = m // K3, m % K3
                if k == 0:
                    wait(dve, s_e_back[i], 16 * K3)
                if m:
                    wait(dve, s_e_x, m)
                V.scalar_tensor_tensor(out=x[:, i, :], in0=e_back[:, m, :], scalar=e_wk[:, i, k:k + 1],
                                       in1=x[:, i, :], op0=ALU.mult, op1=ALU.add).then_inc(s_e_x[0], 1)

        s_out = sem("s_out")

        def store_sp(sp):
            rows = out.rearrange("b (h p) d -> p (b h) d", p=P)
            for b in range(B):
                wait(sp, s_e_x, TPB * K3 * (b + 1))
                sp.dma_start(rows[:, TPB * b:TPB * (b + 1), :], x[:, TPB * b:TPB * (b + 1), :]).then_inc(s_out, 16)
            sp.wait_ge(s_out, 16 * B)

        dve_link, pool_link, act_link = Link(nc.vector, s_dve), Link(nc.gpsimd, s_pool), Link(nc.scalar, s_act)
        block = ctx.enter_context(nc.Block())

        @block.sync
        def _(sp):
            prep_sp(sp)
            f0_sp(sp)
            l1_loads_sp(sp)
            ssm_bc_sp(sp, 1)
            for g in range(GB):
                ssm_load_sp(sp, 1, 0, g)
            x_sp(sp)
            g_sp(sp)
            e_sp(sp)
            store_sp(sp)

        @block.gpsimd
        def _(pool):
            prep_pool(pool)
            f0_const_pool(pool)
            norm_pool(pool, 0)
            norm_pool(pool, 1)
            f0_pool(pool)
            norm_pool(pool, 2)
            norm_pool(pool, 3)
            l1_pool(pool)
            norm_pool(pool, 4)
            x_pool(pool)
            norm_pool(pool, 5)
            norm_pool(pool, 6)
            e_pool(pool)

        @block.scalar
        def _(act):
            prep_act(act, 0, 4)
            gate_act(act)
            l0x_act(act)
            f0_act_eng(act)
            ssm_in_act(act, 1)
            f0_diag_act(act, 0, 4)
            ssm_u_act(act, 1)
            f0_diag_act(act, 4, 14)
            ssm_dt_act(act, 1)
            f0_diag_act(act, 14, 36)
            l1_prep_act(act)
            f0_diag_act(act, 36, NT * K0)
            gated_act(act, 0, 2)
            l1_act(act)
            x_act(act)
            g_act(act)
            gated_act(act, 1, 6)
            e_act(act)

        @block.vector
        def _(dve):
            l0x_dve(dve)
            f0_dve(dve)
            gated_dve(dve, 0, 2)
            l1_dve(dve)
            x_dve(dve)
            g_dve(dve)
            gated_dve(dve, 1, 6)
            e_dve(dve)

        @block.tensor
        def _(pe):
            prep_pe(pe, 0, 4)
            l0x_pe(pe)
            f0_pe(pe)
            ssm_in_pe(pe, 1)
            f0_combine_pe(pe, 0, 14)
            ssm_dt_pe(pe, 1)
            f0_combine_pe(pe, 14, 36)
            l1_prep_pe(pe)
            f0_combine_pe(pe, 36, NT * K0)
            gated_pe(pe, 0)
            l1_pe(pe)
            x_pe(pe)
            g_pe(pe)
            gated_pe(pe, 1)
            e_pe(pe)


_OUTS = [((B, S, D), 'float32')]


def kernel(**inputs):
    import numpy as _np
    import concourse.bacc as _bacc
    from concourse import mybir as _mybir
    from concourse.bass_utils import run_bass_kernel_spmd as _run

    nc = _bacc.Bacc("TRN2", target_bir_lowering=False, num_devices=1)
    arrays, args = {}, {}
    for name in inputs:
        a = _np.ascontiguousarray(inputs[name])
        arrays[f"in_{name}_dram"] = a
        args[name] = nc.dram_tensor(f"in_{name}_dram", a.shape, _mybir.dt.from_np(a.dtype), kind="ExternalInput").ap()
    outs = []
    for i, (shape, dtype) in enumerate(_OUTS):
        dt = _mybir.dt.from_np(_np.dtype(dtype))
        outs.append(nc.dram_tensor(f"out_{i}_dram", shape, dt, kind="ExternalOutput").ap())
    flamingo_kernel(nc, args, outs[0])
    r = _run(nc, [arrays], core_ids=[0])
    return r.results[0]["out_0_dram"]
```
